# Optimizing a Trainium2 kernel written in Bass

```python
import numpy as np
import jax
import jax.numpy as jnp

def _softmax(x, axis=-1):
    return jax.nn.softmax(x, axis=axis)

def _gelu(x):
    return jax.nn.gelu(x, approximate=True)

def _silu(x):
    return jax.nn.silu(x)

def _sigmoid(x):
    return jax.nn.sigmoid(x)

def _layernorm(x, axis=-1, eps=1e-05):
    m = jnp.mean(x, axis=axis, keepdims=True)
    v = jnp.var(x, axis=axis, keepdims=True)
    return (x - m) / jnp.sqrt(v + eps)

def _scatter_add(tgt, idx, src, axis=0):
    return tgt.at[idx].add(src)

def _segment_sum(src, seg, n):
    return jax.ops.segment_sum(src, seg, n)
kernel_name = 'mk_prb_d2_jaxref_r8_d37282'

def setup_inputs(seed: int=0):
    np.random.seed(seed)
    _w = jnp.asarray

    def _L0_attn_setup():
        import jax, jax.numpy as jnp
        import numpy as np
        TOPK = 32
        NEG = -1e+30

        def hadamard(x):
            d = x.shape[-1]
            shape = x.shape
            x = x.reshape(-1, d)
            h = 1
            while h < d:
                x = x.reshape(-1, d // (2 * h), 2, h)
                a, b = (x[:, :, 0, :], x[:, :, 1, :])
                x = jnp.stack([a + b, a - b], axis=2).reshape(-1, d)
                h *= 2
            return (x * d ** (-0.5)).reshape(shape)
        key = jax.random.key(seed)
        ks = jax.random.split(key, 8)
        D, S, B = (256, 256, 1)
        Hi, Di, H, hd = (16, 128, 16, 128)
        w = 0.02
        return {'x': jax.random.normal(ks[0], (B, S, D), jnp.float32), 'wq_idx': jax.random.normal(ks[1], (D, Hi * Di), jnp.float32) * w, 'wk_idx': jax.random.normal(ks[2], (D, Di), jnp.float32) * w, 'w_iw': jax.random.normal(ks[3], (D, Hi), jnp.float32) * w, 'wq': jax.random.normal(ks[4], (D, H * hd), jnp.float32) * w, 'wk': jax.random.normal(ks[5], (D, hd), jnp.float32) * w, 'wv': jax.random.normal(ks[6], (D, hd), jnp.float32) * w, 'wo': jax.random.normal(ks[7], (H * hd, D), jnp.float32) * w}
    _L0_attn_in = _L0_attn_setup()

    def _L0_ffn_setup():
        import jax, jax.numpy as jnp
        import numpy as np
        B, S, D, H, E, TOP_K = (4, 256, 256, 512, 8, 2)
        key = jax.random.key(seed)
        k0, k1, k2, k3, k4 = jax.random.split(key, 5)
        scale = 0.02
        return {'hidden_states': jax.random.normal(k0, (B, S, D), jnp.float32), 'w_router': jax.random.normal(k1, (D, E), jnp.float32) * scale, 'w_gate': jax.random.normal(k2, (E, D, H), jnp.float32) * scale, 'w_up': jax.random.normal(k3, (E, D, H), jnp.float32) * scale, 'w_down': jax.random.normal(k4, (E, H, D), jnp.float32) * scale}
    _L0_ffn_in = _L0_ffn_setup()

    def _L1_attn_setup():
        import jax, jax.numpy as jnp
        import numpy as np
        import math
        D_MODEL = 128
        D_STATE = 16
        D_INNER = 256
        DT_RANK = 64
        DT_MIN, DT_MAX = (0.001, 0.1)
        BATCH, SEQ_LEN = (4, 512)
        key = jax.random.key(seed)
        k_x, k_wx, k_wdt, k_dt = jax.random.split(key, 4)
        x = jax.random.normal(k_x, (BATCH, SEQ_LEN, D_INNER), dtype=jnp.float32)
        A_log = jnp.log(jnp.tile(jnp.arange(1, D_STATE + 1, dtype=jnp.float32), (D_INNER, 1)))
        D_skip = jnp.ones((D_INNER,), dtype=jnp.float32)
        W_x = jax.random.normal(k_wx, (D_INNER, DT_RANK + 2 * D_STATE), dtype=jnp.float32) / math.sqrt(D_INNER)
        W_dt = jax.random.normal(k_wdt, (DT_RANK, D_INNER), dtype=jnp.float32) / math.sqrt(DT_RANK)
        dt_init = jnp.exp(jax.random.uniform(k_dt, (D_INNER,), dtype=jnp.float32) * (math.log(DT_MAX) - math.log(DT_MIN)) + math.log(DT_MIN))
        b_dt = dt_init + jnp.log(-jnp.expm1(-dt_init))
        return {'x': x, 'A_log': A_log, 'D_skip': D_skip, 'W_x': W_x, 'W_dt': W_dt, 'b_dt': b_dt}
    _L1_attn_in = _L1_attn_setup()

    def _L1_ffn_setup():
        import jax, jax.numpy as jnp
        import numpy as np

        def _sparsify_2to4(h):
            B, S, I = h.shape
            g = h.reshape(B, S, I // 4, 4)
            a = jnp.abs(g)
            _, idx = jax.lax.top_k(a, 2)
            pos = jnp.arange(4)
            mask = (pos == idx[..., 0:1]) | (pos == idx[..., 1:2])
            return (g * mask.astype(g.dtype)).reshape(B, S, I)
        key = jax.random.key(seed)
        k1, k2, k3, k4 = jax.random.split(key, 4)
        B, S, H, I = (4, 256, 256, 1024)
        x = jax.random.normal(k1, (B, S, H), dtype=jnp.float32)
        w_gate = jax.random.normal(k2, (H, I), dtype=jnp.float32) / np.sqrt(H)
        w_up = jax.random.normal(k3, (H, I), dtype=jnp.float32) / np.sqrt(H)
        w_down = jax.random.normal(k4, (I, H), dtype=jnp.float32) / np.sqrt(I)
        return {'x': x, 'w_gate': w_gate, 'w_up': w_up, 'w_down': w_down}
    _L1_ffn_in = _L1_ffn_setup()
    _d = {'L0_attn_x': _L0_attn_in['x'], 'L0_attn_wq_idx': _L0_attn_in['wq_idx'], 'L0_attn_wk_idx': _L0_attn_in['wk_idx'], 'L0_attn_w_iw': _L0_attn_in['w_iw'], 'L0_attn_wq': _L0_attn_in['wq'], 'L0_attn_wk': _L0_attn_in['wk'], 'L0_attn_wv': _L0_attn_in['wv'], 'L0_attn_wo': _L0_attn_in['wo'], 'L0_ffn_w_router': _L0_ffn_in['w_router'], 'L0_ffn_w_gate': _L0_ffn_in['w_gate'], 'L0_ffn_w_up': _L0_ffn_in['w_up'], 'L0_ffn_w_down': _L0_ffn_in['w_down'], 'L1_attn_A_log': _L1_attn_in['A_log'], 'L1_attn_D_skip': _L1_attn_in['D_skip'], 'L1_attn_W_x': _L1_attn_in['W_x'], 'L1_attn_W_dt': _L1_attn_in['W_dt'], 'L1_attn_b_dt': _L1_attn_in['b_dt'], 'L1_ffn_w_gate': _L1_ffn_in['w_gate'], 'L1_ffn_w_up': _L1_ffn_in['w_up'], 'L1_ffn_w_down': _L1_ffn_in['w_down']}
    _x0 = _d['L0_attn_x']
    _d['L0_attn_x'] = jax.random.normal(jax.random.fold_in(jax.random.key(seed), 1), (2, 512, 256), dtype=_x0.dtype)
    del _x0
    return _d

def reference(L0_attn_x, L0_attn_wq_idx, L0_attn_wk_idx, L0_attn_w_iw, L0_attn_wq, L0_attn_wk, L0_attn_wv, L0_attn_wo, L0_ffn_w_router, L0_ffn_w_gate, L0_ffn_w_up, L0_ffn_w_down, L1_attn_A_log, L1_attn_D_skip, L1_attn_W_x, L1_attn_W_dt, L1_attn_b_dt, L1_ffn_w_gate, L1_ffn_w_up, L1_ffn_w_down):

    def _L0_attn_ref(x, wq_idx, wk_idx, w_iw, wq, wk, wv, wo):
        import jax, jax.numpy as jnp
        import numpy as np
        TOPK = 32
        NEG = -1e+30

        def hadamard(x):
            d = x.shape[-1]
            shape = x.shape
            x = x.reshape(-1, d)
            h = 1
            while h < d:
                x = x.reshape(-1, d // (2 * h), 2, h)
                a, b = (x[:, :, 0, :], x[:, :, 1, :])
                x = jnp.stack([a + b, a - b], axis=2).reshape(-1, d)
                h *= 2
            return (x * d ** (-0.5)).reshape(shape)
        B, S, D = x.shape
        Di = wk_idx.shape[-1]
        Hi = w_iw.shape[-1]
        hd = wk.shape[-1]
        H = wq.shape[-1] // hd
        qi = hadamard((x @ wq_idx).reshape(B, S, Hi, Di))
        ki = hadamard(x @ wk_idx)
        iw = x @ w_iw
        logits = jax.nn.relu(jnp.einsum('bthd,bsd->bhts', qi, ki))
        I = jnp.einsum('bth,bhts->bts', iw, logits)
        t = jnp.arange(S)
        causal = t[None, :, None] >= t[None, None, :]
        I = jnp.where(causal, I, NEG)
        vals, idx = jax.lax.top_k(I, TOPK)
        valid = vals > NEG / 2
        q = (x @ wq).reshape(B, S, H, hd)
        k = x @ wk
        v = x @ wv
        gather = jax.vmap(lambda kk, ii: kk[ii])
        k_sel, v_sel = (gather(k, idx), gather(v, idx))
        scores = jnp.einsum('bthd,btkd->bhtk', q, k_sel) * hd ** (-0.5)
        scores = jnp.where(valid[:, None], scores, NEG)
        p = jax.nn.softmax(scores, axis=-1)
        o = jnp.einsum('bhtk,btkd->bthd', p, v_sel)
        return o.reshape(B, S, H * hd) @ wo

    def _L0_ffn_ref(hidden_states, w_router, w_gate, w_up, w_down):
        import jax, jax.numpy as jnp
        import numpy as np
        B, S, D, H, E, TOP_K = (4, 256, 256, 512, 8, 2)
        x = hidden_states.reshape(-1, hidden_states.shape[-1])
        T = x.shape[0]
        logits = x @ w_router
        probs = jax.nn.softmax(logits.astype(jnp.float32), axis=-1)
        rw, sel = jax.lax.top_k(probs, TOP_K)
        rw = rw / jnp.sum(rw, axis=-1, keepdims=True)
        rw = rw.astype(x.dtype)
        combine = jnp.zeros((T, E), x.dtype).at[jnp.arange(T)[:, None], sel].set(rw)
        out = jnp.zeros_like(x)
        for e in range(E):
            g = jax.nn.silu(x @ w_gate[e]) * (x @ w_up[e])
            y = g @ w_down[e]
            out = out + combine[:, e:e + 1] * y
        return out.reshape(hidden_states.shape)

    def _L1_attn_ref(x, A_log, D_skip, W_x, W_dt, b_dt):
        import jax, jax.numpy as jnp
        import numpy as np
        import math
        D_MODEL = 128
        D_STATE = 16
        D_INNER = 256
        DT_RANK = 64
        DT_MIN, DT_MAX = (0.001, 0.1)
        BATCH, SEQ_LEN = (4, 512)
        N = D_STATE
        xp = jnp.einsum('bld,de->ble', x, W_x)
        dt_low = xp[..., :DT_RANK]
        B_proj = xp[..., DT_RANK:DT_RANK + N]
        C_proj = xp[..., DT_RANK + N:]
        dt = jax.nn.softplus(jnp.einsum('blr,rd->bld', dt_low, W_dt) + b_dt)
        A = -jnp.exp(A_log)

        def step(h, inp):
            dt_t, Bp_t, C_t, x_t = inp
            dA = jnp.exp(dt_t[..., None] * A)
            h = dA * h + (dt_t * x_t)[..., None] * Bp_t[:, None, :]
            y = jnp.einsum('bdn,bn->bd', h, C_t)
            return (h, y)
        h0 = jnp.zeros((x.shape[0], D_INNER, N), dtype=x.dtype)
        xs = (jnp.swapaxes(dt, 0, 1), jnp.swapaxes(B_proj, 0, 1), jnp.swapaxes(C_proj, 0, 1), jnp.swapaxes(x, 0, 1))
        _, ys = jax.lax.scan(step, h0, xs)
        y = jnp.swapaxes(ys, 0, 1) + x * D_skip
        return y

    def _L1_ffn_ref(x, w_gate, w_up, w_down):
        import jax, jax.numpy as jnp
        import numpy as np

        def _sparsify_2to4(h):
            B, S, I = h.shape
            g = h.reshape(B, S, I // 4, 4)
            a = jnp.abs(g)
            _, idx = jax.lax.top_k(a, 2)
            pos = jnp.arange(4)
            mask = (pos == idx[..., 0:1]) | (pos == idx[..., 1:2])
            return (g * mask.astype(g.dtype)).reshape(B, S, I)
        h = jax.nn.silu(jnp.einsum('bsh,hi->bsi', x, w_gate)) * jnp.einsum('bsh,hi->bsi', x, w_up)
        h_sparse = _sparsify_2to4(h)
        return jnp.einsum('bsi,ih->bsh', h_sparse, w_down)
    x = L0_attn_x
    xn = _layernorm(x, axis=-1)
    x = x + _L0_attn_ref(xn, L0_attn_wq_idx, L0_attn_wk_idx, L0_attn_w_iw, L0_attn_wq, L0_attn_wk, L0_attn_wv, L0_attn_wo) + _L0_ffn_ref(xn, L0_ffn_w_router, L0_ffn_w_gate, L0_ffn_w_up, L0_ffn_w_down)
    xn = _layernorm(x, axis=-1)
    x = x + _L1_attn_ref(xn, L1_attn_A_log, L1_attn_D_skip, L1_attn_W_x, L1_attn_W_dt, L1_attn_b_dt) + _L1_ffn_ref(xn, L1_ffn_w_gate, L1_ffn_w_up, L1_ffn_w_down)
    return x

_drawn_inputs = setup_inputs


def setup_inputs(seed=0):
    import zlib

    import numpy as np

    out = dict(_drawn_inputs(seed))
    spreads = {'L1_attn_D_skip': (1.0, 0.2)}
    factors = {'L0_attn_wq': 6.885,
     'L0_attn_wk': 6.742,
     'L0_ffn_w_router': 3.038,
     'L0_ffn_w_gate': 2.711,
     'L0_ffn_w_up': 2.687,
     'L0_ffn_w_down': 2.686}
    for name, (base, spread) in spreads.items():
        noise = np.random.default_rng([zlib.crc32(name.encode()), seed]).standard_normal(out[name].shape)
        drawn = base * np.exp(spread * noise) if base else spread * noise
        out[name] = jnp.asarray(drawn.astype(out[name].dtype))
    for name, factor in factors.items():
        out[name] = (out[name] * factor).astype(out[name].dtype)
    return out
```

```python
from contextlib import ExitStack

import concourse.bass as bass
from concourse import mybir

F32 = mybir.dt.float32
F32R = mybir.dt.float32r
BF16 = mybir.dt.bfloat16
U32 = mybir.dt.uint32
ALU = mybir.AluOpType
ACT = mybir.ActivationFunctionType
AX = mybir.AxisListType

P = 128
NEG = -1e30
TAKEN = -3e38
EPS = 1e-5


def pipeline(eng, n, unroll, front, back):
    front(0, 0)
    with eng.Fori(0, n // unroll - 1) as i:
        for r in range(unroll):
            front(i * unroll + (r + 1), (r + 1) % unroll)
            back(i * unroll + r, r)
    base = n - unroll
    for r in range(unroll):
        if r + 1 < unroll:
            front(base + r + 1, r + 1)
        back(base + r, r)


def matmul3(pe, out, w_hi, w_lo, x_hi, x_lo, start, stop, **kw):
    pe.matmul(out, w_hi, x_hi, start=start, stop=False, **kw)
    pe.matmul(out, w_hi, x_lo, start=False, stop=False, **kw)
    return pe.matmul(out, w_lo, x_hi, start=False, stop=stop, **kw)


def split_hi(pool, hi, src):
    return pool.tensor_scalar(hi, src, 1.0, 1.0, ALU.mult, ALU.mult)


def two_layers(nc, x, wq_idx, wk_idx, w_iw, wq, wk, wv, wo, w_router, e_gate, e_up, e_down,
               a_log, d_skip, w_x, w_dt, b_dt, f_gate, f_up, f_down, out):
    NB, S, D = x.shape
    KD = D // P
    TOK = NB * S
    NT = TOK // P
    TB = S // P
    DI = wk_idx.shape[1]
    HI = w_iw.shape[1]
    HD = wk.shape[1]
    H = wq.shape[1] // HD
    SCALE = float(HD) ** -0.5
    NE, _, HE = e_gate.shape
    HC = HE // P
    NS = a_log.shape[1]
    R = w_dt.shape[0]
    FI = f_gate.shape[1]
    FC = FI // P
    TOPK = 32
    assert DI == P and HD == P and S == 512 and D == 256

    x_rows = x.rearrange("b (j p) d -> p (b j) d", p=P)
    out_rows = out.rearrange("b (j p) d -> p (b j) d", p=P)
    bc_dram = nc.dram_tensor("bc_scratch", [2, NS, TOK], F32).ap()

    with ExitStack() as top:
        def sem(name):
            return top.enter_context(nc.semaphore(name))

        def sb_in(ctx):
            def sb(name, shape, dt=F32):
                return ctx.enter_context(nc.sbuf_tensor(name, shape, dt))
            return sb

        sb = sb_in(top)
        ps = top.enter_context(nc.psum_tensor("ps", [P, 8, 512], F32))
        acc = sb("acc", [P, NT, D])
        ident = sb("ident", [P, P])
        stand = sem("stand")
        stats = sb("stats", [P, NT, 6])
        mv = sb("mv", [P, NT, 2])
        std = sb("std", [P, NT])
        rstd = sb("rstd", [P, NT])
        xn = sb("xn", [P, NT, D])
        xnT_h = sb("xnT_h", [P, KD, TOK], F32R)
        xnT_l = sb("xnT_l", [P, KD, TOK], F32R)

        def layernorm_vector(dve, have_x, s_stat, s_std, s_rstd, s_xn):
            for j in range(NT):
                if have_x is not None and j % TB == 0:
                    dve.wait_ge(have_x[j // TB], 16)
                dve.bn_stats(stats[:, j, :], acc[:, j, :]).then_inc(s_stat, 1)
            for j in range(NT):
                dve.wait_ge(s_stat, j + 1)
                dve.bn_aggr(mv[:, j, :], stats[:, j, :]).then_inc(s_stat, 1)
            dve.wait_ge(s_stat, 2 * NT)
            dve.tensor_scalar(std[:, :], mv[:, :, 1], EPS, None, ALU.add).then_inc(s_stat, 1)
            dve.wait_ge(s_std, 1)
            dve.reciprocal(rstd[:, :], std[:, :]).then_inc(s_rstd, 1)
            dve.wait_ge(s_rstd, 1)
            for j in range(NT):
                dve.tensor_scalar(xn[:, j, :], acc[:, j, :], mv[:, j, 0:1], rstd[:, j:j + 1],
                                  ALU.subtract, ALU.mult).then_inc(s_xn, 1)

        def transpose_rows(pe, s_xn, s_xt):
            for g in range(NT // 2):
                pe.wait_ge(s_xn, 2 * g + 2)
                for k in range(KD):
                    for m in range(2):
                        last = pe.transpose(ps[:, g, (2 * k + m) * P:(2 * k + m + 1) * P],
                                            xn[:, 2 * g + m, k * P:(k + 1) * P], ident[:, :])
                last.then_inc(s_xt, 1)

        def pair(buf, g):
            return buf[:, :, 2 * g * P:(2 * g + 2) * P]

        def bank_pair(g):
            return ps[:, g, :].rearrange("p (k t) -> p k t", k=KD)

        l0 = ExitStack()
        sbl = sb_in(l0)
        kT_h = sbl("kT_h", [P, TOK], F32R)
        kT_l = sbl("kT_l", [P, TOK], F32R)
        v_h = sbl("v_h", [P, NT, HD], F32R)
        v_l = sbl("v_l", [P, NT, HD], F32R)
        combine = sbl("combine", [P, NT, NE])
        index = sbl("index", [P, NT, S])
        li = ExitStack()
        sbi = sb_in(li)
        kiT_h = sbi("kiT_h", [P, TOK], F32R)
        kiT_l = sbi("kiT_l", [P, TOK], F32R)
        small = sbi("small", [P, NT, HI + NE])
        NV = HD + HI + NE
        with ExitStack() as c:
            s = sb_in(c)
            w_k = s("w_k", [P, 2, KD, P])
            w_k_h = s("w_k_h", [P, 2, KD, P], F32R)
            w_k_l = s("w_k_l", [P, 2, KD, P], F32R)
            w_v = s("w_v", [P, KD, NV])
            w_v_h = s("w_v_h", [P, KD, NV], F32R)
            w_v_l = s("w_v_l", [P, KD, NV], F32R)
            lmax = s("lmax", [P, NT])
            prob = s("prob", [P, NT, NE])
            psum_r = s("psum_r", [P, NT])
            prec = s("prec", [P, NT])
            top8 = s("top8", [P, NT, 8])
            top8i = s("top8i", [P, NT, 8], U32)
            topi = s("topi", [P, NT, 2])
            rws = s("rws", [P, NT])
            rwr = s("rwr", [P, NT])
            rw = s("rw", [P, NT, 2])
            iota = s("iota", [P, NT, NE])
            pick = s("pick", [P, 2, NT, NE])

            x_in = [sem("x_in0"), sem("x_in1")]
            wk_in = sem("wk_in")
            wv_in = sem("wv_in")
            s_ident = sem("s_ident")
            wk_split = sem("wk_split")
            wv_split = sem("wv_split")
            s_stat = sem("s_stat")
            s_std = sem("s_std")
            s_rstd = sem("s_rstd")
            s_xn = sem("s_xn")
            s_xt = sem("s_xt")
            xt_hi = sem("xt_hi")
            xt_lo = sem("xt_lo")
            k_ps = sem("k_ps")
            k_hi = sem("k_hi")
            k_lo = sem("k_lo")
            v_ps = sem("v_ps")
            v_hi = sem("v_hi")
            v_lo = sem("v_lo")
            s_small = sem("s_small")
            s_route = sem("s_route")
            s_shift = sem("s_shift")
            s_exp = sem("s_exp")

            with nc.Block() as block:
                @block.sync
                def _(sp):
                    for b in range(NB):
                        sp.dma_start(acc[:, b * TB:(b + 1) * TB, :],
                                     x_rows[:, b * TB:(b + 1) * TB, :]).then_inc(x_in[b], 16)
                    for n, w in enumerate((wk_idx, wk)):
                        sp.dma_start(w_k[:, n, :, :],
                                     w.rearrange("(k p) n -> p k n", p=P)).then_inc(wk_in, 16)
                    at = 0
                    for w in (wv, w_iw, w_router):
                        sp.dma_start(w_v[:, :, at:at + w.shape[1]],
                                     w.rearrange("(k p) n -> p k n", p=P)).then_inc(wv_in, 16)
                        at += w.shape[1]

                @block.gpsimd
                def _(pool):
                    pool.memset(ident[:, :], 0.0).then_inc(s_ident, 1)
                    pool.wait_ge(s_ident, 1)
                    pool.affine_select(out=ident[:, :], in_=ident[:, :], compare_op=ALU.not_equal,
                                       fill=1.0, base=0, pattern=[[-1, P]],
                                       channel_multiplier=1).then_inc(s_ident, 1)
                    for e in range(NE):
                        pool.memset(iota[:, :, e], float(e)).then_inc(s_ident, 1)
                    pool.memset(index[:, :, :], 0.0).then_inc(s_ident, 1)
                    pool.wait_ge(wk_in, 32)
                    split_hi(pool, w_k_h[:, :, :, :], w_k[:, :, :, :]).then_inc(wk_split, 1)
                    pool.wait_ge(wk_split, 1)
                    pool.tensor_tensor(w_k_l[:, :, :, :], w_k[:, :, :, :],
                                       w_k_h[:, :, :, :].bitcast(F32), ALU.subtract).then_inc(wk_split, 1)
                    pool.wait_ge(wv_in, 48)
                    split_hi(pool, w_v_h[:, :, :], w_v[:, :, :]).then_inc(wv_split, 1)
                    pool.wait_ge(wv_split, 1)
                    pool.tensor_tensor(w_v_l[:, :, :], w_v[:, :, :],
                                       w_v_h[:, :, :].bitcast(F32), ALU.subtract).then_inc(wv_split, 1)

                @block.tensor
                def _(pe):
                    pe.wait_ge(s_ident, 2)
                    transpose_rows(pe, s_xn, s_xt)
                    pe.wait_ge(wk_split, 2)
                    for b in range(NB):
                        pe.wait_ge(xt_lo, (b + 1) * TB // 2)
                        for n in range(2):
                            for k in range(KD):
                                last = matmul3(pe, ps[:, 4 + 2 * b + n, :], w_k_h[:, n, k, :],
                                               w_k_l[:, n, k, :], xnT_h[:, k, b * S:(b + 1) * S],
                                               xnT_l[:, k, b * S:(b + 1) * S], k == 0, k == KD - 1)
                            last.then_inc(k_ps, 1)
                    pe.wait_ge(wv_split, 2)
                    for j in range(NT):
                        o = ps[:, j // 2, (j % 2) * 256:(j % 2) * 256 + NV]
                        for k in range(KD):
                            last = matmul3(pe, o, xnT_h[:, k, j * P:(j + 1) * P],
                                           xnT_l[:, k, j * P:(j + 1) * P], w_v_h[:, k, :],
                                           w_v_l[:, k, :], k == 0, k == KD - 1)
                        last.then_inc(v_ps, 1)

                @block.scalar
                def _(act):
                    act.wait_ge(s_stat, 2 * NT + 1)
                    act.activation(std[:, :], std[:, :], ACT.Sqrt).then_inc(s_std, 1)
                    for g in range(NT // 2):
                        act.wait_ge(s_xt, g + 1)
                        act.activation(pair(xnT_h, g), bank_pair(g), ACT.Copy).then_inc(xt_hi, 1)
                    for b in range(NB):
                        for n, dst in enumerate((kiT_h, kT_h)):
                            act.wait_ge(k_ps, 2 * b + n + 1)
                            act.activation(dst[:, b * S:(b + 1) * S], ps[:, 4 + 2 * b + n, :],
                                           ACT.Copy).then_inc(k_hi, 1)
                    for g in range(NT // 2):
                        act.wait_ge(v_ps, 2 * g + 2)
                        act.activation(v_h[:, 2 * g:2 * g + 2, :],
                                       ps[:, g, :].rearrange("p (j n) -> p j n", j=2)[:, :, 0:HD],
                                       ACT.Copy).then_inc(v_hi, 1)
                    act.wait_ge(s_shift, 1)
                    act.activation(prob[:, :, :], prob[:, :, :], ACT.Exp).then_inc(s_exp, 1)

                @block.vector
                def _(dve):
                    layernorm_vector(dve, x_in, s_stat, s_std, s_rstd, s_xn)
                    for g in range(NT // 2):
                        dve.wait_ge(xt_hi, g + 1)
                        dve.tensor_tensor(pair(xnT_l, g), bank_pair(g), pair(xnT_h, g).bitcast(F32),
                                          ALU.subtract).then_inc(xt_lo, 1)
                    for b in range(NB):
                        for n, (hi, lo) in enumerate(((kiT_h, kiT_l), (kT_h, kT_l))):
                            dve.wait_ge(k_hi, 2 * b + n + 1)
                            dve.tensor_tensor(lo[:, b * S:(b + 1) * S], ps[:, 4 + 2 * b + n, :],
                                              hi[:, b * S:(b + 1) * S].bitcast(F32),
                                              ALU.subtract).then_inc(k_lo, 1)
                    for g in range(NT // 2):
                        dve.wait_ge(v_hi, g + 1)
                        bank = ps[:, g, :].rearrange("p (j n) -> p j n", j=2)
                        dve.tensor_tensor(v_l[:, 2 * g:2 * g + 2, :], bank[:, :, 0:HD],
                                          v_h[:, 2 * g:2 * g + 2, :].bitcast(F32),
                                          ALU.subtract).then_inc(v_lo, 1)
                        dve.tensor_copy(small[:, 2 * g:2 * g + 2, :],
                                        bank[:, :, HD:NV]).then_inc(s_small, 1)
                    step = [0]

                    def then(ins):
                        step[0] += 1
                        ins.then_inc(s_route, 1)
                        dve.wait_ge(s_route, step[0])

                    def wide(a):
                        return a.rearrange("p (j e) -> p j e", e=1).broadcast_to([P, NT, NE])

                    dve.wait_ge(s_small, NT // 2)
                    logits = small[:, :, HI:HI + NE]
                    then(dve.tensor_reduce(lmax[:, :], logits, AX.X, ALU.max))
                    dve.tensor_tensor(prob[:, :, :], logits, wide(lmax[:, :]),
                                      ALU.subtract).then_inc(s_shift, 1)
                    dve.wait_ge(s_exp, 1)
                    then(dve.tensor_reduce(psum_r[:, :], prob[:, :, :], AX.X, ALU.add))
                    then(dve.reciprocal(prec[:, :], psum_r[:, :]))
                    then(dve.tensor_tensor(prob[:, :, :], prob[:, :, :], wide(prec[:, :]), ALU.mult))
                    for j in range(NT):
                        last = dve.max(top8[:, j, :], prob[:, j, :])
                    then(last)
                    for j in range(NT):
                        last = dve.max_index(top8i[:, j, :], top8[:, j, :], prob[:, j, :])
                    then(last)
                    then(dve.tensor_copy(topi[:, :, :], top8i[:, :, 0:2]))
                    then(dve.tensor_tensor(rws[:, :], top8[:, :, 0], top8[:, :, 1], ALU.add))
                    then(dve.reciprocal(rwr[:, :], rws[:, :]))
                    dve.wait_ge(s_ident, 2 + NE)
                    for m in range(2):
                        then(dve.tensor_tensor(rw[:, :, m], top8[:, :, m], rwr[:, :], ALU.mult))
                        then(dve.tensor_tensor(pick[:, m, :, :], iota[:, :, :], wide(topi[:, :, m]),
                                               ALU.is_equal))
                        then(dve.tensor_tensor(pick[:, m, :, :], pick[:, m, :, :], wide(rw[:, :, m]),
                                               ALU.mult))
                    then(dve.tensor_tensor(combine[:, :, :], pick[:, 0, :, :], pick[:, 1, :, :], ALU.add))

        with ExitStack() as c:
            s = sb_in(c)
            w_raw = s("iw_raw", [P, 2, KD, P])
            w_h = s("iw_h", [P, 2, KD, P], F32R)
            w_l = s("iw_l", [P, 2, KD, P], F32R)
            qT_h = s("iqT_h", [P, 2, TOK], F32R)
            qT_l = s("iqT_l", [P, 2, TOK], F32R)
            NR = 4
            relu = s("irelu", [P, NR, S])
            raw_in = [sem("i_raw0"), sem("i_raw1")]
            raw_free = sem("i_raw_free")
            w_hi = sem("i_w_hi")
            w_ready = sem("i_w_ready")
            q_ps = sem("i_q_ps")
            q_hi = sem("i_q_hi")
            q_lo = sem("i_q_lo")
            lg_ps = sem("i_lg_ps")
            relu_ready = sem("i_relu")
            relu_free = sem("i_relu_free")
            wqi = wq_idx.rearrange("(k p) (h n) -> p k h n", p=P, n=DI)

            def width(j):
                return (j % TB + 1) * P

            with nc.Block() as block:
                @block.sync
                def _(sp):
                    with sp.Fori(0, HI // 2) as i:
                        for u in range(2):
                            sp.wait_ge(raw_free, 2 * i + u + 1)
                            sp.dma_start(w_raw[:, u, :, :], wqi[:, :, bass.ds(2 * i + u, 1), :]
                                         .rearrange("p k h n -> p k (h n)")).then_inc(raw_in[u], 16)

                @block.gpsimd
                def _(pool):
                    pool.sem_inc(raw_free, 2)
                    with pool.Fori(0, HI // 2) as i:
                        for u in range(2):
                            pool.wait_ge(raw_in[u], 16 * (i + 1))
                            pool.wait_ge(q_ps, NB * (2 * i + u + 1))
                            pool.sem_inc(stand, 1)
                            split_hi(pool, w_h[:, u, :, :], w_raw[:, u, :, :]).then_inc(w_hi, 1)
                            pool.wait_ge(w_hi, 2 * i + u + 1)
                            pool.tensor_tensor(w_l[:, u, :, :], w_raw[:, u, :, :],
                                               w_h[:, u, :, :].bitcast(F32), ALU.subtract)\
                                .then_inc(w_ready, 1)
                            pool.wait_ge(w_ready, 2 * i + u + 1)
                            pool.sem_inc(raw_free, 1)

                @block.tensor
                def _(pe):
                    pe.sem_inc(q_ps, 2 * NB)

                    def queries(h, u):
                        pe.wait_ge(w_ready, h + 1)
                        pe.wait_ge(q_lo, NB * h + NB)
                        for b in range(NB):
                            for k in range(KD):
                                last = matmul3(pe, ps[:, b, :], w_h[:, u, k, :], w_l[:, u, k, :],
                                               xnT_h[:, k, b * S:(b + 1) * S],
                                               xnT_l[:, k, b * S:(b + 1) * S], k == 0, k == KD - 1)
                            last.then_inc(q_ps, 1)

                    def scores(h, u):
                        for j in range(NT):
                            b = j // TB
                            if j % TB == 0:
                                pe.wait_ge(q_lo, NB * h + NB + b + 1)
                            pe.wait_ge(relu_ready, NT * h + (j + 1))
                            matmul3(pe, ps[:, 2 + j % NR, 0:width(j)],
                                    qT_h[:, u, j * P:(j + 1) * P], qT_l[:, u, j * P:(j + 1) * P],
                                    kiT_h[:, b * S:b * S + width(j)],
                                    kiT_l[:, b * S:b * S + width(j)], True, True).then_inc(lg_ps, 1)

                    pipeline(pe, HI, 2, queries, scores)

                @block.scalar
                def _(act):
                    act.sem_inc(relu_ready, NR)

                    def queries(h, u):
                        for b in range(NB):
                            act.wait_ge(q_ps, NB * h + (b + 1 + 2 * NB))
                            act.activation(qT_h[:, u, b * S:(b + 1) * S], ps[:, b, :],
                                           ACT.Copy).then_inc(q_hi, 1)

                    def scores(h, u):
                        for j in range(NT):
                            act.wait_ge(lg_ps, NT * h + j + 1)
                            act.wait_ge(relu_free, NT * h + j + 1)
                            act.activation(relu[:, j % NR, 0:width(j)], ps[:, 2 + j % NR, 0:width(j)],
                                           ACT.Relu).then_inc(relu_ready, 1)

                    pipeline(act, HI, 2, queries, scores)

                @block.vector
                def _(dve):
                    dve.sem_inc(relu_free, NR)
                    dve.sem_inc(q_lo, NB)

                    def queries(h, u):
                        for b in range(NB):
                            dve.wait_ge(q_hi, NB * h + b + 1)
                            dve.tensor_tensor(qT_l[:, u, b * S:(b + 1) * S], ps[:, b, :],
                                              qT_h[:, u, b * S:(b + 1) * S].bitcast(F32),
                                              ALU.subtract).then_inc(q_lo, 1)

                    def scores(h, u):
                        for j in range(NT):
                            dve.wait_ge(relu_ready, NT * h + (j + 1 + NR))
                            dve.scalar_tensor_tensor(
                                index[:, j, 0:width(j)], relu[:, j % NR, 0:width(j)],
                                small[:, j, bass.ds(h, 1)], index[:, j, 0:width(j)],
                                ALU.mult, ALU.add).then_inc(relu_free, 1)

                    pipeline(dve, HI, 2, queries, scores)

        with ExitStack() as c:
            s = sb_in(c)
            left = s("left", [P, NT, S])
            m8 = s("m8", [P, NT, 8])
            s_causal = sem("t_causal")
            s_round = sem("t_round")
            s_bias = sem("t_bias")
            ROUNDS = TOPK // 8
            with nc.Block() as block:
                @block.gpsimd
                def _(pool):
                    def causal(j):
                        diag = index[:, j, (j % TB) * P:(j % TB + 1) * P]
                        pool.affine_select(out=diag, in_=diag, compare_op=ALU.is_ge, fill=NEG, base=0,
                                           pattern=[[-1, P]], channel_multiplier=1).then_inc(s_causal, 1)

                    for j in range(NT):
                        causal(j)
                    for j in range(0, NT, TB):
                        pool.wait_ge(s_bias, j + 1)
                        causal(j)

                @block.vector
                def _(dve):
                    n = [0]

                    def then(ins):
                        n[0] += 1
                        ins.then_inc(s_round, 1)
                        dve.wait_ge(s_round, n[0])

                    for j in range(NT):
                        w = (j % TB + 1) * P
                        dve.wait_ge(s_causal, j + 1)
                        for r in range(ROUNDS):
                            src = index[:, j, 0:w] if r == 0 else left[:, j, 0:w]
                            then(dve.max(m8[:, j, :], src))
                            then(dve.match_replace(left[:, j, 0:w], m8[:, j, :], src, TAKEN))
                        dve.tensor_scalar(index[:, j, 0:w], left[:, j, 0:w], TAKEN, NEG,
                                          ALU.not_equal, ALU.mult).then_inc(s_bias, 1)
        li.close()

        with ExitStack() as c:
            s = sb_in(c)
            wq_raw = s("wq_raw", [P, 2, KD, HD])
            wo_raw = s("wo_raw", [P, 2, D])
            wq_h = s("wq_h", [P, 2, KD, HD], F32R)
            wq_l = s("wq_l", [P, 2, KD, HD], F32R)
            wo_h = s("wo_h", [P, 2, D], F32R)
            wo_l = s("wo_l", [P, 2, D], F32R)
            qT_h = s("qT_h", [P, 2, S], F32R)
            qT_l = s("qT_l", [P, 2, S], F32R)
            sc = s("sc", [P, 2, TB, S])
            nmax = s("nmax", [P, 2, TB])
            rowsum = s("rowsum", [P, 2, TB])
            rrec = s("rrec", [P, 2, TB])
            pr = s("pr", [P, 2, TB, S])
            pT_h = s("pT_h", [P, 2, TB, S], F32R)
            pT_l = s("pT_l", [P, 2, TB, S], F32R)
            oT_h = s("oT_h", [P, 2, S], F32R)
            oT_l = s("oT_l", [P, 2, S], F32R)
            zero = s("zero", [P, S])
            raw_in = [sem("a_raw0"), sem("a_raw1")]
            raw_free = sem("a_raw_free")
            w_hi = sem("a_w_hi")
            wq_ready = sem("a_wq_ready")
            wo_ready = sem("a_wo_ready")
            wo_used = sem("a_wo_used")
            s_zero = sem("a_zero")
            q_ps = sem("a_q_ps")
            q_hi = sem("a_q_hi")
            q_lo = sem("a_q_lo")
            sc_ps = sem("a_sc_ps")
            sc_ready = sem("a_sc_ready")
            exp_ready = sem("a_exp")
            r_ready = sem("a_r")
            pr_ready = sem("a_pr")
            pt_ps = sem("a_pt_ps")
            pt_hi = sem("a_pt_hi")
            pt_lo = sem("a_pt_lo")
            pv_ps = sem("a_pv_ps")
            o_hi = sem("a_o_hi")
            o_lo = sem("a_o_lo")
            s_res = sem("a_res")
            wq_v = wq.rearrange("(k p) (h n) -> p k h n", p=P, n=HD)
            wo_v = wo.rearrange("(h p) n -> p h n", p=HD)
            Q, S0, PT0, PV, WO0 = 0, 1, 3, 5, 6

            def width(j):
                return (j + 1) * P

            def heads(eng, b, project, attend, weigh, output):
                base = b * H

                def step(h, r, first=False, last=False):
                    if not first:
                        weigh(h - 1, (r + 1) % 2)
                    if not last:
                        project(h + 1, (r + 1) % 2)
                    if not first:
                        output(h - 1, (r + 1) % 2)
                    attend(h, r, not last)

                project(base, 0)
                attend(base - 1, 1, True, False)
                step(base, 0, first=True)
                with eng.Fori(0, H // 2 - 1) as i:
                    step(i * 2 + (base + 1), 1)
                    step(i * 2 + (base + 2), 0)
                step(base + H - 1, 1, last=True)
                weigh(base + H - 1, 1)
                output(base + H - 1, 1)

            with nc.Block() as block:
                @block.sync
                def _(sp):
                    with sp.Fori(0, NB) as b:
                        with sp.Fori(0, H // 2) as i:
                            for u in range(2):
                                sp.wait_ge(raw_free, b * H + 2 * i + (u + 1))
                                sp.dma_start(wq_raw[:, u, :, :], wq_v[:, :, bass.ds(2 * i + u, 1), :]
                                             .rearrange("p k h n -> p k (h n)")).then_inc(raw_in[u], 16)
                                sp.dma_start(wo_raw[:, u, :], wo_v[:, bass.ds(2 * i + u, 1), :]
                                             .rearrange("p h n -> p (h n)")).then_inc(raw_in[u], 16)

                @block.gpsimd
                def _(pool):
                    pool.sem_inc(raw_free, 2)
                    pool.memset(zero[:, :], 0.0).then_inc(s_zero, 1)
                    with pool.Fori(0, NB * H // 2) as i:
                        for u in range(2):
                            pool.wait_ge(raw_in[u], 32 * (i + 1))
                            pool.wait_ge(q_ps, 2 * i + (u + 1))
                            pool.sem_inc(stand, 1)
                            split_hi(pool, wq_h[:, u, :, :], wq_raw[:, u, :, :]).then_inc(w_hi, 1)
                            pool.wait_ge(w_hi, 4 * i + (2 * u + 1))
                            pool.tensor_tensor(wq_l[:, u, :, :], wq_raw[:, u, :, :],
                                               wq_h[:, u, :, :].bitcast(F32),
                                               ALU.subtract).then_inc(wq_ready, 1)
                            pool.wait_ge(wo_used, 2 * i + (u + 1))
                            pool.sem_inc(stand, 1)
                            split_hi(pool, wo_h[:, u, :], wo_raw[:, u, :]).then_inc(w_hi, 1)
                            pool.wait_ge(w_hi, 4 * i + (2 * u + 2))
                            pool.tensor_tensor(wo_l[:, u, :], wo_raw[:, u, :],
                                               wo_h[:, u, :].bitcast(F32),
                                               ALU.subtract).then_inc(wo_ready, 1)
                            pool.wait_ge(wq_ready, 2 * i + (u + 1))
                            pool.wait_ge(wo_ready, 2 * i + (u + 1))
                            pool.sem_inc(raw_free, 1)

                @block.tensor
                def _(pe):
                    pe.sem_inc(q_ps, 2)
                    pe.sem_inc(wo_used, 2)
                    pe.wait_ge(s_zero, 1)
                    for b in range(NB):
                        if b > 0:
                            pe.wait_ge(s_res, b * TB)
                        for m in range(TB // 2):
                            pe.matmul(ps[:, WO0 + m, :], ident[:, :], zero[:, :], start=True, stop=False,
                                      skip_group_check=True)

                        def project(h, u, b=b):
                            pe.wait_ge(wq_ready, h + 1)
                            pe.wait_ge(q_lo, h + 1)
                            for k in range(KD):
                                last = matmul3(pe, ps[:, Q, :], wq_h[:, u, k, :], wq_l[:, u, k, :],
                                               xnT_h[:, k, b * S:(b + 1) * S],
                                               xnT_l[:, k, b * S:(b + 1) * S], k == 0, k == KD - 1)
                            last.then_inc(q_ps, 1)

                        def score(h, u, j, b=b):
                            if j == 0:
                                pe.wait_ge(q_lo, h + 2)
                            pe.wait_ge(sc_ready, TB * h + (j + 1))
                            matmul3(pe, ps[:, S0 + j % 2, 0:width(j)], qT_h[:, u, j * P:(j + 1) * P],
                                    qT_l[:, u, j * P:(j + 1) * P], kT_h[:, b * S:b * S + width(j)],
                                    kT_l[:, b * S:b * S + width(j)], True, True).then_inc(sc_ps, 1)

                        def turn(h, u, j):
                            pe.wait_ge(pr_ready, TB * h + (j + 1))
                            pe.wait_ge(pt_lo, TB * h + (j + 1))
                            for n in range(j + 1):
                                last = pe.transpose(ps[:, PT0 + j % 2, n * P:(n + 1) * P],
                                                    pr[:, u, j, n * P:(n + 1) * P], ident[:, :])
                            last.then_inc(pt_ps, 1)

                        def attend(h, u, next_scores, transposes=True):
                            order = [(0, 0), (1, 0), (1, 1), (0, 1), (1, 2), (1, 3), (0, 2), (0, 3)]
                            for kind, j in order:
                                if kind == 0 and next_scores:
                                    score(h + 1, 1 - u, j)
                                if kind == 1 and transposes:
                                    turn(h, u, j)

                        def weigh(h, u, b=b):
                            pe.wait_ge(pt_lo, TB * h + 2 + TB)
                            pe.wait_ge(o_lo, h + 1)
                            for n in range(TB):
                                last = matmul3(pe, ps[:, PV, n * P:S], v_h[:, b * TB + n, :],
                                               v_l[:, b * TB + n, :], pT_h[:, u, n, n * P:S],
                                               pT_l[:, u, n, n * P:S], n == 0, n == TB - 1)
                            last.then_inc(pv_ps, 1)

                        def output(h, u):
                            pe.wait_ge(wo_ready, h + 1)
                            pe.wait_ge(o_lo, h + 2)
                            for j in range(TB):
                                o = ps[:, WO0 + j // 2, (j % 2) * D:(j % 2 + 1) * D]
                                last = matmul3(pe, o, oT_h[:, u, j * P:(j + 1) * P],
                                               oT_l[:, u, j * P:(j + 1) * P], wo_h[:, u, :],
                                               wo_l[:, u, :], False, False, skip_group_check=True)
                            last.then_inc(wo_used, 1)

                        heads(pe, b, project, attend, weigh, output)

                @block.scalar
                def _(act):
                    for b in range(NB):
                        def project(h, u):
                            act.wait_ge(q_ps, h + 3)
                            act.activation(qT_h[:, u, :], ps[:, Q, :], ACT.Copy).then_inc(q_hi, 1)

                        def attend(h, u, next_scores, transposes=True):
                            if transposes:
                                for j in range(TB):
                                    act.wait_ge(pt_ps, TB * h + (j + 1))
                                    act.activation(
                                        pT_h[:, u, 0:j + 1, j * P:(j + 1) * P],
                                        ps[:, PT0 + j % 2, 0:width(j)].rearrange("p (c t) -> p c t", t=P),
                                        ACT.Copy).then_inc(pt_hi, 1)
                            if next_scores:
                                for j in range(TB):
                                    act.wait_ge(sc_ready, TB * h + (j + TB + 2 + 1))
                                    act.activation(pr[:, 1 - u, j, 0:width(j)], sc[:, 1 - u, j, 0:width(j)],
                                                   ACT.Exp, bias=nmax[:, 1 - u, j:j + 1], scale=-1.0,
                                                   accum_out=rowsum[:, 1 - u, j:j + 1]).then_inc(exp_ready, 1)

                        def weigh(h, u):
                            act.wait_ge(pv_ps, h + 1)
                            act.activation(oT_h[:, u, :], ps[:, PV, :], ACT.Copy).then_inc(o_hi, 1)

                        def output(h, u):
                            pass

                        heads(act, b, project, attend, weigh, output)

                @block.vector
                def _(dve):
                    dve.sem_inc(q_lo, 1)
                    dve.sem_inc(o_lo, 1)
                    dve.sem_inc(sc_ready, 2)
                    dve.sem_inc(pt_lo, 2)
                    for b in range(NB):
                        def project(h, u):
                            dve.wait_ge(q_hi, h + 1)
                            dve.tensor_tensor(qT_l[:, u, :], ps[:, Q, :], qT_h[:, u, :].bitcast(F32),
                                              ALU.subtract).then_inc(q_lo, 1)

                        def masked(h, u, j, b=b):
                            dve.wait_ge(sc_ps, TB * h + (j + 1))
                            dve.sem_inc(stand, 1)
                            dve.tensor_tensor_reduce(
                                sc[:, u, j, 0:width(j)], ps[:, S0 + j % 2, 0:width(j)],
                                index[:, b * TB + j, 0:width(j)], -SCALE, 3e38, ALU.add, ALU.min,
                                nmax[:, u, j:j + 1]).then_inc(sc_ready, 1)

                        def normalise(h, u, j):
                            dve.wait_ge(exp_ready, TB * h + (j + 1))
                            dve.reciprocal(rrec[:, u, j:j + 1], rowsum[:, u, j:j + 1]).then_inc(r_ready, 1)
                            dve.wait_ge(r_ready, TB * h + (j + 1))
                            dve.tensor_scalar(pr[:, u, j, 0:width(j)], pr[:, u, j, 0:width(j)],
                                              rrec[:, u, j:j + 1], None, ALU.mult).then_inc(pr_ready, 1)

                        def turned(h, u, j):
                            dve.wait_ge(pt_hi, TB * h + (j + 1))
                            dst = pT_h[:, u, 0:j + 1, j * P:(j + 1) * P]
                            dve.tensor_tensor(
                                pT_l[:, u, 0:j + 1, j * P:(j + 1) * P],
                                ps[:, PT0 + j % 2, 0:width(j)].rearrange("p (c t) -> p c t", t=P),
                                dst.bitcast(F32), ALU.subtract).then_inc(pt_lo, 1)

                        def attend(h, u, next_scores, transposes=True):
                            for kind, j in [(0, 0), (1, 0), (1, 1), (0, 1), (1, 2), (1, 3), (0, 2), (0, 3)]:
                                if kind == 0 and next_scores:
                                    masked(h + 1, 1 - u, j)
                                if kind == 1 and transposes:
                                    turned(h, u, j)
                            if next_scores:
                                for j in range(TB):
                                    normalise(h + 1, 1 - u, j)

                        def weigh(h, u):
                            dve.wait_ge(o_hi, h + 1)
                            dve.tensor_tensor(oT_l[:, u, :], ps[:, PV, :], oT_h[:, u, :].bitcast(F32),
                                              ALU.subtract).then_inc(o_lo, 1)

                        def output(h, u):
                            pass

                        heads(dve, b, project, attend, weigh, output)
                        dve.wait_ge(wo_used, H * (b + 1) + 2)
                        for j in range(TB):
                            row = acc[:, b * TB + j, :]
                            dve.tensor_tensor(row, ps[:, WO0 + j // 2, (j % 2) * D:(j % 2 + 1) * D], row,
                                              ALU.add).then_inc(s_res, 1)

        with ExitStack() as c:
            s = sb_in(c)
            WE = KD * HE * 2 + HC * D
            raw = s("e_raw", [P, 2, WE])
            we_h = s("we_h", [P, 2, WE], F32R)
            we_l = s("we_l", [P, 2, WE], F32R)
            gate = s("e_gate_s", [P, 2, S])
            hid = s("e_hid", [P, 2, S])
            hT_h = s("e_hT_h", [P, 2, HC, S], F32R)
            hT_l = s("e_hT_l", [P, 2, HC, S], F32R)
            raw_in = [sem("e_raw0"), sem("e_raw1")]
            raw_free = sem("e_raw_free")
            w_hi = sem("e_w_hi")
            w_ready = sem("e_w_ready")
            gu_ps = sem("e_gu_ps")
            s_silu = sem("e_silu")
            s_hid = sem("e_hid_r")
            h_hi = sem("e_h_hi")
            h_lo = sem("e_h_lo")
            y_ps = sem("e_y_ps")
            y_free = sem("e_y_free")
            G0, U0, DN0 = 0, KD * HE, 2 * KD * HE

            def gate_w(w, v, k, n):
                return w[:, v, G0 + k * HE + n * P:G0 + k * HE + (n + 1) * P]

            def up_w(w, v, k, n):
                return w[:, v, U0 + k * HE + n * P:U0 + k * HE + (n + 1) * P]

            def down_w(w, v, n):
                return w[:, v, DN0 + n * D:DN0 + (n + 1) * D]

            UNITS = NE * NB
            with nc.Block() as block:
                @block.sync
                def _(sp):
                    with sp.Fori(0, NE // 2) as i:
                        for v in range(2):
                            sp.wait_ge(raw_free, 2 * i + (v + 1))
                            for at, w, n in ((G0, e_gate, KD), (U0, e_up, KD), (DN0, e_down, HC)):
                                m = w.shape[2]
                                sp.dma_start(raw[:, v, at:at + n * m].rearrange("p (k m) -> p k m", k=n),
                                             w[bass.ds(2 * i + v, 1), :, :]
                                             .rearrange("e (k p) m -> p (e k) m", p=P)).then_inc(raw_in[v], 16)

                @block.gpsimd
                def _(pool):
                    pool.sem_inc(raw_free, 2)
                    with pool.Fori(0, NE // 2) as i:
                        for v in range(2):
                            pool.wait_ge(raw_in[v], 48 * (i + 1))
                            pool.wait_ge(y_ps, NB * TB * (2 * i + (v + 1)))
                            pool.sem_inc(stand, 1)
                            split_hi(pool, we_h[:, v, :], raw[:, v, :]).then_inc(w_hi, 1)
                            pool.wait_ge(w_hi, 2 * i + (v + 1))
                            pool.tensor_tensor(we_l[:, v, :], raw[:, v, :], we_h[:, v, :].bitcast(F32),
                                               ALU.subtract).then_inc(w_ready, 1)
                            pool.wait_ge(w_ready, 2 * i + (v + 1))
                            pool.sem_inc(raw_free, 1)

                @block.tensor
                def _(pe):
                    pe.sem_inc(y_ps, 2 * NB * TB)

                    def hidden(q, r):
                        b, v = r % 2, r // 2
                        if b == 0:
                            pe.wait_ge(w_ready, q // 2 + 1 if isinstance(q, int) else (q - b) // 2 + 1)
                        for n in range(HC):
                            g = n % 2
                            pe.wait_ge(s_hid, HC * q + (n + 1))
                            for bank, w_of in ((2 * g, gate_w), (2 * g + 1, up_w)):
                                for k in range(KD):
                                    last = matmul3(pe, ps[:, bank, :], w_of(we_h, v, k, n), w_of(we_l, v, k, n),
                                                   xnT_h[:, k, b * S:(b + 1) * S],
                                                   xnT_l[:, k, b * S:(b + 1) * S], k == 0, k == KD - 1)
                            last.then_inc(gu_ps, 1)

                    def down(q, r):
                        b, v = r % 2, r // 2
                        pe.wait_ge(h_lo, HC * q + HC)
                        for j in range(TB):
                            if j % 2 == 0:
                                pe.wait_ge(y_free, TB * q + (j + 2))
                            for n in range(HC):
                                last = matmul3(pe, ps[:, 4 + 2 * b + j // 2, (j % 2) * D:(j % 2 + 1) * D],
                                               hT_h[:, b, n, j * P:(j + 1) * P], hT_l[:, b, n, j * P:(j + 1) * P],
                                               down_w(we_h, v, n), down_w(we_l, v, n), n == 0, n == HC - 1)
                            last.then_inc(y_ps, 1)

                    pipeline(pe, UNITS, 4, hidden, down)

                @block.scalar
                def _(act):
                    def hidden(q, r):
                        b = r % 2
                        for n in range(HC):
                            act.wait_ge(gu_ps, HC * q + (n + 1))
                            act.activation(gate[:, n % 2, :], ps[:, 2 * (n % 2), :], ACT.Silu).then_inc(s_silu, 1)
                            act.wait_ge(s_hid, HC * q + (n + 3))
                            act.activation(hT_h[:, b, n, :], hid[:, n % 2, :], ACT.Copy).then_inc(h_hi, 1)

                    def down(q, r):
                        pass

                    pipeline(act, UNITS, 4, hidden, down)

                @block.vector
                def _(dve):
                    dve.sem_inc(s_hid, 2)
                    dve.sem_inc(y_free, 2 * TB)

                    def hidden(q, r):
                        b = r % 2
                        for n in range(HC):
                            dve.wait_ge(s_silu, HC * q + (n + 1))
                            dve.tensor_tensor(hid[:, n % 2, :], gate[:, n % 2, :], ps[:, 2 * (n % 2) + 1, :],
                                              ALU.mult).then_inc(s_hid, 1)
                            dve.wait_ge(h_hi, HC * q + (n + 1))
                            dve.tensor_tensor(hT_l[:, b, n, :], hid[:, n % 2, :], hT_h[:, b, n, :].bitcast(F32),
                                              ALU.subtract).then_inc(h_lo, 1)

                    def down(q, r):
                        b = r % 2
                        for j in range(TB):
                            row = acc[:, b * TB + j, :]
                            if j % 2 == 0:
                                dve.wait_ge(y_ps, TB * q + (j + 2 + 2 * NB * TB))
                            dve.scalar_tensor_tensor(
                                row, ps[:, 4 + 2 * b + j // 2, (j % 2) * D:(j % 2 + 1) * D],
                                combine[:, b * TB + j, bass.ds((q - b) // 2, 1)], row,
                                ALU.mult, ALU.add).then_inc(y_free, 1)

                    pipeline(dve, UNITS, 4, hidden, down)
        l0.close()

        CH = KD
        assert w_x.shape[1] == R + 2 * NS
        dt = sb("dt", [P, CH, TOK])
        xdt = sb("xdt", [P, CH, TOK])
        yT = sb("yT", [P, CH, TOK])
        a_neg = sb("a_neg", [P, CH, NS])
        with ExitStack() as c:
            s = sb_in(c)
            xf = s("xf", [P, KD, TOK])
            w_xs = s("w_xs", [P, KD, R + 2 * NS])
            w_xh = s("w_xh", [P, KD, R + 2 * NS], F32R)
            w_xl = s("w_xl", [P, KD, R + 2 * NS], F32R)
            w_ds = s("w_ds", [R, D])
            w_dh = s("w_dh", [R, D], F32R)
            w_dl = s("w_dl", [R, D], F32R)
            bd = s("bd", [P, CH])
            ds_ = s("dskip", [P, CH])
            dl_h = s("dl_h", [R, TOK], F32R)
            dl_l = s("dl_l", [R, TOK], F32R)
            bc = s("bc", [R + 2 * NS, TOK])
            soft = s("soft", [P, CH, TOK])
            wx_in = sem("m_wx_in")
            wd_in = sem("m_wd_in")
            al_in = sem("m_al_in")
            wx_split = sem("m_wx_split")
            wd_split = sem("m_wd_split")
            s_stat = sem("m_stat")
            s_std = sem("m_std")
            s_rstd = sem("m_rstd")
            s_xn = sem("m_xn")
            s_xt = sem("m_xt")
            xt_hi = sem("m_xt_hi")
            xt_lo = sem("m_xt_lo")
            xp_ps = sem("m_xp_ps")
            dl_hi = sem("m_dl_hi")
            dl_lo = sem("m_dl_lo")
            s_bc = sem("m_bc")
            bc_out = sem("m_bc_out")
            dt_ps = sem("m_dt_ps")
            s_abs = sem("m_abs")
            s_soft = sem("m_soft")
            s_relu = sem("m_relu")
            s_dt = sem("m_dt")
            s_a = sem("m_a")
            s_fin = sem("m_fin")
            with nc.Block() as block:
                @block.sync
                def _(sp):
                    sp.dma_start(w_xs[:, :, :], w_x.rearrange("(k p) n -> p k n", p=P)).then_inc(wx_in, 16)
                    sp.dma_start(w_ds[:, :], w_dt).then_inc(wd_in, 16)
                    sp.dma_start(a_neg[:, :, :], a_log.rearrange("(k p) n -> p k n", p=P)).then_inc(al_in, 16)
                    sp.dma_start(bd[:, :], b_dt).then_inc(al_in, 16)
                    sp.dma_start(ds_[:, :], d_skip).then_inc(al_in, 16)
                    sp.wait_ge(s_bc, NB)
                    sp.dma_start(bc_dram.rearrange("g n t -> (g n) t"), bc[R:R + 2 * NS, :]).then_inc(bc_out, 16)
                    sp.wait_ge(bc_out, 16)

                @block.gpsimd
                def _(pool):
                    pool.wait_ge(wx_in, 16)
                    split_hi(pool, w_xh[:, :, :], w_xs[:, :, :]).then_inc(wx_split, 1)
                    pool.wait_ge(wx_split, 1)
                    pool.tensor_tensor(w_xl[:, :, :], w_xs[:, :, :], w_xh[:, :, :].bitcast(F32),
                                       ALU.subtract).then_inc(wx_split, 1)
                    pool.wait_ge(wd_in, 16)
                    split_hi(pool, w_dh[:, :], w_ds[:, :]).then_inc(wd_split, 1)
                    pool.wait_ge(wd_split, 1)
                    pool.tensor_tensor(w_dl[:, :], w_ds[:, :], w_dh[:, :].bitcast(F32),
                                       ALU.subtract).then_inc(wd_split, 1)

                @block.tensor
                def _(pe):
                    transpose_rows(pe, s_xn, s_xt)
                    pe.wait_ge(wx_split, 2)
                    for b in range(NB):
                        pe.wait_ge(xt_lo, (b + 1) * TB // 2)
                        for k in range(KD):
                            last = matmul3(pe, ps[0:R + 2 * NS, 4 + b, :], w_xh[:, k, :], w_xl[:, k, :],
                                           xnT_h[:, k, b * S:(b + 1) * S], xnT_l[:, k, b * S:(b + 1) * S],
                                           k == 0, k == KD - 1)
                        last.then_inc(xp_ps, 1)
                    pe.wait_ge(wd_split, 2)
                    for b in range(NB):
                        pe.wait_ge(dl_lo, b + 1)
                        for k in range(CH):
                            matmul3(pe, ps[:, 2 * b + k, :], w_dh[:, k * P:(k + 1) * P],
                                    w_dl[:, k * P:(k + 1) * P], dl_h[:, b * S:(b + 1) * S],
                                    dl_l[:, b * S:(b + 1) * S], True, True).then_inc(dt_ps, 1)

                @block.scalar
                def _(act):
                    act.wait_ge(s_stat, 2 * NT + 1)
                    act.activation(std[:, :], std[:, :], ACT.Sqrt).then_inc(s_std, 1)
                    for g in range(NT // 2):
                        act.wait_ge(s_xt, g + 1)
                        act.activation(pair(xnT_h, g), bank_pair(g), ACT.Copy).then_inc(xt_hi, 1)
                        act.activation(pair(xf, g), bank_pair(g), ACT.Copy).then_inc(xt_hi, 1)
                    for b in range(NB):
                        act.wait_ge(xp_ps, b + 1)
                        act.activation(dl_h[:, b * S:(b + 1) * S], ps[0:R, 4 + b, :], ACT.Copy).then_inc(dl_hi, 1)
                        act.activation(bc[R:R + 2 * NS, b * S:(b + 1) * S], ps[R:R + 2 * NS, 4 + b, :],
                                       ACT.Copy).then_inc(s_bc, 1)
                    act.wait_ge(al_in, 48)
                    for n in range(NB * CH):
                        b, k = n // CH, n % CH
                        act.wait_ge(dt_ps, n + 1)
                        act.activation(soft[:, k, b * S:(b + 1) * S], ps[:, n, :], ACT.Abs,
                                       bias=bd[:, k:k + 1]).then_inc(s_abs, 1)
                    act.wait_ge(s_abs, NB * CH)
                    act.activation(soft[:, :, :], soft[:, :, :], ACT.Exp, scale=-1.0).then_inc(s_soft, 1)
                    act.wait_ge(s_soft, 1)
                    act.activation(soft[:, :, :], soft[:, :, :], ACT.Ln, bias=1.0).then_inc(s_soft, 1)
                    act.activation(a_neg[:, :, :], a_neg[:, :, :], ACT.Exp).then_inc(s_a, 1)

                @block.vector
                def _(dve):
                    layernorm_vector(dve, None, s_stat, s_std, s_rstd, s_xn)
                    for g in range(NT // 2):
                        dve.wait_ge(xt_hi, 2 * g + 2)
                        dve.tensor_tensor(pair(xnT_l, g), pair(xf, g), pair(xnT_h, g).bitcast(F32),
                                          ALU.subtract).then_inc(xt_lo, 1)
                    for b in range(NB):
                        dve.wait_ge(dl_hi, b + 1)
                        dve.wait_ge(s_bc, b + 1)
                        dve.tensor_tensor(dl_l[:, b * S:(b + 1) * S], ps[0:R, 4 + b, :],
                                          dl_h[:, b * S:(b + 1) * S].bitcast(F32),
                                          ALU.subtract).then_inc(dl_lo, 1)
                    dve.wait_ge(al_in, 48)
                    for k in range(CH):
                        dve.tensor_scalar(yT[:, k, :], xf[:, k, :], ds_[:, k:k + 1], None,
                                          ALU.mult).then_inc(s_fin, 1)
                    for n in range(NB * CH):
                        b, k = n // CH, n % CH
                        dve.wait_ge(s_abs, n + 1)
                        dve.tensor_scalar(dt[:, k, b * S:(b + 1) * S], ps[:, n, :], bd[:, k:k + 1], 0.0,
                                          ALU.add, ALU.max).then_inc(s_relu, 1)
                    dve.wait_ge(s_a, 1)
                    dve.tensor_scalar(a_neg[:, :, :], a_neg[:, :, :], -1.0, None, ALU.mult).then_inc(s_fin, 1)
                    dve.wait_ge(s_relu, NB * CH)
                    dve.wait_ge(s_soft, 2)
                    dve.tensor_tensor(dt[:, :, :], dt[:, :, :], soft[:, :, :], ALU.add).then_inc(s_dt, 1)
                    dve.wait_ge(s_dt, 1)
                    dve.tensor_tensor(xdt[:, :, :], dt[:, :, :], xf[:, :, :], ALU.mult).then_inc(s_fin, 1)

        with ExitStack() as c:
            s = sb_in(c)
            bcast = s("bcast", [P, 2, 2, TOK])
            da = s("da", [P, 2, CH, NB, S])
            dbx = s("dbx", [P, CH, TOK])
            hst = s("hst", [P, CH, TOK])
            hc = s("hc", [P, 2, CH, TOK])
            fraw = s("fraw", [P, 1024])
            xcur_h = s("xcur_h", [P, KD, P], F32R)
            xcur_l = s("xcur_l", [P, KD, P], F32R)
            wg_h = s("wg_h", [P, KD, FI], F32R)
            wg_l = s("wg_l", [P, KD, FI], F32R)
            wu_h = s("wu_h", [P, KD, FI], F32R)
            wu_l = s("wu_l", [P, KD, FI], F32R)
            wd_h = s("wd_h", [P, FC, D], F32R)
            wd_l = s("wd_l", [P, FC, D], F32R)
            sil = s("sil", [P, 2, 512])
            hid = s("f_hid", [P, FI])
            mag = s("f_mag", [P, FI])
            cmp = s("f_cmp", [P, 6, FI // 4], BF16)
            win = s("f_win", [P, 8, FI // 4], BF16)
            hT = s("f_hT", [P, FC, P])
            hT_h = s("f_hT_h", [P, FC, P], F32R)
            hT_l = s("f_hT_l", [P, FC, P], F32R)
            bc_in = [sem("z_bc0"), sem("z_bc1")]
            da_zero = sem("z_da_zero")
            x_cur = sem("z_x_cur")
            acc_add = sem("z_acc_add")
            da_ready = sem("z_da")
            s_dbx = sem("z_dbx")
            s_scan = sem("z_scan")
            hc_ready = sem("z_hc")
            y_add = sem("z_y_add")
            fr_in = sem("z_fr_in")
            fr_hi = sem("z_fr_hi")
            fr_lo = sem("z_fr_lo")
            gu_ps = sem("z_gu_ps")
            s_silu = sem("z_silu")
            s_prod = sem("z_prod")
            s_abs = sem("z_abs")
            s_cmp = sem("z_cmp")
            s_sparse = sem("z_sparse")
            ht_ps = sem("z_ht_ps")
            ht_cp = sem("z_ht_cp")
            ht_hi = sem("z_ht_hi")
            ht_lo = sem("z_ht_lo")
            dn_ps = sem("z_dn_ps")
            yt_ps = sem("z_yt_ps")
            s_out = sem("z_out")
            out_done = sem("z_out_done")
            bc_v = bc_dram.rearrange("g n t -> n g t")
            pieces = []
            for w, hi, lo in ((f_gate, wg_h, wg_l), (f_up, wu_h, wu_l)):
                for k in range(KD):
                    pieces.append((w[k * P:(k + 1) * P, :], hi[:, k, :], lo[:, k, :]))
            for m in range(2):
                half = FC // 2
                src = f_down[m * half * P:(m + 1) * half * P, :].rearrange("(c p) n -> p c n", p=P)
                pieces.append((src, wd_h[:, m * half:(m + 1) * half, :], wd_l[:, m * half:(m + 1) * half, :]))

            def piece_raw(ap):
                if len(ap.shape) == 2:
                    return fraw[:, 0:ap.shape[1]]
                return fraw[:, :].rearrange("p (c n) -> p c n", n=ap.shape[2])

            NSTEP = NS // NT
            with nc.Block() as block:
                @block.sync
                def _(sp):
                    for n, (src, _, _) in enumerate(pieces):
                        if n > 0:
                            sp.wait_ge(fr_lo, n)
                        sp.dma_start(piece_raw(src), src).then_inc(fr_in, 16)
                    with sp.Fori(0, NS // 2) as i:
                        for u in range(2):
                            sp.wait_ge(hc_ready, 2 * i + (u + 1))
                            sp.dma_start(bcast[:, u, :, :], bc_v[bass.ds(2 * i + u, 1), :, :]
                                         .broadcast_to([P, 2, TOK])).then_inc(bc_in[u], 16)
                    for b in range(NB):
                        sp.wait_ge(s_out, TB // 2 * (b + 1))
                        sp.dma_start(out_rows[:, b * TB:(b + 1) * TB, :],
                                     acc[:, b * TB:(b + 1) * TB, :]).then_inc(out_done, 16)
                    sp.wait_ge(out_done, 16 * NB)

                @block.gpsimd
                def _(pool):
                    pool.sem_inc(y_add, 2)
                    pool.sem_inc(ht_lo, 1)
                    for u in range(2):
                        for k in range(CH):
                            pool.memset(da[:, u, k, :, 0:1], 0.0).then_inc(da_zero, 1)
                    for n, (src, hi, lo) in enumerate(pieces):
                        pool.wait_ge(fr_in, 16 * (n + 1))
                        split_hi(pool, hi, piece_raw(src)).then_inc(fr_hi, 1)
                        pool.wait_ge(fr_hi, n + 1)
                        pool.tensor_tensor(lo, piece_raw(src), hi.bitcast(F32), ALU.subtract).then_inc(fr_lo, 1)
                    with pool.Fori(0, NT) as i:
                        pool.wait_ge(ht_cp, 2 * i + 4)
                        pool.wait_ge(dn_ps, i + 1)
                        pool.sem_inc(stand, 1)
                        split_hi(pool, hT_h[:, :, :], hT[:, :, :]).then_inc(ht_hi, 1)
                        pool.wait_ge(ht_hi, i + 1)
                        pool.tensor_tensor(hT_l[:, :, :], hT[:, :, :], hT_h[:, :, :].bitcast(F32),
                                           ALU.subtract).then_inc(ht_lo, 1)
                        for u in range(2):
                            pool.wait_ge(hc_ready, 2 * i + (u + 3))
                            pool.wait_ge(y_add, 2 * i + (u + 2))
                            pool.tensor_tensor(yT[:, :, :], yT[:, :, :], hc[:, u, :, :],
                                               ALU.add).then_inc(y_add, 1)

                @block.tensor
                def _(pe):
                    pe.sem_inc(dn_ps, 1)
                    pe.wait_ge(fr_lo, len(pieces))

                    def hidden(i, r):
                        pe.wait_ge(x_cur, 2 * i + 2)
                        for m in range(2):
                            pe.wait_ge(s_prod, 2 * i + (m + 1))
                            for bank, wh, wl in ((2 * m, wg_h, wg_l), (2 * m + 1, wu_h, wu_l)):
                                for k in range(KD):
                                    last = matmul3(pe, ps[:, bank, :], xcur_h[:, k, :], xcur_l[:, k, :],
                                                   wh[:, k, m * 512:(m + 1) * 512],
                                                   wl[:, k, m * 512:(m + 1) * 512], k == 0, k == KD - 1)
                            last.then_inc(gu_ps, 1)

                    def down(i, r):
                        pe.wait_ge(s_sparse, 4 * i + 4)
                        pe.wait_ge(ht_cp, 2 * i + 2)
                        for m in range(2):
                            for n in range(4):
                                q = 4 * m + n
                                last = pe.transpose(ps[:, 4 + m, n * P:(n + 1) * P],
                                                    hid[:, q * P:(q + 1) * P], ident[:, :])
                            last.then_inc(ht_ps, 1)
                        pe.wait_ge(ht_lo, i + 2)
                        pe.wait_ge(acc_add, i + 1)
                        for n in range(FC):
                            last = matmul3(pe, ps[:, 6, 0:D], hT_h[:, n, :], hT_l[:, n, :], wd_h[:, n, :],
                                           wd_l[:, n, :], n == 0, n == FC - 1)
                        last.then_inc(dn_ps, 1)

                    pipeline(pe, NT, 1, hidden, down)
                    pe.wait_ge(y_add, NS + 2)
                    for g in range(NT // 2):
                        for m in range(2):
                            for k in range(CH):
                                last = pe.transpose(ps[:, g, (2 * m + k) * P:(2 * m + k + 1) * P],
                                                    yT[:, k, (2 * g + m) * P:(2 * g + m + 1) * P], ident[:, :])
                        last.then_inc(yt_ps, 1)

                @block.scalar
                def _(act):
                    act.sem_inc(ht_cp, 2)

                    def decay(i, u):
                        act.wait_ge(s_scan, 2 * i + (u + 1))
                        for k in range(CH):
                            act.activation(da[:, u, k, :, 1:S],
                                           dt[:, k, :].rearrange("p (b t) -> p b t", b=NB)[:, :, 1:S],
                                           ACT.Exp, scale=a_neg[:, k, bass.ds(2 * i + u, 1)])\
                                .then_inc(da_ready, 1)

                    def silu(i):
                        act.wait_ge(gu_ps, 2 * i + 1)
                        for m in range(2):
                            act.wait_ge(gu_ps, 2 * i + (m + 1))
                            act.activation(sil[:, m, :], ps[:, 2 * m, :], ACT.Silu).then_inc(s_silu, 1)

                    def fetch(i):
                        for src, dst in ((xnT_h, xcur_h), (xnT_l, xcur_l)):
                            act.activation(dst[:, :, :], src[:, :, bass.ds(i * P, P)], ACT.Copy)\
                                .then_inc(x_cur, 1)

                    def magnitude(i):
                        act.wait_ge(s_prod, 2 * i + 4)
                        act.activation(mag[:, :], hid[:, :], ACT.Abs).then_inc(s_abs, 1)

                    def turned(i):
                        act.wait_ge(ht_lo, i + 1)
                        for m in range(2):
                            act.wait_ge(ht_ps, 2 * i + (m + 1))
                            act.activation(hT[:, 4 * m:4 * m + 4, :],
                                           ps[:, 4 + m, :].rearrange("p (c t) -> p c t", t=P),
                                           ACT.Copy).then_inc(ht_cp, 1)

                    act.wait_ge(da_zero, 4)
                    fetch(0)
                    silu(0)
                    magnitude(0)
                    decay(0, 0)
                    decay(0, 1)
                    with act.Fori(0, NT - 1) as i:
                        act.wait_ge(gu_ps, 2 * i + 2)
                        fetch(i + 1)
                        turned(i)
                        silu(i + 1)
                        decay(i + 1, 0)
                        magnitude(i + 1)
                        decay(i + 1, 1)
                    turned(NT - 1)

                @block.vector
                def _(dve):
                    dve.sem_inc(s_scan, 2)
                    dve.sem_inc(hc_ready, 2)
                    dve.sem_inc(s_prod, 2)
                    dve.sem_inc(acc_add, 1)

                    def state(i, u):
                        dve.wait_ge(bc_in[u], 16 * (i + 1))
                        b_all = bcast[:, u, 0:1, :].broadcast_to([P, CH, TOK])
                        c_all = bcast[:, u, 1:2, :].broadcast_to([P, CH, TOK])
                        dve.tensor_tensor(dbx[:, :, :], xdt[:, :, :], b_all, ALU.mult).then_inc(s_dbx, 1)
                        dve.wait_ge(s_dbx, 2 * i + (u + 1))
                        dve.wait_ge(da_ready, 4 * i + (2 * u + 2))
                        dve.tensor_tensor_scan(hst[:, :, :].rearrange("p k t -> p (k t)"),
                                               da[:, u, :, :, :].rearrange("p k b t -> p (k b t)"),
                                               dbx[:, :, :].rearrange("p k t -> p (k t)"), 0.0,
                                               ALU.mult, ALU.add).then_inc(s_scan, 1)
                        dve.wait_ge(s_scan, 2 * i + (u + 3))
                        dve.wait_ge(y_add, 2 * i + (u + 1))
                        dve.tensor_tensor(hc[:, u, :, :], hst[:, :, :], c_all, ALU.mult).then_inc(hc_ready, 1)

                    def product(i):
                        dve.wait_ge(ht_ps, 2 * i)
                        product_first(i)

                    def product_first(i):
                        for m in range(2):
                            dve.wait_ge(s_silu, 2 * i + (m + 1))
                            dve.tensor_tensor(hid[:, m * 512:(m + 1) * 512], sil[:, m, :], ps[:, 2 * m + 1, :],
                                              ALU.mult).then_inc(s_prod, 1)

                    def sparsify(i):
                        h4 = hid[:, :].rearrange("p (g f) -> p f g", f=4)
                        a4 = mag[:, :].rearrange("p (g f) -> p f g", f=4)
                        G = FI // 4
                        dve.wait_ge(s_abs, i + 1)
                        for at, first, n in ((0, 0, 3), (3, 1, 2), (5, 2, 1)):
                            dve.tensor_tensor(cmp[:, at:at + n, :],
                                              a4[:, first:first + 1, :].broadcast_to([P, n, G]),
                                              a4[:, first + 1:4, :], ALU.is_ge).then_inc(s_cmp, 1)
                        c01, c02, c03, c12, c13, c23 = (cmp[:, n, :] for n in range(6))
                        dve.wait_ge(s_cmp, 10 * i + 3)
                        dve.tensor_tensor(win[:, 0, :], c01, c02, ALU.add).then_inc(s_cmp, 1)
                        dve.tensor_tensor(win[:, 1:3, :], cmp[:, 3:5, :], cmp[:, 4:6, :], ALU.add)\
                            .then_inc(s_cmp, 1)
                        dve.tensor_tensor(win[:, 3, :], c02, c12, ALU.add).then_inc(s_cmp, 1)
                        dve.wait_ge(s_cmp, 10 * i + 6)
                        dve.tensor_tensor(win[:, 5, :], win[:, 1, :], c01, ALU.subtract).then_inc(s_cmp, 1)
                        dve.tensor_tensor(win[:, 4, :], win[:, 0, :], c03, ALU.add).then_inc(s_cmp, 1)
                        dve.tensor_tensor(win[:, 7, :], win[:, 2, :], c03, ALU.add).then_inc(s_cmp, 1)
                        dve.tensor_tensor(win[:, 6, :], c23, win[:, 3, :], ALU.subtract).then_inc(s_cmp, 1)
                        dve.wait_ge(s_cmp, 10 * i + 10)
                        for f, bound, op in ((0, 2.0, ALU.is_ge), (1, 1.0, ALU.is_ge), (3, 1.0, ALU.is_le),
                                             (2, 0.0, ALU.is_ge)):
                            dve.scalar_tensor_tensor(h4[:, f, :], win[:, 4 + f, :], bound, h4[:, f, :],
                                                     op, ALU.mult).then_inc(s_sparse, 1)

                    def residual(i):
                        dve.wait_ge(dn_ps, i + 2)
                        row = acc[:, bass.ds(i, 1), :].rearrange("p a d -> p (a d)")
                        dve.tensor_tensor(row, ps[:, 6, 0:D], row, ALU.add).then_inc(acc_add, 1)

                    product_first(0)
                    sparsify(0)
                    with dve.Fori(0, NT - 1) as i:
                        state(i, 0)
                        product(i + 1)
                        state(i, 1)
                        sparsify(i + 1)
                        residual(i)
                    state(NT - 1, 0)
                    state(NT - 1, 1)
                    residual(NT - 1)
                    dve.wait_ge(acc_add, NT + 1)
                    for g in range(NT // 2):
                        dve.wait_ge(yt_ps, g + 1)
                        rows = acc[:, 2 * g:2 * g + 2, :].rearrange("p j d -> p (j d)")
                        dve.tensor_tensor(rows, ps[:, g, :], rows, ALU.add).then_inc(s_out, 1)


_INS = ['L0_attn_x', 'L0_attn_wq_idx', 'L0_attn_wk_idx', 'L0_attn_w_iw', 'L0_attn_wq', 'L0_attn_wk',
        'L0_attn_wv', 'L0_attn_wo', 'L0_ffn_w_router', 'L0_ffn_w_gate', 'L0_ffn_w_up', 'L0_ffn_w_down',
        'L1_attn_A_log', 'L1_attn_D_skip', 'L1_attn_W_x', 'L1_attn_W_dt', 'L1_attn_b_dt',
        'L1_ffn_w_gate', 'L1_ffn_w_up', 'L1_ffn_w_down']


def kernel(**inputs):
    import numpy as _np
    import concourse.bacc as _bacc
    from concourse import mybir as _mybir
    from concourse.bass_utils import run_bass_kernel_spmd as _run

    nc = _bacc.Bacc("TRN2", target_bir_lowering=False, num_devices=1)
    arrays, args = {}, []
    for name in _INS:
        a = inputs[name]
        if a.ndim == 1:
            a = a.reshape(-1, P).T
        a = _np.ascontiguousarray(a)
        arrays[f"in_{name}"] = a
        args.append(nc.dram_tensor(f"in_{name}", a.shape, _mybir.dt.from_np(a.dtype), kind="ExternalInput").ap())
    shape = inputs['L0_attn_x'].shape
    args.append(nc.dram_tensor("out", shape, _mybir.dt.float32, kind="ExternalOutput").ap())
    two_layers(nc, *args)
    r = _run(nc, [arrays], core_ids=[0])
    return r.results[0]["out"]
```

```python
from contextlib import ExitStack

import concourse.bass as bass
from concourse import mybir

F32 = mybir.dt.float32
F32R = mybir.dt.float32r
BF16 = mybir.dt.bfloat16
U32 = mybir.dt.uint32
I32 = mybir.dt.int32
ALU = mybir.AluOpType
ACT = mybir.ActivationFunctionType
AX = mybir.AxisListType

P = 128
NEG = -1e30
TAKEN = -3e38
EPS = 1e-5


def pipeline(eng, n, unroll, front, back):
    front(0, 0)
    with eng.Fori(0, n // unroll - 1) as i:
        for r in range(unroll):
            front(i * unroll + (r + 1), (r + 1) % unroll)
            back(i * unroll + r, r)
    base = n - unroll
    for r in range(unroll):
        if r + 1 < unroll:
            front(base + r + 1, r + 1)
        back(base + r, r)


def matmul3(pe, out, w_hi, w_lo, x_hi, x_lo, start, stop, **kw):
    pe.matmul(out, w_hi, x_hi, start=start, stop=False, **kw)
    pe.matmul(out, w_hi, x_lo, start=False, stop=False, **kw)
    return pe.matmul(out, w_lo, x_hi, start=False, stop=stop, **kw)


def split_hi(pool, hi, src):
    return pool.tensor_scalar(hi, src, 1.0, 1.0, ALU.mult, ALU.mult)


def two_layers(nc, x, wq_idx, wk_idx, w_iw, wq, wk, wv, wo, w_router, e_weights,
               a_log, d_skip, w_x, w_dt, b_dt, f_weights, out):
    NB, S, D = x.shape
    KD = D // P
    TOK = NB * S
    NT = TOK // P
    TB = S // P
    DI = wk_idx.shape[1]
    HI = w_iw.shape[1]
    HD = wk.shape[1]
    H = wq.shape[1] // HD
    SCALE = float(HD) ** -0.5
    NE, _, WE = e_weights.shape
    HE = WE // (3 * KD)
    HC = HE // P
    PICKS = 2
    BLOCKS = PICKS * TOK // P + NE
    assert (PICKS * TOK + NE * (P - 1)) // P <= BLOCKS
    NS = a_log.shape[1]
    R = w_dt.shape[0]
    FI = f_weights.shape[1] // (3 * KD)
    FC = FI // P
    TOPK = 32
    assert DI == P and HD == P and S == 512 and D == 256

    x_rows = x.rearrange("b (j p) d -> p (b j) d", p=P)
    out_rows = out.rearrange("b (j p) d -> p (b j) d", p=P)
    slots_dram = nc.dram_tensor("slots_scratch", [BLOCKS * P, D], F32).ap()
    y_dram = nc.dram_tensor("y_scratch", [BLOCKS * P, D], F32).ap()
    bc_dram = nc.dram_tensor("bc_scratch", [2, NS, TOK], F32).ap()

    with ExitStack() as top:
        def sem(name):
            return top.enter_context(nc.semaphore(name))

        def sb_in(ctx):
            def sb(name, shape, dt=F32):
                return ctx.enter_context(nc.sbuf_tensor(name, shape, dt))
            return sb

        sb = sb_in(top)
        ps = top.enter_context(nc.psum_tensor("ps", [P, 8, 512], F32))
        acc = sb("acc", [P, NT, D])
        ident = sb("ident", [P, P])
        stand = sem("stand")
        stats = sb("stats", [P, NT, 6])
        mv = sb("mv", [P, NT, 2])
        std = sb("std", [P, NT])
        rstd = sb("rstd", [P, NT])
        xn = sb("xn", [P, NT, D])
        xnT_h = sb("xnT_h", [P, KD, TOK], F32R)
        xnT_l = sb("xnT_l", [P, KD, TOK], F32R)

        def layernorm_vector(dve, have_x, s_stat, s_std, s_rstd, s_xn):
            for j in range(NT):
                if have_x is not None and j % TB == 0:
                    dve.wait_ge(have_x[j // TB], 16)
                dve.bn_stats(stats[:, j, :], acc[:, j, :]).then_inc(s_stat, 1)
            for j in range(NT):
                dve.wait_ge(s_stat, j + 1)
                dve.bn_aggr(mv[:, j, :], stats[:, j, :]).then_inc(s_stat, 1)
            dve.wait_ge(s_stat, 2 * NT)
            dve.tensor_scalar(std[:, :], mv[:, :, 1], EPS, None, ALU.add).then_inc(s_stat, 1)
            dve.wait_ge(s_std, 1)
            dve.reciprocal(rstd[:, :], std[:, :]).then_inc(s_rstd, 1)
            dve.wait_ge(s_rstd, 1)
            for j in range(NT):
                dve.tensor_scalar(xn[:, j, :], acc[:, j, :], mv[:, j, 0:1], rstd[:, j:j + 1],
                                  ALU.subtract, ALU.mult).then_inc(s_xn, 1)

        def transpose_rows(pe, s_xn, s_xt):
            for g in range(NT // 2):
                pe.wait_ge(s_xn, 2 * g + 2)
                for k in range(KD):
                    for m in range(2):
                        last = pe.transpose(ps[:, g, (2 * k + m) * P:(2 * k + m + 1) * P],
                                            xn[:, 2 * g + m, k * P:(k + 1) * P], ident[:, :])
                last.then_inc(s_xt, 1)

        def pair(buf, g):
            return buf[:, :, 2 * g * P:(2 * g + 2) * P]

        def bank_pair(g):
            return ps[:, g, :].rearrange("p (k t) -> p k t", k=KD)

        l0 = top.enter_context(ExitStack())
        sbl = sb_in(l0)
        kT_h = sbl("kT_h", [P, TOK], F32R)
        kT_l = sbl("kT_l", [P, TOK], F32R)
        v_h = sbl("v_h", [P, NT, HD], F32R)
        v_l = sbl("v_l", [P, NT, HD], F32R)
        rw = sbl("rw", [P, NT, PICKS])
        slot = sbl("slot", [P, NT, PICKS], U32)
        block_expert = sbl("block_expert", [P, BLOCKS], I32)
        index = sbl("index", [P, NT, S])
        le = ExitStack()
        ew = sb_in(le)("ew", [P, NE, WE])
        assert NE == HI // 2
        ew_in = sem("ew_in")
        li = ExitStack()
        sbi = sb_in(li)
        kiT_h = sbi("kiT_h", [P, TOK], F32R)
        kiT_l = sbi("kiT_l", [P, TOK], F32R)
        small = sbi("small", [P, NT, HI + NE])
        NV = HD + HI + NE
        with ExitStack() as c:
            s = sb_in(c)
            w_k = s("w_k", [P, 2, KD, P])
            w_k_h = s("w_k_h", [P, 2, KD, P], F32R)
            w_k_l = s("w_k_l", [P, 2, KD, P], F32R)
            w_v = s("w_v", [P, KD, NV])
            w_v_h = s("w_v_h", [P, KD, NV], F32R)
            w_v_l = s("w_v_l", [P, KD, NV], F32R)
            lmax = s("lmax", [P, NT])
            prob = s("prob", [P, NT, NE])
            psum_r = s("psum_r", [P, NT])
            prec = s("prec", [P, NT])
            top8 = s("top8", [P, NT, 8])
            top8i = s("top8i", [P, NT, 8], U32)
            topi = s("topi", [P, NT, 2])
            rws = s("rws", [P, NT])
            rwr = s("rwr", [P, NT])
            iota = s("iota", [P, NT, NE])
            pick = s("pick", [P, PICKS, NT, NE])
            sel = s("sel", [P, NT, NE])
            before = s("before", [P, P])
            ones = s("ones", [P, P])
            total = s("total", [P, NE, NT])
            chain = s("chain", [P, NE, NT])
            upto = s("upto", [P, NE, NT])
            place = s("place", [P, NT, NE])
            limit = s("limit", [P, NE, NT])
            more = s("more", [P, NE, NT])
            nblk = s("nblk", [P, NE])
            eone = s("eone", [P, NE])
            bend = s("bend", [P, NE])
            bstart = s("bstart", [P, NE])
            slotf = s("slotf", [P, NT, PICKS])
            bnum = s("bnum", [P, BLOCKS, NE])
            bexp = s("bexp", [P, BLOCKS])
            zero = s("zero_row", [P, D])

            x_in = [sem("x_in0"), sem("x_in1")]
            wk_in = sem("wk_in")
            wv_in = sem("wv_in")
            s_ident = sem("s_ident")
            wk_split = sem("wk_split")
            wv_split = sem("wv_split")
            s_stat = sem("s_stat")
            s_std = sem("s_std")
            s_rstd = sem("s_rstd")
            s_xn = sem("s_xn")
            s_xt = sem("s_xt")
            xt_hi = sem("xt_hi")
            xt_lo = sem("xt_lo")
            k_ps = sem("k_ps")
            k_hi = sem("k_hi")
            k_lo = sem("k_lo")
            v_ps = sem("v_ps")
            v_hi = sem("v_hi")
            v_lo = sem("v_lo")
            s_small = sem("s_small")
            s_route = sem("s_route")
            s_shift = sem("s_shift")
            s_exp = sem("s_exp")
            s_const = sem("s_const")
            s_zero = sem("s_zero")
            s_cleared = sem("s_cleared")
            s_sel = sem("s_sel")
            rank_ps = sem("rank_ps")

            NCONST = NE + 3 + NT + BLOCKS
            with nc.Block() as block:
                @block.sync
                def _(sp):
                    for b in range(NB):
                        sp.dma_start(acc[:, b * TB:(b + 1) * TB, :],
                                     x_rows[:, b * TB:(b + 1) * TB, :]).then_inc(x_in[b], 16)
                    for n, w in enumerate((wk_idx, wk)):
                        sp.dma_start(w_k[:, n, :, :],
                                     w.rearrange("(k p) n -> p k n", p=P)).then_inc(wk_in, 16)
                    at = 0
                    for w in (wv, w_iw, w_router):
                        sp.dma_start(w_v[:, :, at:at + w.shape[1]],
                                     w.rearrange("(k p) n -> p k n", p=P)).then_inc(wv_in, 16)
                        at += w.shape[1]
                    sp.wait_ge(s_zero, 1)
                    sp.dma_start(slots_dram.rearrange("(n p) d -> p n d", p=P),
                                 zero[:, :].rearrange("p (n d) -> p n d", n=1)
                                 .broadcast_to([P, BLOCKS, D])).then_inc(s_cleared, 16)
                    sp.wait_ge(s_cleared, 16)

                @block.gpsimd
                def _(pool):
                    pool.memset(ident[:, :], 0.0).then_inc(s_ident, 1)
                    pool.wait_ge(s_ident, 1)
                    pool.affine_select(out=ident[:, :], in_=ident[:, :], compare_op=ALU.not_equal,
                                       fill=1.0, base=0, pattern=[[-1, P]],
                                       channel_multiplier=1).then_inc(s_ident, 1)
                    pool.memset(zero[:, :], 0.0).then_inc(s_zero, 1)
                    pool.wait_ge(wk_in, 32)
                    split_hi(pool, w_k_h[:, :, :, :], w_k[:, :, :, :]).then_inc(wk_split, 1)
                    pool.wait_ge(wk_split, 1)
                    pool.tensor_tensor(w_k_l[:, :, :, :], w_k[:, :, :, :],
                                       w_k_h[:, :, :, :].bitcast(F32), ALU.subtract).then_inc(wk_split, 1)
                    pool.wait_ge(wv_in, 48)
                    split_hi(pool, w_v_h[:, :, :], w_v[:, :, :]).then_inc(wv_split, 1)
                    pool.wait_ge(wv_split, 1)
                    pool.tensor_tensor(w_v_l[:, :, :], w_v[:, :, :],
                                       w_v_h[:, :, :].bitcast(F32), ALU.subtract).then_inc(wv_split, 1)
                    for e in range(NE):
                        pool.memset(iota[:, :, e], float(e)).then_inc(s_const, 1)
                    pool.memset(ones[:, :], 1.0).then_inc(s_const, 1)
                    pool.memset(chain[:, :, :], 1.0).then_inc(s_const, 1)
                    pool.memset(eone[:, :], 1.0).then_inc(s_const, 1)
                    for j in range(NT):
                        pool.memset(limit[:, :, j], float(P * j)).then_inc(s_const, 1)
                    for n in range(BLOCKS):
                        pool.memset(bnum[:, n, :], float(n)).then_inc(s_const, 1)
                    pool.wait_ge(s_const, NCONST)
                    pool.memset(chain[:, :, 0:1], 0.0).then_inc(s_const, 1)
                    pool.affine_select(out=before[:, :], in_=ones[:, :], compare_op=ALU.is_gt, fill=0.0,
                                       base=0, pattern=[[1, P]], channel_multiplier=-1).then_inc(s_const, 1)
                    for j in range(NT):
                        w = (j % TB + 1) * P
                        pool.memset(index[:, j, 0:w], 0.0)
                        if w < S:
                            pool.memset(index[:, j, w:S], NEG)

                @block.tensor
                def _(pe):
                    pe.wait_ge(s_ident, 2)
                    transpose_rows(pe, s_xn, s_xt)
                    pe.wait_ge(wk_split, 2)
                    for b in range(NB):
                        pe.wait_ge(xt_lo, (b + 1) * TB // 2)
                        for n in range(2):
                            for k in range(KD):
                                last = matmul3(pe, ps[:, 4 + 2 * b + n, :], w_k_h[:, n, k, :],
                                               w_k_l[:, n, k, :], xnT_h[:, k, b * S:(b + 1) * S],
                                               xnT_l[:, k, b * S:(b + 1) * S], k == 0, k == KD - 1)
                            last.then_inc(k_ps, 1)
                    pe.wait_ge(wv_split, 2)
                    for j in range(NT):
                        o = ps[:, j // 2, (j % 2) * 256:(j % 2) * 256 + NV]
                        for k in range(KD):
                            last = matmul3(pe, o, xnT_h[:, k, j * P:(j + 1) * P],
                                           xnT_l[:, k, j * P:(j + 1) * P], w_v_h[:, k, :],
                                           w_v_l[:, k, :], k == 0, k == KD - 1)
                        last.then_inc(v_ps, 1)
                    pe.wait_ge(s_const, NCONST + 2)
                    pe.wait_ge(s_sel, 1)
                    flat = sel[:, :, :].rearrange("p j e -> p (j e)")
                    pe.matmul(ps[:, 4, 0:NT * NE], before[:, :], flat, start=True, stop=True)
                    pe.matmul(ps[:, 5, 0:NT * NE], ones[:, :], flat, start=True, stop=True).then_inc(rank_ps, 1)

                @block.scalar
                def _(act):
                    act.wait_ge(s_stat, 2 * NT + 1)
                    act.activation(std[:, :], std[:, :], ACT.Sqrt).then_inc(s_std, 1)
                    for g in range(NT // 2):
                        act.wait_ge(s_xt, g + 1)
                        act.activation(pair(xnT_h, g), bank_pair(g), ACT.Copy).then_inc(xt_hi, 1)
                    for b in range(NB):
                        for n, dst in enumerate((kiT_h, kT_h)):
                            act.wait_ge(k_ps, 2 * b + n + 1)
                            act.activation(dst[:, b * S:(b + 1) * S], ps[:, 4 + 2 * b + n, :],
                                           ACT.Copy).then_inc(k_hi, 1)
                    for g in range(NT // 2):
                        act.wait_ge(v_ps, 2 * g + 2)
                        act.activation(v_h[:, 2 * g:2 * g + 2, :],
                                       ps[:, g, :].rearrange("p (j n) -> p j n", j=2)[:, :, 0:HD],
                                       ACT.Copy).then_inc(v_hi, 1)
                    act.wait_ge(s_shift, 1)
                    act.activation(prob[:, :, :], prob[:, :, :], ACT.Exp).then_inc(s_exp, 1)

                @block.vector
                def _(dve):
                    layernorm_vector(dve, x_in, s_stat, s_std, s_rstd, s_xn)
                    for g in range(NT // 2):
                        dve.wait_ge(xt_hi, g + 1)
                        dve.tensor_tensor(pair(xnT_l, g), bank_pair(g), pair(xnT_h, g).bitcast(F32),
                                          ALU.subtract).then_inc(xt_lo, 1)
                    for b in range(NB):
                        for n, (hi, lo) in enumerate(((kiT_h, kiT_l), (kT_h, kT_l))):
                            dve.wait_ge(k_hi, 2 * b + n + 1)
                            dve.tensor_tensor(lo[:, b * S:(b + 1) * S], ps[:, 4 + 2 * b + n, :],
                                              hi[:, b * S:(b + 1) * S].bitcast(F32),
                                              ALU.subtract).then_inc(k_lo, 1)
                    for g in range(NT // 2):
                        dve.wait_ge(v_hi, g + 1)
                        bank = ps[:, g, :].rearrange("p (j n) -> p j n", j=2)
                        dve.tensor_tensor(v_l[:, 2 * g:2 * g + 2, :], bank[:, :, 0:HD],
                                          v_h[:, 2 * g:2 * g + 2, :].bitcast(F32),
                                          ALU.subtract).then_inc(v_lo, 1)
                        dve.tensor_copy(small[:, 2 * g:2 * g + 2, :],
                                        bank[:, :, HD:NV]).then_inc(s_small, 1)
                    step = [0]

                    def then(ins):
                        step[0] += 1
                        ins.then_inc(s_route, 1)
                        dve.wait_ge(s_route, step[0])

                    def wide(a):
                        return a.rearrange("p (j e) -> p j e", e=1).broadcast_to([P, NT, NE])

                    dve.wait_ge(s_small, NT // 2)
                    logits = small[:, :, HI:HI + NE]
                    then(dve.tensor_reduce(lmax[:, :], logits, AX.X, ALU.max))
                    dve.tensor_tensor(prob[:, :, :], logits, wide(lmax[:, :]),
                                      ALU.subtract).then_inc(s_shift, 1)
                    dve.wait_ge(s_exp, 1)
                    then(dve.tensor_reduce(psum_r[:, :], prob[:, :, :], AX.X, ALU.add))
                    then(dve.reciprocal(prec[:, :], psum_r[:, :]))
                    then(dve.tensor_tensor(prob[:, :, :], prob[:, :, :], wide(prec[:, :]), ALU.mult))
                    for j in range(NT):
                        last = dve.max(top8[:, j, :], prob[:, j, :])
                    then(last)
                    for j in range(NT):
                        last = dve.max_index(top8i[:, j, :], top8[:, j, :], prob[:, j, :])
                    then(last)
                    then(dve.tensor_copy(topi[:, :, :], top8i[:, :, 0:2]))
                    then(dve.tensor_tensor(rws[:, :], top8[:, :, 0], top8[:, :, 1], ALU.add))
                    then(dve.reciprocal(rwr[:, :], rws[:, :]))
                    dve.wait_ge(s_const, NCONST + 2)
                    for m in range(PICKS):
                        then(dve.tensor_tensor(rw[:, :, m], top8[:, :, m], rwr[:, :], ALU.mult))
                        then(dve.tensor_tensor(pick[:, m, :, :], iota[:, :, :], wide(topi[:, :, m]),
                                               ALU.is_equal))
                    dve.tensor_tensor(sel[:, :, :], pick[:, 0, :, :], pick[:, 1, :, :],
                                      ALU.add).then_inc(s_sel, 1)
                    dve.wait_ge(rank_ps, 1)
                    tot_ps = ps[:, 5, 0:NT * NE].rearrange("p (j e) -> p e j", e=NE)
                    rank = ps[:, 4, 0:NT * NE].rearrange("p (j e) -> p j e", e=NE)
                    then(dve.tensor_copy(total[:, :, :], tot_ps))
                    then(dve.tensor_tensor_scan(upto[:, :, :].rearrange("p e j -> p (e j)"),
                                                chain[:, :, :].rearrange("p e j -> p (e j)"),
                                                total[:, :, :].rearrange("p e j -> p (e j)"),
                                                0.0, ALU.mult, ALU.add))
                    then(dve.tensor_tensor(more[:, :, :], upto[:, :, NT - 1:NT].broadcast_to([P, NE, NT]),
                                           limit[:, :, :], ALU.is_gt))
                    then(dve.tensor_reduce(nblk[:, :], more[:, :, :], AX.X, ALU.add))
                    then(dve.tensor_tensor_scan(bend[:, :], eone[:, :], nblk[:, :], 0.0, ALU.mult, ALU.add))
                    then(dve.tensor_tensor(bstart[:, :], bend[:, :], nblk[:, :], ALU.subtract))
                    then(dve.tensor_scalar(bstart[:, :], bstart[:, :], float(P), None, ALU.mult))
                    then(dve.tensor_tensor(upto[:, :, :], upto[:, :, :], total[:, :, :], ALU.subtract))
                    then(dve.tensor_tensor(place[:, :, :], rank, upto[:, :, :].rearrange("p e j -> p j e"),
                                           ALU.add))
                    then(dve.tensor_tensor(place[:, :, :], place[:, :, :],
                                           bstart[:, :].rearrange("p (j e) -> p j e", j=1)
                                           .broadcast_to([P, NT, NE]), ALU.add))
                    for m in range(PICKS):
                        then(dve.tensor_tensor(pick[:, m, :, :], pick[:, m, :, :], place[:, :, :], ALU.mult))
                        then(dve.tensor_reduce(slotf[:, :, m], pick[:, m, :, :], AX.X, ALU.add))
                    then(dve.tensor_copy(slot[:, :, :], slotf[:, :, :]))
                    then(dve.tensor_tensor(bnum[:, :, :], bnum[:, :, :],
                                           bend[:, :].rearrange("p (n e) -> p n e", n=1)
                                           .broadcast_to([P, BLOCKS, NE]), ALU.is_ge))
                    then(dve.tensor_reduce(bexp[:, :], bnum[:, :, :], AX.X, ALU.add))
                    then(dve.tensor_scalar(bexp[:, :], bexp[:, :], float(NE - 1), None, ALU.min))
                    then(dve.tensor_copy(block_expert[:, :], bexp[:, :]))

        with ExitStack() as c:
            s = sb_in(c)
            w_raw = s("iw_raw", [P, 2, KD, P])
            w_h = s("iw_h", [P, 2, KD, P], F32R)
            w_l = s("iw_l", [P, 2, KD, P], F32R)
            qT_h = s("iqT_h", [P, 2, TOK], F32R)
            qT_l = s("iqT_l", [P, 2, TOK], F32R)
            NR = 4
            relu = s("irelu", [P, NR, S])
            raw_in = [sem("i_raw0"), sem("i_raw1")]
            raw_free = sem("i_raw_free")
            w_hi = sem("i_w_hi")
            w_ready = sem("i_w_ready")
            q_ps = sem("i_q_ps")
            q_hi = sem("i_q_hi")
            q_lo = sem("i_q_lo")
            lg_ps = sem("i_lg_ps")
            relu_ready = sem("i_relu")
            relu_free = sem("i_relu_free")
            s_scatter = sem("i_scatter")
            s_causal = sem("i_causal")
            wqi = wq_idx.rearrange("(k p) (h n) -> p k h n", p=P, n=DI)

            def width(j):
                return (j % TB + 1) * P

            with nc.Block() as block:
                @block.sync
                def _(sp):
                    def load(i):
                        for u in range(2):
                            sp.wait_ge(raw_free, 2 * i + u + 1)
                            sp.dma_start(w_raw[:, u, :, :], wqi[:, :, bass.ds(2 * i + u, 1), :]
                                         .rearrange("p k h n -> p k (h n)")).then_inc(raw_in[u], 16)

                    def load_expert(i):
                        sp.dma_start(ew[:, bass.ds(i, 1), :].rearrange("p e m -> p (e m)"),
                                     e_weights[bass.ds(i, 1), :, :].rearrange("e p m -> p (e m)"))\
                            .then_inc(ew_in, 16)

                    load(0)
                    with sp.Fori(1, HI // 2) as i:
                        load(i)
                        load_expert(i - 1)
                    load_expert(HI // 2 - 1)
                    sp.wait_ge(ew_in, 16 * NE)

                @block.gpsimd
                def _(pool):
                    pool.sem_inc(raw_free, 2)

                    def split(i):
                        for u in range(2):
                            pool.wait_ge(raw_in[u], 16 * (i + 1))
                            pool.wait_ge(q_ps, NB * (2 * i + u + 1))
                            pool.sem_inc(stand, 1)
                            split_hi(pool, w_h[:, u, :, :], w_raw[:, u, :, :]).then_inc(w_hi, 1)
                            pool.wait_ge(w_hi, 2 * i + u + 1)
                            pool.tensor_tensor(w_l[:, u, :, :], w_raw[:, u, :, :],
                                               w_h[:, u, :, :].bitcast(F32), ALU.subtract)\
                                .then_inc(w_ready, 1)
                            pool.wait_ge(w_ready, 2 * i + u + 1)
                            pool.sem_inc(raw_free, 1)

                    split(0)
                    for j in range(NT):
                        for m in range(PICKS):
                            pool.indirect_dma_start(
                                slots_dram, bass.IndirectOffsetOnAxis(slot[:, j, m:m + 1], 0),
                                xn[:, j, :], None).then_inc(s_scatter, 16)
                    with pool.Fori(1, HI // 2) as i:
                        split(i)
                    pool.wait_ge(relu_free, NT * HI + NR)
                    for j in range(NT):
                        diag = index[:, j, (j % TB) * P:(j % TB + 1) * P]
                        pool.affine_select(out=diag, in_=diag, compare_op=ALU.is_ge, fill=NEG, base=0,
                                           pattern=[[-1, P]], channel_multiplier=1).then_inc(s_causal, 1)
                    pool.wait_ge(s_scatter, 16 * NT * PICKS)
                    pool.wait_ge(s_causal, NT)

                @block.tensor
                def _(pe):
                    pe.sem_inc(q_ps, 2 * NB)

                    def queries(h, u):
                        pe.wait_ge(w_ready, h + 1)
                        pe.wait_ge(q_lo, NB * h + NB)
                        for b in range(NB):
                            for k in range(KD):
                                last = matmul3(pe, ps[:, b, :], w_h[:, u, k, :], w_l[:, u, k, :],
                                               xnT_h[:, k, b * S:(b + 1) * S],
                                               xnT_l[:, k, b * S:(b + 1) * S], k == 0, k == KD - 1)
                            last.then_inc(q_ps, 1)

                    def scores(h, u):
                        for j in range(NT):
                            b = j // TB
                            if j % TB == 0:
                                pe.wait_ge(q_lo, NB * h + NB + b + 1)
                            pe.wait_ge(relu_ready, NT * h + (j + 1))
                            matmul3(pe, ps[:, 2 + j % NR, 0:width(j)],
                                    qT_h[:, u, j * P:(j + 1) * P], qT_l[:, u, j * P:(j + 1) * P],
                                    kiT_h[:, b * S:b * S + width(j)],
                                    kiT_l[:, b * S:b * S + width(j)], True, True).then_inc(lg_ps, 1)

                    pipeline(pe, HI, 2, queries, scores)

                @block.scalar
                def _(act):
                    act.sem_inc(relu_ready, NR)

                    def queries(h, u):
                        for b in range(NB):
                            act.wait_ge(q_ps, NB * h + (b + 1 + 2 * NB))
                            act.activation(qT_h[:, u, b * S:(b + 1) * S], ps[:, b, :],
                                           ACT.Copy).then_inc(q_hi, 1)

                    def scores(h, u):
                        for j in range(NT):
                            act.wait_ge(lg_ps, NT * h + j + 1)
                            act.wait_ge(relu_free, NT * h + j + 1)
                            act.activation(relu[:, j % NR, 0:width(j)], ps[:, 2 + j % NR, 0:width(j)],
                                           ACT.Relu).then_inc(relu_ready, 1)

                    pipeline(act, HI, 2, queries, scores)

                @block.vector
                def _(dve):
                    dve.sem_inc(relu_free, NR)
                    dve.sem_inc(q_lo, NB)

                    def queries(h, u):
                        for b in range(NB):
                            dve.wait_ge(q_hi, NB * h + b + 1)
                            dve.tensor_tensor(qT_l[:, u, b * S:(b + 1) * S], ps[:, b, :],
                                              qT_h[:, u, b * S:(b + 1) * S].bitcast(F32),
                                              ALU.subtract).then_inc(q_lo, 1)

                    def scores(h, u):
                        for j in range(NT):
                            dve.wait_ge(relu_ready, NT * h + (j + 1 + NR))
                            dve.scalar_tensor_tensor(
                                index[:, j, 0:width(j)], relu[:, j % NR, 0:width(j)],
                                small[:, j, bass.ds(h, 1)], index[:, j, 0:width(j)],
                                ALU.mult, ALU.add).then_inc(relu_free, 1)

                    pipeline(dve, HI, 2, queries, scores)

        li.close()

        with ExitStack() as c:
            s = sb_in(c)
            xg = s("xg", [P, 2, D])
            xT = s("xT", [P, 2, KD, P])
            gate = s("e_gate", [P, 2, HE])
            hid = s("e_hid", [P, 2, HE])
            hT = s("e_hT", [P, 2, HC, P])
            y = s("e_y", [P, 2, D])
            left = s("left", [P, 2, S])
            m8 = s("m8", [P, 2, 8])
            xg_in = [sem("e_xg0"), sem("e_xg1")]
            xt_ps = sem("e_xt_ps")
            xt_cp = sem("e_xt_cp")
            gu_ps = sem("e_gu_ps")
            s_silu = sem("e_silu")
            s_hid = sem("e_hid_r")
            ht_ps = sem("e_ht_ps")
            ht_cp = sem("e_ht_cp")
            y_ps = sem("e_y_ps")
            y_cp = sem("e_y_cp")
            y_out = [sem("e_y_out0"), sem("e_y_out1")]
            s_round = sem("t_round")
            s_bias = sem("t_bias")
            s_fix = sem("t_fix")
            ROUNDS = TOPK // 8
            G0, U0, DN0 = 0, KD * HE, 2 * KD * HE
            UN = 6
            TI = NT * UN // BLOCKS
            assert BLOCKS % UN == 0 and UN % 2 == 0 and TI * (BLOCKS // UN) == NT
            ewf = ew[:, :, :].rearrange("p e m -> p (e m)")
            slots_v = slots_dram.rearrange("(n p) d -> p n d", p=P)
            y_v = y_dram.rearrange("(n p) d -> p n d", p=P)

            def blocks(eng, enter, expand, leave, middle):
                def step(n, u, first=False, last=False):
                    if not last:
                        enter(n + 1, 1 - u)
                    expand(n, u)
                    if not first:
                        leave(n - 1, 1 - u)
                    middle(n, u)

                enter(0, 0)
                step(0, 0, first=True)
                for r in range(1, UN):
                    step(r, r % 2)
                with eng.Fori(1, BLOCKS // UN - 1) as i:
                    for r in range(UN):
                        step(i * UN + r, r % 2)
                for r in range(UN):
                    step(BLOCKS - UN + r, r % 2, last=r == UN - 1)
                leave(BLOCKS - 1, 1)

            def nothing(n, u):
                pass

            with nc.Block() as block:
                @block.sync
                def _(sp):
                    with sp.Fori(0, BLOCKS // 2) as i:
                        for u in range(2):
                            sp.wait_ge(xt_ps, 2 * i + (u + 1))
                            sp.dma_start(xg[:, u, :], slots_v[:, bass.ds(2 * i + u, 1), :]
                                         .rearrange("p n d -> p (n d)")).then_inc(xg_in[u], 16)

                @block.gpsimd
                def _(pool):
                    with pool.Fori(0, BLOCKS // 2) as i:
                        for u in range(2):
                            pool.wait_ge(y_cp, 2 * i + (u + 3))
                            pool.dma_start(y_v[:, bass.ds(2 * i + u, 1), :]
                                           .rearrange("p n d -> p (n d)"), y[:, u, :]).then_inc(y_out[u], 16)
                    for j in range(0, NT, TB):
                        pool.wait_ge(s_bias, j + 1)
                        diag = index[:, j, 0:P]
                        pool.affine_select(out=diag, in_=diag, compare_op=ALU.is_ge, fill=NEG, base=0,
                                           pattern=[[-1, P]], channel_multiplier=1).then_inc(s_fix, 1)
                    pool.wait_ge(s_fix, NB)
                    for u in range(2):
                        pool.wait_ge(y_out[u], 16 * (BLOCKS // 2))

                @block.tensor
                def _(pe):
                    pe.sem_inc(xt_ps, 2)
                    pe.sem_inc(gu_ps, 2)
                    pe.sem_inc(y_ps, 2)

                    def enter(n, u):
                        pe.wait_ge(xg_in[u], 16 * ((n - u) // 2 + 1))
                        pe.wait_ge(xt_cp, n + 1)
                        for k in range(KD):
                            last = pe.transpose(ps[:, 4, k * P:(k + 1) * P], xg[:, u, k * P:(k + 1) * P],
                                                ident[:, :])
                        last.then_inc(xt_ps, 1)

                    def expand(n, u):
                        e = pe.value_load(block_expert[0:1, bass.ds(n, 1)], min_val=0, max_val=NE - 1)
                        pe.wait_ge(xt_cp, n + 2)
                        pe.wait_ge(s_hid, n + 1)
                        for bank, at in ((2 * u, G0), (2 * u + 1, U0)):
                            for k in range(KD):
                                last = pe.matmul(ps[:, bank, :], xT[:, u, k, :],
                                                 ewf[:, bass.ds(e * WE + (at + k * HE), HE)],
                                                 start=k == 0, stop=k == KD - 1)
                        last.then_inc(gu_ps, 1)

                    def leave(n, u):
                        e = pe.value_load(block_expert[0:1, bass.ds(n, 1)], min_val=0, max_val=NE - 1)
                        pe.wait_ge(ht_cp, n + 2)
                        pe.wait_ge(y_cp, n + 1)
                        for c in range(HC):
                            last = pe.matmul(ps[:, 6 + u, 0:D], hT[:, u, c, :],
                                             ewf[:, bass.ds(e * WE + (DN0 + c * D), D)],
                                             start=c == 0, stop=c == HC - 1)
                        last.then_inc(y_ps, 1)

                    def middle(n, u):
                        pe.wait_ge(s_hid, n + 3)
                        pe.wait_ge(ht_cp, n + 1)
                        for c in range(HC):
                            last = pe.transpose(ps[:, 5, c * P:(c + 1) * P], hid[:, u, c * P:(c + 1) * P],
                                                ident[:, :])
                        last.then_inc(ht_ps, 1)

                    blocks(pe, enter, expand, leave, middle)

                @block.scalar
                def _(act):
                    act.sem_inc(xt_cp, 1)
                    act.sem_inc(ht_cp, 1)

                    def enter(n, u):
                        act.wait_ge(xt_ps, n + 3)
                        act.wait_ge(gu_ps, n + 1)
                        act.activation(xT[:, u, :, :], ps[:, 4, 0:D].rearrange("p (k t) -> p k t", k=KD),
                                       ACT.Copy).then_inc(xt_cp, 1)

                    def expand(n, u):
                        act.wait_ge(gu_ps, n + 3)
                        act.activation(gate[:, u, :], ps[:, 2 * u, :], ACT.Silu).then_inc(s_silu, 1)

                    def middle(n, u):
                        act.wait_ge(ht_ps, n + 1)
                        act.wait_ge(y_ps, n + 1)
                        act.activation(hT[:, u, :, :], ps[:, 5, :].rearrange("p (c t) -> p c t", c=HC),
                                       ACT.Copy).then_inc(ht_cp, 1)

                    blocks(act, enter, expand, nothing, middle)

                @block.vector
                def _(dve):
                    dve.sem_inc(s_hid, 2)
                    dve.sem_inc(y_cp, 2)

                    def expand(n, u):
                        dve.wait_ge(s_silu, n + 1)
                        dve.tensor_tensor(hid[:, u, :], gate[:, u, :], ps[:, 2 * u + 1, :],
                                          ALU.mult).then_inc(s_hid, 1)

                    def leave(n, u):
                        dve.wait_ge(y_ps, n + 3)
                        if not isinstance(n, int) or n >= 2:
                            dve.wait_ge(y_out[u], 16 * ((n - u) // 2))
                        dve.tensor_copy(y[:, u, :], ps[:, 6 + u, 0:D]).then_inc(y_cp, 1)

                    def select(i, t, part):
                        tile = bass.ds(TI * i + t, 1)
                        done = 9 * (TI * i + t)
                        w = left[:, t, :]
                        if part == 0:
                            dve.tensor_copy(w, index[:, tile, :].rearrange("p a s -> p (a s)"))\
                                .then_inc(s_round, 1)
                        for r in ((0,), (1, 2), (3,))[part]:
                            dve.wait_ge(s_round, done + (2 * r + 1))
                            dve.sem_inc(stand, 1)
                            dve.max(m8[:, t, :], w).then_inc(s_round, 1)
                            dve.wait_ge(s_round, done + (2 * r + 2))
                            dve.sem_inc(stand, 1)
                            dve.match_replace(w, m8[:, t, :], w, TAKEN).then_inc(s_round, 1)
                        if part == 2:
                            dve.wait_ge(s_round, done + 9)
                            dve.tensor_scalar(index[:, tile, :].rearrange("p a s -> p (a s)"), w, TAKEN, NEG,
                                              ALU.not_equal, ALU.mult).then_inc(s_bias, 1)

                    def step(i, r, first=False):
                        n, u = (i * UN + r, r % 2)
                        expand(n, u)
                        if not first:
                            leave(n - 1, 1 - u)
                        select(i, r // 3, r % 3)

                    for r in range(UN):
                        step(0, r, first=r == 0)
                    with dve.Fori(1, BLOCKS // UN) as i:
                        for r in range(UN):
                            step(i, r)
                    leave(BLOCKS - 1, 1)
        le.close()

        fw_h = sb("fw_h", [P, 3 * KD * FI], F32R)
        fw_l = sb("fw_l", [P, 3 * KD * FI], F32R)
        with ExitStack() as c:
            s = sb_in(c)
            wq_raw = s("wq_raw", [P, 2, KD, HD])
            wo_raw = s("wo_raw", [P, 2, D])
            wq_h = s("wq_h", [P, 2, KD, HD], F32R)
            wq_l = s("wq_l", [P, 2, KD, HD], F32R)
            wo_h = s("wo_h", [P, 2, D], F32R)
            wo_l = s("wo_l", [P, 2, D], F32R)
            qT_h = s("qT_h", [P, 2, S], F32R)
            qT_l = s("qT_l", [P, 2, S], F32R)
            sc = s("sc", [P, 2, TB, S])
            nmax = s("nmax", [P, 2, TB])
            rowsum = s("rowsum", [P, 2, TB])
            rrec = s("rrec", [P, 2, TB])
            pr = sc
            pT_h = s("pT_h", [P, 2, TB, S], F32R)
            pT_l = s("pT_l", [P, 2, TB, S], F32R)
            oT_h = s("oT_h", [P, 2, S], F32R)
            oT_l = s("oT_l", [P, 2, S], F32R)
            zero = s("zero", [P, S])
            FP = 3 * KD * FI // (NB * H // 2)
            f_raw = s("f_raw", [P, FP])
            y_pick = (xn, s("y_pick", [P, NT, D]))
            f_in = sem("f_in")
            f_hi = sem("f_hi")
            f_split = sem("f_split")
            y_in = sem("a_y_in")
            y_sum = sem("a_y_sum")
            Y_STEPS = NT * PICKS + 2 * 4
            raw_in = [sem("a_raw0"), sem("a_raw1")]
            raw_free = sem("a_raw_free")
            wq_hi = sem("a_wq_hi")
            wo_hi = sem("a_wo_hi")
            wq_ready = sem("a_wq_ready")
            wo_ready = sem("a_wo_ready")
            wo_used = sem("a_wo_used")
            s_zero = sem("a_zero")
            q_ps = sem("a_q_ps")
            q_hi = sem("a_q_hi")
            q_lo = sem("a_q_lo")
            sc_ps = sem("a_sc_ps")
            sc_ready = sem("a_sc_ready")
            exp_ready = sem("a_exp")
            r_ready = sem("a_r")
            pr_ready = sem("a_pr")
            pt_ps = sem("a_pt_ps")
            pt_hi = sem("a_pt_hi")
            pt_lo = sem("a_pt_lo")
            pv_ps = sem("a_pv_ps")
            o_hi = sem("a_o_hi")
            o_lo = sem("a_o_lo")
            s_res = sem("a_res")
            wq_v = wq.rearrange("(k p) (h n) -> p k h n", p=P, n=HD)
            wo_v = wo.rearrange("(h p) n -> p h n", p=HD)
            Q, S0, PT0, PV, WO0 = 0, 1, 3, 5, 6

            def width(j):
                return (j + 1) * P

            def heads(eng, step):
                step(-1, 1, None, None, 0)
                step(0, 0, None, 0, 0)
                for b in range(NB):
                    with eng.Fori(0, H // 2 - 1) as i:
                        step(i * 2 + (b * H + 1), 1, b, b, b)
                        step(i * 2 + (b * H + 2), 0, b, b, b)
                    after = b + 1 if b + 1 < NB else None
                    step(b * H + H - 1, 1, b, b, after)
                    step(b * H + H, 0, b, after, after)

            def closes(h, before):
                return before is not None and isinstance(h, int) and h == (before + 1) * H

            with nc.Block() as block:
                @block.sync
                def _(sp):
                    with sp.Fori(0, NB) as b:
                        with sp.Fori(0, H // 2) as i:
                            for u in range(2):
                                sp.wait_ge(raw_free, b * H + 2 * i + (u + 1))
                                sp.dma_start(wq_raw[:, u, :, :], wq_v[:, :, bass.ds(2 * i + u, 1), :]
                                             .rearrange("p k h n -> p k (h n)")).then_inc(raw_in[u], 16)
                                sp.dma_start(wo_raw[:, u, :], wo_v[:, bass.ds(2 * i + u, 1), :]
                                             .rearrange("p h n -> p (h n)")).then_inc(raw_in[u], 16)
                            sp.wait_ge(f_split, b * (H // 2) + i + 1)
                            sp.dma_start(f_raw[:, :], f_weights[:, bass.ds((b * (H // 2) + i) * FP, FP)])\
                                .then_inc(f_in, 16)

                @block.gpsimd
                def _(pool):
                    pool.sem_inc(raw_free, 2)
                    pool.sem_inc(f_split, 1)
                    pool.memset(zero[:, :], 0.0).then_inc(s_zero, 1)

                    def split_q(i, u):
                        pool.wait_ge(raw_in[u], 32 * (i + 1))
                        pool.wait_ge(q_ps, 2 * i + (u + 1))
                        pool.sem_inc(stand, 1)
                        split_hi(pool, wq_h[:, u, :, :], wq_raw[:, u, :, :]).then_inc(wq_hi, 1)
                        pool.wait_ge(wq_hi, 2 * i + (u + 1))
                        pool.tensor_tensor(wq_l[:, u, :, :], wq_raw[:, u, :, :],
                                           wq_h[:, u, :, :].bitcast(F32),
                                           ALU.subtract).then_inc(wq_ready, 1)

                    def split_o(i, u):
                        pool.wait_ge(wo_used, 2 * i + (u + 1))
                        pool.sem_inc(stand, 1)
                        split_hi(pool, wo_h[:, u, :], wo_raw[:, u, :]).then_inc(wo_hi, 1)
                        pool.wait_ge(wo_hi, 2 * i + (u + 1))
                        pool.tensor_tensor(wo_l[:, u, :], wo_raw[:, u, :],
                                           wo_h[:, u, :].bitcast(F32),
                                           ALU.subtract).then_inc(wo_ready, 1)
                        pool.wait_ge(wq_ready, 2 * i + (u + 1))
                        pool.wait_ge(wo_ready, 2 * i + (u + 1))
                        pool.sem_inc(raw_free, 1)

                    def split(i, more=True):
                        split_q(i, 1)
                        split_o(i, 0)
                        if more:
                            split_q(i + 1, 0)
                        split_o(i, 1)
                        pool.wait_ge(f_in, 16 * (i + 1))
                        piece = bass.ds(i * FP, FP)
                        pool.tensor_copy(fw_h[:, piece], f_raw[:, :]).then_inc(f_hi, 1)
                        pool.wait_ge(f_hi, i + 1)
                        pool.tensor_tensor(fw_l[:, piece], f_raw[:, :], fw_h[:, piece].bitcast(F32),
                                           ALU.subtract).then_inc(f_split, 1)

                    n = [0]

                    def then(ins):
                        n[0] += 1
                        ins.then_inc(y_sum, 1)
                        pool.wait_ge(y_sum, n[0])

                    GR = NT // 4
                    split_q(0, 0)
                    for i in range(4):
                        split(i)
                        for j in range(i * GR, (i + 1) * GR):
                            for m in range(PICKS):
                                pool.indirect_dma_start(
                                    y_pick[m][:, j, :], None, y_dram,
                                    bass.IndirectOffsetOnAxis(slot[:, j, m:m + 1], 0)).then_inc(y_in, 16)
                    for i in range(4):
                        split(4 + i)
                        pool.wait_ge(y_in, 16 * NT * PICKS)
                        for j in range(i * GR, (i + 1) * GR):
                            for m in range(PICKS):
                                last = pool.tensor_scalar(y_pick[m][:, j, :], y_pick[m][:, j, :],
                                                          rw[:, j, m:m + 1], 1.0, ALU.mult, ALU.mult)
                                then(last)
                        part = slice(i * GR, (i + 1) * GR)
                        then(pool.tensor_tensor(y_pick[0][:, part, :], y_pick[0][:, part, :],
                                                y_pick[1][:, part, :], ALU.add))
                        then(pool.tensor_tensor(acc[:, part, :], acc[:, part, :], y_pick[0][:, part, :],
                                                ALU.add))
                    assert n[0] == Y_STEPS
                    with pool.Fori(8, NB * H // 2 - 1) as i:
                        split(i)
                    split(NB * H // 2 - 1, more=False)

                @block.tensor
                def _(pe):
                    pe.sem_inc(q_ps, 2)
                    pe.sem_inc(wo_used, 2)
                    pe.wait_ge(s_zero, 1)

                    def clear_output():
                        for m in range(TB // 2):
                            pe.matmul(ps[:, WO0 + m, :], ident[:, :], zero[:, :], start=True, stop=False,
                                      skip_group_check=True)

                    def project(h, u, b):
                        pe.wait_ge(wq_ready, h + 1)
                        pe.wait_ge(q_lo, h + 1)
                        for k in range(KD):
                            last = matmul3(pe, ps[:, Q, :], wq_h[:, u, k, :], wq_l[:, u, k, :],
                                           xnT_h[:, k, b * S:(b + 1) * S],
                                           xnT_l[:, k, b * S:(b + 1) * S], k == 0, k == KD - 1)
                        last.then_inc(q_ps, 1)

                    def score(h, u, b, j):
                        if j == 0:
                            pe.wait_ge(q_lo, h + 2)
                        pe.wait_ge(sc_ready, TB * h + (j + 1))
                        matmul3(pe, ps[:, S0 + j % 2, 0:width(j)], qT_h[:, u, j * P:(j + 1) * P],
                                qT_l[:, u, j * P:(j + 1) * P], kT_h[:, b * S:b * S + width(j)],
                                kT_l[:, b * S:b * S + width(j)], True, True).then_inc(sc_ps, 1)

                    def turn(h, u, j):
                        pe.wait_ge(pr_ready, TB * h + (j + 1))
                        pe.wait_ge(pt_lo, TB * h + (j + 1))
                        for n in range(j + 1):
                            last = pe.transpose(ps[:, PT0 + j % 2, n * P:(n + 1) * P],
                                                pr[:, u, j, n * P:(n + 1) * P], ident[:, :])
                        last.then_inc(pt_ps, 1)

                    def weigh(h, u, b):
                        pe.wait_ge(pt_lo, TB * h + (2 + TB))
                        pe.wait_ge(o_lo, h + 1)
                        for n in range(TB):
                            last = matmul3(pe, ps[:, PV, n * P:S], v_h[:, b * TB + n, :],
                                           v_l[:, b * TB + n, :], pT_h[:, u, n, n * P:S],
                                           pT_l[:, u, n, n * P:S], n == 0, n == TB - 1)
                        last.then_inc(pv_ps, 1)

                    def output(h, u, tiles):
                        pe.wait_ge(wo_ready, h + 1)
                        pe.wait_ge(o_lo, h + 2)
                        for j in tiles:
                            o = ps[:, WO0 + j // 2, (j % 2) * D:(j % 2 + 1) * D]
                            last = matmul3(pe, o, oT_h[:, u, j * P:(j + 1) * P],
                                           oT_l[:, u, j * P:(j + 1) * P], wo_h[:, u, :],
                                           wo_l[:, u, :], False, False, skip_group_check=True)
                        if j == TB - 1:
                            last.then_inc(wo_used, 1)

                    def step(h, u, before, now, after):
                        v = 1 - u
                        if after is not None:
                            project(h + 1, v, after)
                        if now is not None:
                            turn(h, u, 0)
                            turn(h, u, 1)
                        if before is not None:
                            weigh(h - 1, v, before)
                        if after is not None:
                            score(h + 1, v, after, 0)
                            score(h + 1, v, after, 1)
                        if now is not None:
                            turn(h, u, 2)
                        if before is not None:
                            output(h - 1, v, (0, 1))
                        if now is not None:
                            turn(h, u, 3)
                        if after is not None:
                            score(h + 1, v, after, 2)
                        if before is not None:
                            output(h - 1, v, (2, 3))
                        if after is not None:
                            score(h + 1, v, after, 3)
                        if closes(h, before) and now is not None:
                            pe.wait_ge(s_res, (before + 1) * TB)
                            clear_output()

                    clear_output()
                    heads(pe, step)

                @block.scalar
                def _(act):
                    def query(h, u):
                        act.wait_ge(q_ps, h + 3)
                        act.activation(qT_h[:, u, :], ps[:, Q, :], ACT.Copy).then_inc(q_hi, 1)

                    def turned(h, u, j):
                        act.wait_ge(pt_ps, TB * h + (j + 1))
                        act.activation(
                            pT_h[:, u, 0:j + 1, j * P:(j + 1) * P],
                            ps[:, PT0 + j % 2, 0:width(j)].rearrange("p (c t) -> p c t", t=P),
                            ACT.Copy).then_inc(pt_hi, 1)

                    def exponential(h, u, j):
                        act.wait_ge(sc_ready, TB * h + (j + 2 + 1))
                        act.activation(pr[:, u, j, 0:width(j)], sc[:, u, j, 0:width(j)],
                                       ACT.Exp, bias=nmax[:, u, j:j + 1], scale=-1.0,
                                       accum_out=rowsum[:, u, j:j + 1]).then_inc(exp_ready, 1)

                    def weighed(h, u):
                        act.wait_ge(pv_ps, h + 1)
                        act.activation(oT_h[:, u, :], ps[:, PV, :], ACT.Copy).then_inc(o_hi, 1)

                    def step(h, u, before, now, after):
                        v = 1 - u
                        if after is not None:
                            query(h + 1, v)
                        if now is not None:
                            exponential(h, u, 3)
                            turned(h, u, 0)
                            turned(h, u, 1)
                        if before is not None:
                            weighed(h - 1, v)
                        if now is not None:
                            turned(h, u, 2)
                        if after is not None:
                            exponential(h + 1, v, 0)
                            exponential(h + 1, v, 1)
                        if now is not None:
                            turned(h, u, 3)
                        if after is not None:
                            exponential(h + 1, v, 2)

                    heads(act, step)

                @block.vector
                def _(dve):
                    dve.sem_inc(q_lo, 1)
                    dve.sem_inc(o_lo, 1)
                    dve.sem_inc(sc_ready, 2)
                    dve.sem_inc(pt_lo, 2)

                    def query(h, u):
                        dve.wait_ge(q_hi, h + 1)
                        dve.tensor_tensor(qT_l[:, u, :], ps[:, Q, :], qT_h[:, u, :].bitcast(F32),
                                          ALU.subtract).then_inc(q_lo, 1)

                    def masked(h, u, b, j):
                        dve.wait_ge(sc_ps, TB * h + (j + 1))
                        dve.sem_inc(stand, 1)
                        dve.tensor_tensor_reduce(
                            sc[:, u, j, 0:width(j)], ps[:, S0 + j % 2, 0:width(j)],
                            index[:, b * TB + j, 0:width(j)], -SCALE, 3e38, ALU.add, ALU.min,
                            nmax[:, u, j:j + 1]).then_inc(sc_ready, 1)

                    def normalise(h, u, j):
                        dve.wait_ge(exp_ready, TB * h + (j + 1))
                        dve.reciprocal(rrec[:, u, j:j + 1], rowsum[:, u, j:j + 1]).then_inc(r_ready, 1)
                        dve.wait_ge(r_ready, TB * h + (j + 1))
                        dve.tensor_scalar(pr[:, u, j, 0:width(j)], pr[:, u, j, 0:width(j)],
                                          rrec[:, u, j:j + 1], None, ALU.mult).then_inc(pr_ready, 1)

                    def turned(h, u, j):
                        dve.wait_ge(pt_hi, TB * h + (j + 1))
                        dve.tensor_tensor(
                            pT_l[:, u, 0:j + 1, j * P:(j + 1) * P],
                            ps[:, PT0 + j % 2, 0:width(j)].rearrange("p (c t) -> p c t", t=P),
                            pT_h[:, u, 0:j + 1, j * P:(j + 1) * P].bitcast(F32),
                            ALU.subtract).then_inc(pt_lo, 1)

                    def weighed(h, u):
                        dve.wait_ge(o_hi, h + 1)
                        dve.tensor_tensor(oT_l[:, u, :], ps[:, PV, :], oT_h[:, u, :].bitcast(F32),
                                          ALU.subtract).then_inc(o_lo, 1)

                    def step(h, u, before, now, after):
                        v = 1 - u
                        if after is not None:
                            query(h + 1, v)
                        if now is not None:
                            normalise(h, u, 2)
                            turned(h, u, 0)
                            normalise(h, u, 3)
                            turned(h, u, 1)
                        if before is not None:
                            weighed(h - 1, v)
                        if after is not None:
                            masked(h + 1, v, after, 0)
                            masked(h + 1, v, after, 1)
                        if now is not None:
                            turned(h, u, 2)
                        if after is not None:
                            normalise(h + 1, v, 0)
                        if now is not None:
                            turned(h, u, 3)
                        if after is not None:
                            masked(h + 1, v, after, 2)
                            normalise(h + 1, v, 1)
                            masked(h + 1, v, after, 3)
                        if closes(h, before):
                            dve.wait_ge(y_sum, Y_STEPS)
                            dve.wait_ge(wo_used, (before + 1) * H + 2)
                            for j in range(TB):
                                row = acc[:, before * TB + j, :]
                                dve.tensor_tensor(row, ps[:, WO0 + j // 2, (j % 2) * D:(j % 2 + 1) * D],
                                                  row, ALU.add).then_inc(s_res, 1)

                    heads(dve, step)

        CH = KD
        assert w_x.shape[1] == R + 2 * NS
        dt = sb("dt", [P, CH, TOK])
        xdt = sb("xdt", [P, CH, TOK])
        yT = sb("yT", [P, CH, TOK])
        a_neg = sb("a_neg", [P, CH, NS])
        with ExitStack() as c:
            s = sb_in(c)
            xf = s("xf", [P, KD, TOK])
            w_xs = s("w_xs", [P, KD, R + 2 * NS])
            w_xh = s("w_xh", [P, KD, R + 2 * NS], F32R)
            w_xl = s("w_xl", [P, KD, R + 2 * NS], F32R)
            w_ds = s("w_ds", [R, D])
            w_dh = s("w_dh", [R, D], F32R)
            w_dl = s("w_dl", [R, D], F32R)
            bd = s("bd", [P, CH])
            ds_ = s("dskip", [P, CH])
            dl_h = s("dl_h", [R, TOK], F32R)
            dl_l = s("dl_l", [R, TOK], F32R)
            bc = s("bc", [R + 2 * NS, TOK])
            soft = s("soft", [P, CH, TOK])
            wx_in = sem("m_wx_in")
            wd_in = sem("m_wd_in")
            al_in = sem("m_al_in")
            wx_split = sem("m_wx_split")
            wd_split = sem("m_wd_split")
            s_stat = sem("m_stat")
            s_std = sem("m_std")
            s_rstd = sem("m_rstd")
            s_xn = sem("m_xn")
            s_xt = sem("m_xt")
            xt_hi = sem("m_xt_hi")
            xt_lo = sem("m_xt_lo")
            xp_ps = sem("m_xp_ps")
            dl_hi = sem("m_dl_hi")
            dl_lo = sem("m_dl_lo")
            s_bc = sem("m_bc")
            bc_out = sem("m_bc_out")
            dt_ps = sem("m_dt_ps")
            s_abs = sem("m_abs")
            s_soft = sem("m_soft")
            s_relu = sem("m_relu")
            s_dt = sem("m_dt")
            s_a = sem("m_a")
            s_fin = sem("m_fin")
            with nc.Block() as block:
                @block.sync
                def _(sp):
                    sp.dma_start(w_xs[:, :, :], w_x.rearrange("(k p) n -> p k n", p=P)).then_inc(wx_in, 16)
                    sp.dma_start(w_ds[:, :], w_dt).then_inc(wd_in, 16)
                    sp.dma_start(a_neg[:, :, :], a_log.rearrange("(k p) n -> p k n", p=P)).then_inc(al_in, 16)
                    sp.dma_start(bd[:, :], b_dt).then_inc(al_in, 16)
                    sp.dma_start(ds_[:, :], d_skip).then_inc(al_in, 16)
                    sp.wait_ge(s_bc, NB)
                    sp.dma_start(bc_dram.rearrange("g n t -> (g n) t"), bc[R:R + 2 * NS, :]).then_inc(bc_out, 16)
                    sp.wait_ge(bc_out, 16)

                @block.gpsimd
                def _(pool):
                    pool.wait_ge(wx_in, 16)
                    split_hi(pool, w_xh[:, :, :], w_xs[:, :, :]).then_inc(wx_split, 1)
                    pool.wait_ge(wx_split, 1)
                    pool.tensor_tensor(w_xl[:, :, :], w_xs[:, :, :], w_xh[:, :, :].bitcast(F32),
                                       ALU.subtract).then_inc(wx_split, 1)
                    pool.wait_ge(wd_in, 16)
                    split_hi(pool, w_dh[:, :], w_ds[:, :]).then_inc(wd_split, 1)
                    pool.wait_ge(wd_split, 1)
                    pool.tensor_tensor(w_dl[:, :], w_ds[:, :], w_dh[:, :].bitcast(F32),
                                       ALU.subtract).then_inc(wd_split, 1)

                @block.tensor
                def _(pe):
                    transpose_rows(pe, s_xn, s_xt)
                    pe.wait_ge(wx_split, 2)
                    for b in range(NB):
                        pe.wait_ge(xt_lo, (b + 1) * TB // 2)
                        for k in range(KD):
                            last = matmul3(pe, ps[0:R + 2 * NS, 4 + b, :], w_xh[:, k, :], w_xl[:, k, :],
                                           xnT_h[:, k, b * S:(b + 1) * S], xnT_l[:, k, b * S:(b + 1) * S],
                                           k == 0, k == KD - 1)
                        last.then_inc(xp_ps, 1)
                    pe.wait_ge(wd_split, 2)
                    for b in range(NB):
                        pe.wait_ge(dl_lo, b + 1)
                        for k in range(CH):
                            matmul3(pe, ps[:, 2 * b + k, :], w_dh[:, k * P:(k + 1) * P],
                                    w_dl[:, k * P:(k + 1) * P], dl_h[:, b * S:(b + 1) * S],
                                    dl_l[:, b * S:(b + 1) * S], True, True).then_inc(dt_ps, 1)

                @block.scalar
                def _(act):
                    act.wait_ge(s_stat, 2 * NT + 1)
                    act.activation(std[:, :], std[:, :], ACT.Sqrt).then_inc(s_std, 1)
                    for g in range(NT // 2):
                        act.wait_ge(s_xt, g + 1)
                        act.activation(pair(xnT_h, g), bank_pair(g), ACT.Copy).then_inc(xt_hi, 1)
                        act.activation(pair(xf, g), bank_pair(g), ACT.Copy).then_inc(xt_hi, 1)
                    for b in range(NB):
                        act.wait_ge(xp_ps, b + 1)
                        act.activation(dl_h[:, b * S:(b + 1) * S], ps[0:R, 4 + b, :], ACT.Copy).then_inc(dl_hi, 1)
                        act.activation(bc[R:R + 2 * NS, b * S:(b + 1) * S], ps[R:R + 2 * NS, 4 + b, :],
                                       ACT.Copy).then_inc(s_bc, 1)
                    act.wait_ge(al_in, 48)
                    for n in range(NB * CH):
                        b, k = n // CH, n % CH
                        act.wait_ge(dt_ps, n + 1)
                        act.activation(soft[:, k, b * S:(b + 1) * S], ps[:, n, :], ACT.Abs,
                                       bias=bd[:, k:k + 1]).then_inc(s_abs, 1)
                    act.wait_ge(s_abs, NB * CH)
                    act.activation(soft[:, :, :], soft[:, :, :], ACT.Exp, scale=-1.0).then_inc(s_soft, 1)
                    act.wait_ge(s_soft, 1)
                    act.activation(soft[:, :, :], soft[:, :, :], ACT.Ln, bias=1.0).then_inc(s_soft, 1)
                    act.activation(a_neg[:, :, :], a_neg[:, :, :], ACT.Exp).then_inc(s_a, 1)

                @block.vector
                def _(dve):
                    layernorm_vector(dve, None, s_stat, s_std, s_rstd, s_xn)
                    for g in range(NT // 2):
                        dve.wait_ge(xt_hi, 2 * g + 2)
                        dve.tensor_tensor(pair(xnT_l, g), pair(xf, g), pair(xnT_h, g).bitcast(F32),
                                          ALU.subtract).then_inc(xt_lo, 1)
                    for b in range(NB):
                        dve.wait_ge(dl_hi, b + 1)
                        dve.wait_ge(s_bc, b + 1)
                        dve.tensor_tensor(dl_l[:, b * S:(b + 1) * S], ps[0:R, 4 + b, :],
                                          dl_h[:, b * S:(b + 1) * S].bitcast(F32),
                                          ALU.subtract).then_inc(dl_lo, 1)
                    dve.wait_ge(al_in, 48)
                    for k in range(CH):
                        dve.tensor_scalar(yT[:, k, :], xf[:, k, :], ds_[:, k:k + 1], None,
                                          ALU.mult).then_inc(s_fin, 1)
                    for n in range(NB * CH):
                        b, k = n // CH, n % CH
                        dve.wait_ge(s_abs, n + 1)
                        dve.tensor_scalar(dt[:, k, b * S:(b + 1) * S], ps[:, n, :], bd[:, k:k + 1], 0.0,
                                          ALU.add, ALU.max).then_inc(s_relu, 1)
                    dve.wait_ge(s_a, 1)
                    dve.tensor_scalar(a_neg[:, :, :], a_neg[:, :, :], -1.0, None, ALU.mult).then_inc(s_fin, 1)
                    dve.wait_ge(s_relu, NB * CH)
                    dve.wait_ge(s_soft, 2)
                    dve.tensor_tensor(dt[:, :, :], dt[:, :, :], soft[:, :, :], ALU.add).then_inc(s_dt, 1)
                    dve.wait_ge(s_dt, 1)
                    dve.tensor_tensor(xdt[:, :, :], dt[:, :, :], xf[:, :, :], ALU.mult).then_inc(s_fin, 1)

        with ExitStack() as c:
            s = sb_in(c)
            bcast = index[:, :, :].rearrange("p (u g a) s -> p u g (a s)", u=2, g=2)
            da = s("da", [P, 2, CH, NB, S])
            dbx = s("dbx", [P, CH, TOK])
            hst = dbx
            hc = s("hc", [P, 2, CH, TOK])
            xcur_h = s("xcur_h", [P, KD, P], F32R)
            xcur_l = s("xcur_l", [P, KD, P], F32R)
            wg_h, wg_l, wu_h, wu_l = (
                w[:, at * KD * FI:(at + 1) * KD * FI].rearrange("p (k n) -> p k n", k=KD)
                for at in range(2) for w in (fw_h, fw_l))
            wd_h, wd_l = (w[:, 2 * KD * FI:].rearrange("p (c n) -> p c n", c=FC) for w in (fw_h, fw_l))
            sil = s("sil", [P, 2, 512])
            hid = s("f_hid", [P, FI])
            mag = xn[:, NT // 2:, :].rearrange("p j d -> p (j d)")
            hT = xn[:, 0:NT // 2, :].rearrange("p j (c t) -> p (j c) t", t=P)
            cmp = s("f_cmp", [P, 6, FI // 4], BF16)
            win = s("f_win", [P, 8, FI // 4], BF16)
            hT_h = s("f_hT_h", [P, FC, P], F32R)
            hT_l = s("f_hT_l", [P, FC, P], F32R)
            bc_in = [sem("z_bc0"), sem("z_bc1")]
            da_zero = sem("z_da_zero")
            x_cur = sem("z_x_cur")
            acc_add = sem("z_acc_add")
            da_ready = sem("z_da")
            s_dbx = sem("z_dbx")
            s_scan = sem("z_scan")
            hc_ready = sem("z_hc")
            y_add = sem("z_y_add")
            gu_ps = sem("z_gu_ps")
            s_silu = sem("z_silu")
            s_prod = sem("z_prod")
            s_abs = sem("z_abs")
            s_cmp = sem("z_cmp")
            s_sparse = sem("z_sparse")
            ht_ps = sem("z_ht_ps")
            ht_cp = sem("z_ht_cp")
            ht_hi = sem("z_ht_hi")
            ht_lo = sem("z_ht_lo")
            dn_ps = sem("z_dn_ps")
            yt_ps = sem("z_yt_ps")
            s_out = sem("z_out")
            out_done = sem("z_out_done")
            bc_v = bc_dram.rearrange("g n t -> n g t")
            with nc.Block() as block:
                @block.sync
                def _(sp):
                    with sp.Fori(0, NS // 2) as i:
                        for u in range(2):
                            sp.wait_ge(hc_ready, 2 * i + (u + 1))
                            sp.dma_start(bcast[:, u, :, :], bc_v[bass.ds(2 * i + u, 1), :, :]
                                         .broadcast_to([P, 2, TOK])).then_inc(bc_in[u], 16)
                    for b in range(NB):
                        sp.wait_ge(s_out, TB // 2 * (b + 1))
                        sp.dma_start(out_rows[:, b * TB:(b + 1) * TB, :],
                                     acc[:, b * TB:(b + 1) * TB, :]).then_inc(out_done, 16)
                    sp.wait_ge(out_done, 16 * NB)

                @block.gpsimd
                def _(pool):
                    pool.sem_inc(y_add, 2)
                    pool.sem_inc(ht_lo, 1)
                    for u in range(2):
                        for k in range(CH):
                            pool.memset(da[:, u, k, :, 0:1], 0.0).then_inc(da_zero, 1)
                    with pool.Fori(0, NT) as i:
                        pool.wait_ge(ht_cp, 2 * i + 4)
                        pool.wait_ge(dn_ps, i + 1)
                        pool.sem_inc(stand, 1)
                        split_hi(pool, hT_h[:, :, :], hT[:, :, :]).then_inc(ht_hi, 1)
                        pool.wait_ge(ht_hi, i + 1)
                        pool.tensor_tensor(hT_l[:, :, :], hT[:, :, :], hT_h[:, :, :].bitcast(F32),
                                           ALU.subtract).then_inc(ht_lo, 1)
                        for u in range(2):
                            pool.wait_ge(hc_ready, 2 * i + (u + 3))
                            pool.wait_ge(y_add, 2 * i + (u + 2))
                            pool.tensor_tensor(yT[:, :, :], yT[:, :, :], hc[:, u, :, :],
                                               ALU.add).then_inc(y_add, 1)

                @block.tensor
                def _(pe):
                    pe.sem_inc(dn_ps, 1)

                    def hidden(i, r):
                        pe.wait_ge(x_cur, 2 * i + 2)
                        for m in range(2):
                            pe.wait_ge(s_prod, 2 * i + (m + 1))
                            for bank, wh, wl in ((2 * m, wg_h, wg_l), (2 * m + 1, wu_h, wu_l)):
                                for k in range(KD):
                                    last = matmul3(pe, ps[:, bank, :], xcur_h[:, k, :], xcur_l[:, k, :],
                                                   wh[:, k, m * 512:(m + 1) * 512],
                                                   wl[:, k, m * 512:(m + 1) * 512], k == 0, k == KD - 1)
                            last.then_inc(gu_ps, 1)

                    def down(i, r):
                        pe.wait_ge(s_sparse, 4 * i + 4)
                        pe.wait_ge(ht_cp, 2 * i + 2)
                        for m in range(2):
                            for n in range(4):
                                q = 4 * m + n
                                last = pe.transpose(ps[:, 4 + m, n * P:(n + 1) * P],
                                                    hid[:, q * P:(q + 1) * P], ident[:, :])
                            last.then_inc(ht_ps, 1)
                        pe.wait_ge(ht_lo, i + 2)
                        pe.wait_ge(acc_add, i + 1)
                        for n in range(FC):
                            last = matmul3(pe, ps[:, 6, 0:D], hT_h[:, n, :], hT_l[:, n, :], wd_h[:, n, :],
                                           wd_l[:, n, :], n == 0, n == FC - 1)
                        last.then_inc(dn_ps, 1)

                    pipeline(pe, NT, 1, hidden, down)
                    pe.wait_ge(y_add, NS + 2)
                    for g in range(NT // 2):
                        for m in range(2):
                            for k in range(CH):
                                last = pe.transpose(ps[:, g, (2 * m + k) * P:(2 * m + k + 1) * P],
                                                    yT[:, k, (2 * g + m) * P:(2 * g + m + 1) * P], ident[:, :])
                        last.then_inc(yt_ps, 1)

                @block.scalar
                def _(act):
                    act.sem_inc(ht_cp, 2)

                    def decay(i, u):
                        act.wait_ge(s_scan, 2 * i + (u + 1))
                        for k in range(CH):
                            act.activation(da[:, u, k, :, 1:S],
                                           dt[:, k, :].rearrange("p (b t) -> p b t", b=NB)[:, :, 1:S],
                                           ACT.Exp, scale=a_neg[:, k, bass.ds(2 * i + u, 1)])\
                                .then_inc(da_ready, 1)

                    def silu(i):
                        act.wait_ge(gu_ps, 2 * i + 1)
                        for m in range(2):
                            act.wait_ge(gu_ps, 2 * i + (m + 1))
                            act.activation(sil[:, m, :], ps[:, 2 * m, :], ACT.Silu).then_inc(s_silu, 1)

                    def fetch(i):
                        for src, dst in ((xnT_h, xcur_h), (xnT_l, xcur_l)):
                            act.activation(dst[:, :, :], src[:, :, bass.ds(i * P, P)], ACT.Copy)\
                                .then_inc(x_cur, 1)

                    def magnitude(i):
                        act.wait_ge(s_prod, 2 * i + 4)
                        act.activation(mag, hid[:, :], ACT.Abs).then_inc(s_abs, 1)

                    def turned(i):
                        act.wait_ge(ht_lo, i + 1)
                        for m in range(2):
                            act.wait_ge(ht_ps, 2 * i + (m + 1))
                            act.activation(hT[:, 4 * m:4 * m + 4, :],
                                           ps[:, 4 + m, :].rearrange("p (c t) -> p c t", t=P),
                                           ACT.Copy).then_inc(ht_cp, 1)

                    act.wait_ge(da_zero, 4)
                    fetch(0)
                    silu(0)
                    magnitude(0)
                    decay(0, 0)
                    decay(0, 1)
                    with act.Fori(0, NT - 1) as i:
                        act.wait_ge(gu_ps, 2 * i + 2)
                        fetch(i + 1)
                        turned(i)
                        silu(i + 1)
                        decay(i + 1, 0)
                        magnitude(i + 1)
                        decay(i + 1, 1)
                    turned(NT - 1)

                @block.vector
                def _(dve):
                    dve.sem_inc(s_scan, 2)
                    dve.sem_inc(hc_ready, 2)
                    dve.sem_inc(s_prod, 2)
                    dve.sem_inc(acc_add, 1)

                    def state(i, u):
                        dve.wait_ge(bc_in[u], 16 * (i + 1))
                        dve.wait_ge(hc_ready, 2 * i + (u + 2))
                        b_all = bcast[:, u, 0:1, :].broadcast_to([P, CH, TOK])
                        c_all = bcast[:, u, 1:2, :].broadcast_to([P, CH, TOK])
                        dve.tensor_tensor(dbx[:, :, :], xdt[:, :, :], b_all, ALU.mult).then_inc(s_dbx, 1)
                        dve.wait_ge(s_dbx, 2 * i + (u + 1))
                        dve.wait_ge(da_ready, 4 * i + (2 * u + 2))
                        dve.tensor_tensor_scan(hst[:, :, :].rearrange("p k t -> p (k t)"),
                                               da[:, u, :, :, :].rearrange("p k b t -> p (k b t)"),
                                               dbx[:, :, :].rearrange("p k t -> p (k t)"), 0.0,
                                               ALU.mult, ALU.add).then_inc(s_scan, 1)
                        dve.wait_ge(s_scan, 2 * i + (u + 3))
                        dve.wait_ge(y_add, 2 * i + (u + 1))
                        dve.tensor_tensor(hc[:, u, :, :], hst[:, :, :], c_all, ALU.mult).then_inc(hc_ready, 1)

                    def product(i):
                        dve.wait_ge(ht_ps, 2 * i)
                        product_first(i)

                    def product_first(i):
                        for m in range(2):
                            dve.wait_ge(s_silu, 2 * i + (m + 1))
                            dve.tensor_tensor(hid[:, m * 512:(m + 1) * 512], sil[:, m, :], ps[:, 2 * m + 1, :],
                                              ALU.mult).then_inc(s_prod, 1)

                    def sparsify(i):
                        h4 = hid[:, :].rearrange("p (g f) -> p f g", f=4)
                        a4 = mag.rearrange("p (g f) -> p f g", f=4)
                        G = FI // 4
                        dve.wait_ge(s_abs, i + 1)
                        for at, first, n in ((0, 0, 3), (3, 1, 2), (5, 2, 1)):
                            dve.tensor_tensor(cmp[:, at:at + n, :],
                                              a4[:, first:first + 1, :].broadcast_to([P, n, G]),
                                              a4[:, first + 1:4, :], ALU.is_ge).then_inc(s_cmp, 1)
                        c01, c02, c03, c12, c13, c23 = (cmp[:, n, :] for n in range(6))
                        dve.wait_ge(s_cmp, 10 * i + 3)
                        dve.tensor_tensor(win[:, 0, :], c01, c02, ALU.add).then_inc(s_cmp, 1)
                        dve.tensor_tensor(win[:, 1:3, :], cmp[:, 3:5, :], cmp[:, 4:6, :], ALU.add)\
                            .then_inc(s_cmp, 1)
                        dve.tensor_tensor(win[:, 3, :], c02, c12, ALU.add).then_inc(s_cmp, 1)
                        dve.wait_ge(s_cmp, 10 * i + 6)
                        dve.tensor_tensor(win[:, 5, :], win[:, 1, :], c01, ALU.subtract).then_inc(s_cmp, 1)
                        dve.tensor_tensor(win[:, 4, :], win[:, 0, :], c03, ALU.add).then_inc(s_cmp, 1)
                        dve.tensor_tensor(win[:, 7, :], win[:, 2, :], c03, ALU.add).then_inc(s_cmp, 1)
                        dve.tensor_tensor(win[:, 6, :], c23, win[:, 3, :], ALU.subtract).then_inc(s_cmp, 1)
                        dve.wait_ge(s_cmp, 10 * i + 10)
                        for f, bound, op in ((0, 2.0, ALU.is_ge), (1, 1.0, ALU.is_ge), (3, 1.0, ALU.is_le),
                                             (2, 0.0, ALU.is_ge)):
                            dve.scalar_tensor_tensor(h4[:, f, :], win[:, 4 + f, :], bound, h4[:, f, :],
                                                     op, ALU.mult).then_inc(s_sparse, 1)

                    def residual(i):
                        dve.wait_ge(dn_ps, i + 2)
                        row = acc[:, bass.ds(i, 1), :].rearrange("p a d -> p (a d)")
                        dve.tensor_tensor(row, ps[:, 6, 0:D], row, ALU.add).then_inc(acc_add, 1)

                    product_first(0)
                    sparsify(0)
                    with dve.Fori(0, NT - 1) as i:
                        state(i, 0)
                        product(i + 1)
                        state(i, 1)
                        sparsify(i + 1)
                        residual(i)
                    state(NT - 1, 0)
                    state(NT - 1, 1)
                    residual(NT - 1)
                    dve.wait_ge(acc_add, NT + 1)
                    for g in range(NT // 2):
                        dve.wait_ge(yt_ps, g + 1)
                        rows = acc[:, 2 * g:2 * g + 2, :].rearrange("p j d -> p (j d)")
                        dve.tensor_tensor(rows, ps[:, g, :], rows, ALU.add).then_inc(s_out, 1)


_INS = ['L0_attn_x', 'L0_attn_wq_idx', 'L0_attn_wk_idx', 'L0_attn_w_iw', 'L0_attn_wq', 'L0_attn_wk',
        'L0_attn_wv', 'L0_attn_wo', 'L0_ffn_w_router', 'L0_experts',
        'L1_attn_A_log', 'L1_attn_D_skip', 'L1_attn_W_x', 'L1_attn_W_dt', 'L1_attn_b_dt', 'L1_mlp']


def kernel(**inputs):
    import numpy as _np
    import concourse.bacc as _bacc
    from concourse import mybir as _mybir
    from concourse.bass_utils import run_bass_kernel_spmd as _run

    def by_partition(w):
        w = w.reshape(*w.shape[:-2], -1, P, w.shape[-1])
        w = _np.moveaxis(w, -3, -2)
        return w.reshape(*w.shape[:-2], -1)

    given = dict(inputs)
    for name, layer in (('L0_experts', 'L0_ffn'), ('L1_mlp', 'L1_ffn')):
        given[name] = _np.concatenate([by_partition(_np.asarray(inputs[f'{layer}_{w}']))
                                       for w in ('w_gate', 'w_up', 'w_down')], axis=-1)

    nc = _bacc.Bacc("TRN2", target_bir_lowering=False, num_devices=1)
    arrays, args = {}, []
    for name in _INS:
        a = given[name]
        if a.ndim == 1:
            a = a.reshape(-1, P).T
        a = _np.ascontiguousarray(a)
        arrays[f"in_{name}"] = a
        args.append(nc.dram_tensor(f"in_{name}", a.shape, _mybir.dt.from_np(a.dtype), kind="ExternalInput").ap())
    shape = inputs['L0_attn_x'].shape
    args.append(nc.dram_tensor("out", shape, _mybir.dt.float32, kind="ExternalOutput").ap())
    two_layers(nc, *args)
    r = _run(nc, [arrays], core_ids=[0])
    return r.results[0]["out"]
```

```python
from contextlib import ExitStack

import concourse.bass as bass
from concourse import mybir

F32 = mybir.dt.float32
F32R = mybir.dt.float32r
BF16 = mybir.dt.bfloat16
U32 = mybir.dt.uint32
I32 = mybir.dt.int32
ALU = mybir.AluOpType
ACT = mybir.ActivationFunctionType
AX = mybir.AxisListType

P = 128
NEG = -1e30
TAKEN = -3e38
EPS = 1e-5


def pipeline(eng, n, unroll, front, back, after=()):
    front(0, 0)
    peeled = -(-len(after) // unroll) * unroll
    for k in range(peeled):
        front(k + 1, (k + 1) % unroll)
        back(k, k % unroll)
        if k < len(after) and after[k] is not None:
            after[k]()
    with eng.Fori(peeled // unroll, n // unroll - 1) as i:
        for r in range(unroll):
            front(i * unroll + (r + 1), (r + 1) % unroll)
            back(i * unroll + r, r)
    base = n - unroll
    for r in range(unroll):
        if r + 1 < unroll:
            front(base + r + 1, r + 1)
        back(base + r, r)


def matmul3(pe, out, w_hi, w_lo, x_hi, x_lo, start, stop, **kw):
    pe.matmul(out, w_hi, x_hi, start=start, stop=False, **kw)
    pe.matmul(out, w_hi, x_lo, start=False, stop=False, **kw)
    return pe.matmul(out, w_lo, x_hi, start=False, stop=stop, **kw)


def split_hi(pool, hi, src):
    return pool.tensor_scalar(hi, src, 1.0, 1.0, ALU.mult, ALU.mult)


def two_layers(nc, x, wq_idx, wk_idx, w_iw, wq, wk, wv, wo, w_router, e_weights,
               a_log, d_skip, w_x, w_dt, b_dt, f_weights, out):
    NB, S, D = x.shape
    KD = D // P
    TOK = NB * S
    NT = TOK // P
    TB = S // P
    DI = wk_idx.shape[1]
    HI = w_iw.shape[1]
    HD = wk.shape[1]
    H = wq.shape[1] // HD
    SCALE = float(HD) ** -0.5
    NE, _, WE = e_weights.shape
    HE = WE // (3 * KD)
    HC = HE // P
    PICKS = 2
    BLOCKS = (PICKS * TOK + NE * (P - 1)) // P
    NS = a_log.shape[1]
    R = w_dt.shape[0]
    FI = f_weights.shape[1] // (3 * KD)
    FC = FI // P
    TOPK = 32
    assert DI == P and HD == P and S == 512 and D == 256

    x_rows = x.rearrange("b (j p) d -> p (b j) d", p=P)
    out_rows = out.rearrange("b (j p) d -> p (b j) d", p=P)
    slots_dram = nc.dram_tensor("slots_scratch", [BLOCKS * P, D], F32).ap()
    y_dram = nc.dram_tensor("y_scratch", [BLOCKS * P, D], F32).ap()
    b_dram = nc.dram_tensor("b_scratch", [NS, TOK], F32).ap()
    b_rows = b_dram.rearrange("(n a) t -> n a t", a=1)

    with ExitStack() as top:
        def sem(name):
            return top.enter_context(nc.semaphore(name))

        def sb_in(ctx):
            def sb(name, shape, dt=F32):
                return ctx.enter_context(nc.sbuf_tensor(name, shape, dt))
            return sb

        sb = sb_in(top)
        ps = top.enter_context(nc.psum_tensor("ps", [P, 8, 512], F32))
        acc = sb("acc", [P, NT, D])
        ident = sb("ident", [P, P])
        stand = sem("stand")
        stats = sb("stats", [P, NT, 6])
        mv = sb("mv", [P, NT, 2])
        std = sb("std", [P, NT])
        rstd = sb("rstd", [P, NT])
        xn = sb("xn", [P, NT, D])
        xnT_h = sb("xnT_h", [P, KD, TOK], F32R)
        xnT_l = sb("xnT_l", [P, KD, TOK], F32R)

        class Norm:
            def __init__(self, name):
                self.stat, self.std, self.rstd, self.xn = (
                    sem(f"{name}_{what}") for what in ("stat", "std", "rstd", "xn"))

        def norm_stats(dve, b, s):
            tiles = range(b * TB, (b + 1) * TB)
            done = b * (2 * TB + 1)
            for j in tiles:
                dve.bn_stats(stats[:, j, :], acc[:, j, :]).then_inc(s.stat, 1)
            for n, j in enumerate(tiles):
                dve.wait_ge(s.stat, done + n + 1)
                dve.bn_aggr(mv[:, j, :], stats[:, j, :]).then_inc(s.stat, 1)
            dve.wait_ge(s.stat, done + 2 * TB)
            dve.tensor_scalar(std[:, b * TB:(b + 1) * TB], mv[:, b * TB:(b + 1) * TB, 1], EPS, None,
                              ALU.add).then_inc(s.stat, 1)

        def norm_root(act, b, s):
            act.wait_ge(s.stat, (b + 1) * (2 * TB + 1))
            part = std[:, b * TB:(b + 1) * TB]
            act.activation(part, part, ACT.Sqrt).then_inc(s.std, 1)

        def norm_scale(dve, b, s):
            dve.wait_ge(s.std, b + 1)
            part = slice(b * TB, (b + 1) * TB)
            dve.reciprocal(rstd[:, part], std[:, part]).then_inc(s.rstd, 1)
            dve.wait_ge(s.rstd, b + 1)
            for j in range(b * TB, (b + 1) * TB):
                dve.tensor_scalar(xn[:, j, :], acc[:, j, :], mv[:, j, 0:1], rstd[:, j:j + 1],
                                  ALU.subtract, ALU.mult).then_inc(s.xn, 1)

        def transpose_rows(pe, s_xn, s_xt):
            for g in range(NT // 2):
                pe.wait_ge(s_xn, 2 * g + 2)
                for k in range(KD):
                    for m in range(2):
                        last = pe.transpose(ps[:, g, (2 * k + m) * P:(2 * k + m + 1) * P],
                                            xn[:, 2 * g + m, k * P:(k + 1) * P], ident[:, :])
                last.then_inc(s_xt, 1)

        def pair(buf, g):
            return buf[:, :, 2 * g * P:(2 * g + 2) * P]

        def bank_pair(g):
            return ps[:, g, :].rearrange("p (k t) -> p k t", k=KD)

        l0 = top.enter_context(ExitStack())
        sbl = sb_in(l0)
        kT_h = sbl("kT_h", [P, TOK], F32R)
        kT_l = sbl("kT_l", [P, TOK], F32R)
        v_h = sbl("v_h", [P, NT, HD], F32R)
        v_l = sbl("v_l", [P, NT, HD], F32R)
        rw = sbl("rw", [P, NT, PICKS])
        slot = sbl("slot", [P, NT, PICKS], U32)
        block_expert = sbl("block_expert", [P, BLOCKS], I32)
        index = sbl("index", [P, NT, S])
        wq_raw = sbl("wq_raw", [P, 2, KD, P])
        wq_h = sbl("wq_h", [P, 2, KD, P], F32R)
        wq_l = sbl("wq_l", [P, 2, KD, P], F32R)
        xg = sbl("xg", [P, 2, D])
        le = ExitStack()
        ew = sb_in(le)("ew", [P, NE, WE])
        assert NE == HI // 2
        ew_in = sem("ew_in")
        li = ExitStack()
        sbi = sb_in(li)
        kiT_h = sbi("kiT_h", [P, TOK], F32R)
        kiT_l = sbi("kiT_l", [P, TOK], F32R)
        small = sbi("small", [P, NT, HI + NE])
        NV = HD + HI + NE
        lmax = sbi("lmax", [P, NT])
        prob = sbi("prob", [P, NT, NE])
        psum_r = sbi("psum_r", [P, NT])
        prec = sbi("prec", [P, NT])
        top8 = sbi("top8", [P, NT, 8])
        top8i = sbi("top8i", [P, NT, 8], U32)
        topi = sbi("topi", [P, NT, 2])
        rws = sbi("rws", [P, NT])
        rwr = sbi("rwr", [P, NT])
        iota = sbi("iota", [P, NT, NE])
        pick = sbi("pick", [P, PICKS, NT, NE])
        sel = sbi("sel", [P, NT, NE])
        before = sbi("before", [P, P])
        ones = sbi("ones", [P, P])
        total = sbi("total", [P, NE, NT])
        chain = sbi("chain", [P, NE, NT])
        upto = sbi("upto", [P, NE, NT])
        place = sbi("place", [P, NT, NE])
        limit = sbi("limit", [P, NE, NT])
        more = sbi("more", [P, NE, NT])
        nblk = sbi("nblk", [P, NE])
        eone = sbi("eone", [P, NE])
        bend = sbi("bend", [P, NE])
        bstart = sbi("bstart", [P, NE])
        slotf = sbi("slotf", [P, NT, PICKS])
        bnum = sbi("bnum", [P, BLOCKS, NE])
        bexp = sbi("bexp", [P, BLOCKS])
        raw_in = [sem("i_raw0"), sem("i_raw1")]
        raw_free = sem("i_raw_free")
        w_hi = sem("i_w_hi")
        w_ready = sem("i_w_ready")
        q_ps = sem("i_q_ps")
        s_const = sem("s_const")
        NCONST = NE + 3 + NT + BLOCKS
        wqi = wq_idx.rearrange("(k p) (h n) -> p k h n", p=P, n=DI)

        def load_index_weights(sp, i, u):
            sp.dma_start(wq_raw[:, u, :, :], wqi[:, :, bass.ds(2 * i + u, 1), :]
                         .rearrange("p k h n -> p k (h n)")).then_inc(raw_in[u], 16)

        def split_index_weights(pool, i):
            for u in range(2):
                pool.wait_ge(raw_in[u], 16 * (i + 1))
                if not isinstance(i, int) or i > 0:
                    pool.wait_ge(q_ps, NB * (2 * i + u + 1))
                pool.sem_inc(stand, 1)
                split_hi(pool, wq_h[:, u, :, :], wq_raw[:, u, :, :]).then_inc(w_hi, 1)
                pool.wait_ge(w_hi, 2 * i + u + 1)
                pool.tensor_tensor(wq_l[:, u, :, :], wq_raw[:, u, :, :],
                                   wq_h[:, u, :, :].bitcast(F32), ALU.subtract)\
                    .then_inc(w_ready, 1)
                pool.wait_ge(w_ready, 2 * i + u + 1)
                pool.sem_inc(raw_free, 1)

        with ExitStack() as c:
            s = sb_in(c)
            w_k = s("w_k", [P, 2, KD, P])
            w_k_h = s("w_k_h", [P, 2, KD, P], F32R)
            w_k_l = s("w_k_l", [P, 2, KD, P], F32R)
            w_v = s("w_v", [P, KD, NV])
            w_v_h = s("w_v_h", [P, KD, NV], F32R)
            w_v_l = s("w_v_l", [P, KD, NV], F32R)
            zero = s("zero_row", [P, D])

            x_in = [sem("x_in0"), sem("x_in1")]
            wk_in = sem("wk_in")
            wv_in = sem("wv_in")
            s_ident = sem("s_ident")
            wk_split = sem("wk_split")
            wv_split = sem("wv_split")
            norm = Norm("norm")
            s_xt = sem("s_xt")
            xt_hi = sem("xt_hi")
            xt_lo = sem("xt_lo")
            k_ps = sem("k_ps")
            k_hi = sem("k_hi")
            k_lo = sem("k_lo")
            v_ps = sem("v_ps")
            v_hi = sem("v_hi")
            v_lo = sem("v_lo")
            s_small = sem("s_small")
            s_zero = sem("s_zero")
            s_cleared = sem("s_cleared")

            with nc.Block() as block:
                @block.sync
                def _(sp):
                    for b in range(NB):
                        sp.dma_start(acc[:, b * TB:(b + 1) * TB, :],
                                     x_rows[:, b * TB:(b + 1) * TB, :]).then_inc(x_in[b], 16)
                    for n, w in enumerate((wk_idx, wk)):
                        sp.dma_start(w_k[:, n, :, :],
                                     w.rearrange("(k p) n -> p k n", p=P)).then_inc(wk_in, 16)
                    at = 0
                    for w in (wv, w_iw, w_router):
                        sp.dma_start(w_v[:, :, at:at + w.shape[1]],
                                     w.rearrange("(k p) n -> p k n", p=P)).then_inc(wv_in, 16)
                        at += w.shape[1]
                    for u in range(2):
                        load_index_weights(sp, 0, u)
                    sp.wait_ge(s_zero, 1)
                    sp.dma_start(slots_dram.rearrange("(n p) d -> p n d", p=P),
                                 zero[:, :].rearrange("p (n d) -> p n d", n=1)
                                 .broadcast_to([P, BLOCKS, D])).then_inc(s_cleared, 16)
                    sp.wait_ge(s_cleared, 16)

                @block.gpsimd
                def _(pool):
                    pool.memset(ident[:, :], 0.0).then_inc(s_ident, 1)
                    pool.wait_ge(s_ident, 1)
                    pool.affine_select(out=ident[:, :], in_=ident[:, :], compare_op=ALU.not_equal,
                                       fill=1.0, base=0, pattern=[[-1, P]],
                                       channel_multiplier=1).then_inc(s_ident, 1)
                    pool.memset(zero[:, :], 0.0).then_inc(s_zero, 1)
                    pool.wait_ge(wk_in, 32)
                    split_hi(pool, w_k_h[:, :, :, :], w_k[:, :, :, :]).then_inc(wk_split, 1)
                    pool.wait_ge(wk_split, 1)
                    pool.tensor_tensor(w_k_l[:, :, :, :], w_k[:, :, :, :],
                                       w_k_h[:, :, :, :].bitcast(F32), ALU.subtract).then_inc(wk_split, 1)
                    pool.wait_ge(wv_in, 48)
                    split_hi(pool, w_v_h[:, :, :], w_v[:, :, :]).then_inc(wv_split, 1)
                    pool.wait_ge(wv_split, 1)
                    pool.tensor_tensor(w_v_l[:, :, :], w_v[:, :, :],
                                       w_v_h[:, :, :].bitcast(F32), ALU.subtract).then_inc(wv_split, 1)
                    for e in range(NE):
                        pool.memset(iota[:, :, e], float(e)).then_inc(s_const, 1)
                    pool.memset(ones[:, :], 1.0).then_inc(s_const, 1)
                    pool.memset(chain[:, :, :], 1.0).then_inc(s_const, 1)
                    pool.memset(eone[:, :], 1.0).then_inc(s_const, 1)
                    for j in range(NT):
                        pool.memset(limit[:, :, j], float(P * j)).then_inc(s_const, 1)
                    for n in range(BLOCKS):
                        pool.memset(bnum[:, n, :], float(n)).then_inc(s_const, 1)
                    pool.wait_ge(s_const, NCONST)
                    pool.memset(chain[:, :, 0:1], 0.0).then_inc(s_const, 1)
                    pool.affine_select(out=before[:, :], in_=ones[:, :], compare_op=ALU.is_gt, fill=0.0,
                                       base=0, pattern=[[1, P]], channel_multiplier=-1).then_inc(s_const, 1)
                    split_index_weights(pool, 0)
                    for j in range(NT):
                        w = (j % TB + 1) * P
                        pool.memset(index[:, j, 0:w], 0.0)
                        if w < S:
                            pool.memset(index[:, j, w:S], NEG)

                @block.tensor
                def _(pe):
                    pe.wait_ge(s_ident, 2)
                    transpose_rows(pe, norm.xn, s_xt)
                    pe.wait_ge(wk_split, 2)
                    for b in range(NB):
                        pe.wait_ge(xt_lo, (b + 1) * TB // 2)
                        for n in range(2):
                            for k in range(KD):
                                last = matmul3(pe, ps[:, 4 + 2 * b + n, :], w_k_h[:, n, k, :],
                                               w_k_l[:, n, k, :], xnT_h[:, k, b * S:(b + 1) * S],
                                               xnT_l[:, k, b * S:(b + 1) * S], k == 0, k == KD - 1)
                            last.then_inc(k_ps, 1)
                    pe.wait_ge(wv_split, 2)
                    for j in range(NT):
                        o = ps[:, j // 2, (j % 2) * 256:(j % 2) * 256 + NV]
                        for k in range(KD):
                            last = matmul3(pe, o, xnT_h[:, k, j * P:(j + 1) * P],
                                           xnT_l[:, k, j * P:(j + 1) * P], w_v_h[:, k, :],
                                           w_v_l[:, k, :], k == 0, k == KD - 1)
                        last.then_inc(v_ps, 1)

                @block.scalar
                def _(act):
                    for b in range(NB):
                        norm_root(act, b, norm)
                    for g in range(NT // 2):
                        act.wait_ge(s_xt, g + 1)
                        act.activation(pair(xnT_h, g), bank_pair(g), ACT.Copy).then_inc(xt_hi, 1)
                    for b in range(NB):
                        for n, dst in enumerate((kiT_h, kT_h)):
                            act.wait_ge(k_ps, 2 * b + n + 1)
                            act.activation(dst[:, b * S:(b + 1) * S], ps[:, 4 + 2 * b + n, :],
                                           ACT.Copy).then_inc(k_hi, 1)
                    for g in range(NT // 2):
                        act.wait_ge(v_ps, 2 * g + 2)
                        act.activation(v_h[:, 2 * g:2 * g + 2, :],
                                       ps[:, g, :].rearrange("p (j n) -> p j n", j=2)[:, :, 0:HD],
                                       ACT.Copy).then_inc(v_hi, 1)

                @block.vector
                def _(dve):
                    for b in range(NB):
                        dve.wait_ge(x_in[b], 16)
                        norm_stats(dve, b, norm)
                    for b in range(NB):
                        norm_scale(dve, b, norm)
                    for g in range(NT // 2):
                        dve.wait_ge(xt_hi, g + 1)
                        dve.tensor_tensor(pair(xnT_l, g), bank_pair(g), pair(xnT_h, g).bitcast(F32),
                                          ALU.subtract).then_inc(xt_lo, 1)
                    for b in range(NB):
                        for n, (hi, lo) in enumerate(((kiT_h, kiT_l), (kT_h, kT_l))):
                            dve.wait_ge(k_hi, 2 * b + n + 1)
                            dve.tensor_tensor(lo[:, b * S:(b + 1) * S], ps[:, 4 + 2 * b + n, :],
                                              hi[:, b * S:(b + 1) * S].bitcast(F32),
                                              ALU.subtract).then_inc(k_lo, 1)
                    for g in range(NT // 2):
                        dve.wait_ge(v_hi, g + 1)
                        bank = ps[:, g, :].rearrange("p (j n) -> p j n", j=2)
                        dve.tensor_tensor(v_l[:, 2 * g:2 * g + 2, :], bank[:, :, 0:HD],
                                          v_h[:, 2 * g:2 * g + 2, :].bitcast(F32),
                                          ALU.subtract).then_inc(v_lo, 1)
                        dve.tensor_copy(small[:, 2 * g:2 * g + 2, :],
                                        bank[:, :, HD:NV]).then_inc(s_small, 1)

        slots_v = slots_dram.rearrange("(n p) d -> p n d", p=P)
        y_v = y_dram.rearrange("(n p) d -> p n d", p=P)
        xg_in = [sem("e_xg0"), sem("e_xg1")]
        y_out = [sem("e_y_out0"), sem("e_y_out1")]
        y_last = sem("e_y_last")

        def load_rows(sp, i, u):
            sp.dma_start(xg[:, u, :], slots_v[:, bass.ds(2 * i + u, 1), :]
                         .rearrange("p n d -> p (n d)")).then_inc(xg_in[u], 16)

        q_in = [sem("a_q_in0"), sem("a_q_in1")]
        wq_hi = sem("a_wq_hi")
        wq_ready = sem("a_wq_ready")
        a_q_ps = sem("a_q_ps")
        wq_v = wq.rearrange("(k p) (h n) -> p k h n", p=P, n=HD)

        def load_q(sp, i, u):
            sp.dma_start(wq_raw[:, u, :, :], wq_v[:, :, bass.ds(2 * i + u, 1), :]
                         .rearrange("p k h n -> p k (h n)")).then_inc(q_in[u], 16)

        def split_q(pool, i, u):
            pool.wait_ge(q_in[u], 16 * (i + 1))
            if not isinstance(i, int) or i > 0:
                pool.wait_ge(a_q_ps, 2 * i + (u + 1))
            pool.sem_inc(stand, 1)
            split_hi(pool, wq_h[:, u, :, :], wq_raw[:, u, :, :]).then_inc(wq_hi, 1)
            pool.wait_ge(wq_hi, 2 * i + (u + 1))
            pool.tensor_tensor(wq_l[:, u, :, :], wq_raw[:, u, :, :],
                               wq_h[:, u, :, :].bitcast(F32), ALU.subtract).then_inc(wq_ready, 1)

        with ExitStack() as c:
            s = sb_in(c)
            qT_h = s("iqT_h", [P, 2, TOK], F32R)
            qT_l = s("iqT_l", [P, 2, TOK], F32R)
            NR = 4
            relu = s("irelu", [P, NR, S])
            q_hi = sem("i_q_hi")
            q_lo = sem("i_q_lo")
            lg_ps = sem("i_lg_ps")
            relu_ready = sem("i_relu")
            relu_free = sem("i_relu_free")
            s_scatter = sem("i_scatter")
            s_route = sem("s_route")
            s_shift = sem("s_shift")
            s_exp = sem("s_exp")
            s_sel = sem("s_sel")
            rank_ps = sem("rank_ps")
            s_slot = sem("s_slot")
            s_causal = sem("i_causal")

            def width(j):
                return (j % TB + 1) * P

            with nc.Block() as block:
                @block.sync
                def _(sp):
                    def load_expert(i):
                        sp.dma_start(ew[:, bass.ds(i, 1), :].rearrange("p e m -> p (e m)"),
                                     e_weights[bass.ds(i, 1), :, :].rearrange("e p m -> p (e m)"))\
                            .then_inc(ew_in, 16)

                    with sp.Fori(1, HI // 2) as i:
                        for u in range(2):
                            sp.wait_ge(raw_free, 2 * i + u - 1)
                            load_index_weights(sp, i, u)
                        load_expert(i - 1)
                    load_expert(HI // 2 - 1)
                    sp.wait_ge(w_ready, HI)
                    for u in range(2):
                        load_q(sp, 0, u)
                    sp.wait_ge(s_scatter, 16 * NT * PICKS)
                    for u in range(2):
                        load_rows(sp, 0, u)
                    sp.wait_ge(ew_in, 16 * NE)

                @block.gpsimd
                def _(pool):
                    PEELED = 3
                    with pool.Fori(1, HI // 2 - PEELED) as i:
                        split_index_weights(pool, i)
                    for r in range(PEELED):
                        split_index_weights(pool, HI // 2 - PEELED + r)
                        pool.wait_ge(s_slot, 1)
                        for j in range(r * NT // PEELED, (r + 1) * NT // PEELED):
                            for m in range(PICKS):
                                pool.indirect_dma_start(
                                    slots_dram, bass.IndirectOffsetOnAxis(slot[:, j, m:m + 1], 0),
                                    xn[:, j, :], None).then_inc(s_scatter, 16)
                    for j in range(NT):
                        pool.wait_ge(relu_free, NT * (HI - 1) + NR + j + 1)
                        diag = index[:, j, (j % TB) * P:(j % TB + 1) * P]
                        pool.affine_select(out=diag, in_=diag, compare_op=ALU.is_ge, fill=NEG, base=0,
                                           pattern=[[-1, P]], channel_multiplier=1).then_inc(s_causal, 1)
                    pool.wait_ge(s_causal, NT)

                @block.tensor
                def _(pe):
                    pe.sem_inc(q_ps, 2 * NB)

                    def queries(h, u):
                        pe.wait_ge(w_ready, h + 1)
                        pe.wait_ge(q_lo, NB * h + NB)
                        for b in range(NB):
                            for k in range(KD):
                                last = matmul3(pe, ps[:, b, :], wq_h[:, u, k, :], wq_l[:, u, k, :],
                                               xnT_h[:, k, b * S:(b + 1) * S],
                                               xnT_l[:, k, b * S:(b + 1) * S], k == 0, k == KD - 1)
                            last.then_inc(q_ps, 1)

                    def scores(h, u):
                        for j in range(NT):
                            b = j // TB
                            if j % TB == 0:
                                pe.wait_ge(q_lo, NB * h + NB + b + 1)
                            pe.wait_ge(relu_ready, NT * h + (j + 1))
                            matmul3(pe, ps[:, 2 + j % NR, 0:width(j)],
                                    qT_h[:, u, j * P:(j + 1) * P], qT_l[:, u, j * P:(j + 1) * P],
                                    kiT_h[:, b * S:b * S + width(j)],
                                    kiT_l[:, b * S:b * S + width(j)], True, True).then_inc(lg_ps, 1)

                    def rank():
                        pe.wait_ge(s_const, NCONST + 2)
                        pe.wait_ge(s_sel, 1)
                        flat = sel[:, :, :].rearrange("p j e -> p (j e)")
                        pe.matmul(ps[:, 6, 0:NT * NE], before[:, :], flat, start=True, stop=True)
                        pe.matmul(ps[:, 7, 0:NT * NE], ones[:, :], flat, start=True, stop=True)\
                            .then_inc(rank_ps, 1)

                    pipeline(pe, HI, 2, queries, scores, (None,) * 5 + (rank,))

                @block.scalar
                def _(act):
                    act.sem_inc(relu_ready, NR)

                    def queries(h, u):
                        for b in range(NB):
                            act.wait_ge(q_ps, NB * h + (b + 1 + 2 * NB))
                            act.activation(qT_h[:, u, b * S:(b + 1) * S], ps[:, b, :],
                                           ACT.Copy).then_inc(q_hi, 1)

                    def scores(h, u):
                        for j in range(NT):
                            act.wait_ge(lg_ps, NT * h + j + 1)
                            act.wait_ge(relu_free, NT * h + j + 1)
                            act.activation(relu[:, j % NR, 0:width(j)], ps[:, 2 + j % NR, 0:width(j)],
                                           ACT.Relu).then_inc(relu_ready, 1)

                    def router_exp():
                        act.wait_ge(s_shift, 1)
                        act.activation(prob[:, :, :], prob[:, :, :], ACT.Exp).then_inc(s_exp, 1)

                    pipeline(act, HI, 2, queries, scores, (None, router_exp))

                @block.vector
                def _(dve):
                    dve.sem_inc(relu_free, NR)
                    dve.sem_inc(q_lo, NB)

                    def queries(h, u):
                        for b in range(NB):
                            dve.wait_ge(q_hi, NB * h + b + 1)
                            dve.tensor_tensor(qT_l[:, u, b * S:(b + 1) * S], ps[:, b, :],
                                              qT_h[:, u, b * S:(b + 1) * S].bitcast(F32),
                                              ALU.subtract).then_inc(q_lo, 1)

                    def scores(h, u):
                        for j in range(NT):
                            dve.wait_ge(relu_ready, NT * h + (j + 1 + NR))
                            dve.scalar_tensor_tensor(
                                index[:, j, 0:width(j)], relu[:, j % NR, 0:width(j)],
                                small[:, j, bass.ds(h, 1)], index[:, j, 0:width(j)],
                                ALU.mult, ALU.add).then_inc(relu_free, 1)

                    step = [0]

                    def then(ins):
                        step[0] += 1
                        ins.then_inc(s_route, 1)
                        dve.wait_ge(s_route, step[0])

                    def wide(a):
                        return a.rearrange("p (j e) -> p j e", e=1).broadcast_to([P, NT, NE])

                    logits = small[:, :, HI:HI + NE]

                    def shift():
                        then(dve.tensor_reduce(lmax[:, :], logits, AX.X, ALU.max))
                        dve.tensor_tensor(prob[:, :, :], logits, wide(lmax[:, :]),
                                          ALU.subtract).then_inc(s_shift, 1)

                    def softmax():
                        dve.wait_ge(s_exp, 1)
                        then(dve.tensor_reduce(psum_r[:, :], prob[:, :, :], AX.X, ALU.add))
                        then(dve.reciprocal(prec[:, :], psum_r[:, :]))
                        then(dve.tensor_tensor(prob[:, :, :], prob[:, :, :], wide(prec[:, :]), ALU.mult))

                    def top_two():
                        for j in range(NT):
                            last = dve.max(top8[:, j, :], prob[:, j, :])
                        then(last)
                        for j in range(NT):
                            last = dve.max_index(top8i[:, j, :], top8[:, j, :], prob[:, j, :])
                        then(last)
                        then(dve.tensor_copy(topi[:, :, :], top8i[:, :, 0:2]))

                    def picks():
                        then(dve.tensor_tensor(rws[:, :], top8[:, :, 0], top8[:, :, 1], ALU.add))
                        then(dve.reciprocal(rwr[:, :], rws[:, :]))
                        dve.wait_ge(s_const, NCONST + 2)
                        for m in range(PICKS):
                            then(dve.tensor_tensor(rw[:, :, m], top8[:, :, m], rwr[:, :], ALU.mult))
                            then(dve.tensor_tensor(pick[:, m, :, :], iota[:, :, :], wide(topi[:, :, m]),
                                                   ALU.is_equal))
                        dve.tensor_tensor(sel[:, :, :], pick[:, 0, :, :], pick[:, 1, :, :],
                                          ALU.add).then_inc(s_sel, 1)

                    tot_ps = ps[:, 7, 0:NT * NE].rearrange("p (j e) -> p e j", e=NE)
                    rank = ps[:, 6, 0:NT * NE].rearrange("p (j e) -> p j e", e=NE)

                    def counts():
                        dve.wait_ge(rank_ps, 1)
                        then(dve.tensor_copy(total[:, :, :], tot_ps))
                        then(dve.tensor_tensor_scan(upto[:, :, :].rearrange("p e j -> p (e j)"),
                                                    chain[:, :, :].rearrange("p e j -> p (e j)"),
                                                    total[:, :, :].rearrange("p e j -> p (e j)"),
                                                    0.0, ALU.mult, ALU.add))
                        then(dve.tensor_tensor(more[:, :, :], upto[:, :, NT - 1:NT].broadcast_to([P, NE, NT]),
                                               limit[:, :, :], ALU.is_gt))
                        then(dve.tensor_reduce(nblk[:, :], more[:, :, :], AX.X, ALU.add))

                    def starts():
                        then(dve.tensor_tensor_scan(bend[:, :], eone[:, :], nblk[:, :], 0.0,
                                                    ALU.mult, ALU.add))
                        then(dve.tensor_tensor(bstart[:, :], bend[:, :], nblk[:, :], ALU.subtract))
                        then(dve.tensor_scalar(bstart[:, :], bstart[:, :], float(P), None, ALU.mult))
                        then(dve.tensor_tensor(upto[:, :, :], upto[:, :, :], total[:, :, :], ALU.subtract))
                        then(dve.tensor_tensor(place[:, :, :], rank, upto[:, :, :].rearrange("p e j -> p j e"),
                                               ALU.add))
                        then(dve.tensor_tensor(place[:, :, :], place[:, :, :],
                                               bstart[:, :].rearrange("p (j e) -> p j e", j=1)
                                               .broadcast_to([P, NT, NE]), ALU.add))

                    def slots():
                        for m in range(PICKS):
                            then(dve.tensor_tensor(pick[:, m, :, :], pick[:, m, :, :], place[:, :, :],
                                                   ALU.mult))
                            then(dve.tensor_reduce(slotf[:, :, m], pick[:, m, :, :], AX.X, ALU.add))
                        dve.tensor_copy(slot[:, :, :], slotf[:, :, :]).then_inc(s_slot, 1)

                    def experts():
                        then(dve.tensor_tensor(bnum[:, :, :], bnum[:, :, :],
                                               bend[:, :].rearrange("p (n e) -> p n e", n=1)
                                               .broadcast_to([P, BLOCKS, NE]), ALU.is_ge))
                        then(dve.tensor_reduce(bexp[:, :], bnum[:, :, :], AX.X, ALU.add))
                        then(dve.tensor_scalar(bexp[:, :], bexp[:, :], float(NE - 1), None, ALU.min))
                        then(dve.tensor_copy(block_expert[:, :], bexp[:, :]))

                    pipeline(dve, HI, 2, queries, scores,
                             (shift, None, softmax, top_two, picks, None, counts, starts, slots, experts))

        li.close()

        with ExitStack() as c:
            s = sb_in(c)
            y = s("e_y", [P, 2, D])
            xT = s("xT", [P, 2, KD, P])
            gate = s("e_gate", [P, 2, HE])
            hid = s("e_hid", [P, 2, HE])
            hT = s("e_hT", [P, 2, HC, P])
            left = s("left", [P, 2, S])
            m8 = s("m8", [P, 2, 8])
            xt_ps = sem("e_xt_ps")
            xt_cp = sem("e_xt_cp")
            gu_ps = sem("e_gu_ps")
            s_silu = sem("e_silu")
            s_hid = sem("e_hid_r")
            ht_ps = sem("e_ht_ps")
            ht_cp = sem("e_ht_cp")
            y_ps = sem("e_y_ps")
            y_cp = sem("e_y_cp")
            s_round = sem("t_round")
            s_bias = sem("t_bias")
            s_fix = sem("t_fix")
            ROUNDS = TOPK // 8
            G0, U0, DN0 = 0, KD * HE, 2 * KD * HE
            UN = 6
            GROUPS = -(-BLOCKS // UN)
            TI = NT // GROUPS
            assert UN % 2 == 0 and TI * GROUPS == NT and TI * 3 == UN
            ewf = ew[:, :, :].rearrange("p e m -> p (e m)")

            def blocks(eng, enter, expand, leave, middle):
                def step(n, u, first=False, last=False):
                    if not last:
                        enter(n + 1, 1 - u)
                    expand(n, u)
                    if not first:
                        leave(n - 1, 1 - u)
                    middle(n, u)

                enter(0, 0)
                step(0, 0, first=True)
                for r in range(1, UN):
                    step(r, r % 2)
                with eng.Fori(1, GROUPS - 1) as i:
                    for r in range(UN):
                        step(i * UN + r, r % 2)
                for n in range(UN * (GROUPS - 1), BLOCKS):
                    step(n, n % 2, last=n == BLOCKS - 1)
                leave(BLOCKS - 1, (BLOCKS - 1) % 2)

            def nothing(n, u):
                pass

            with nc.Block() as block:
                @block.sync
                def _(sp):
                    with sp.Fori(1, BLOCKS // 2) as i:
                        for u in range(2):
                            sp.wait_ge(xt_ps, 2 * i + (u + 1))
                            load_rows(sp, i, u)
                    for n in range(BLOCKS // 2 * 2, BLOCKS):
                        sp.wait_ge(xt_ps, n + 1)
                        load_rows(sp, n // 2, n % 2)
                    sp.wait_ge(y_cp, BLOCKS + 2)
                    sp.dma_start(y_dram[(BLOCKS - 1) * P:, :], y[:, (BLOCKS - 1) % 2, :])\
                        .then_inc(y_last, 16)

                @block.gpsimd
                def _(pool):
                    for u in range(2):
                        split_q(pool, 0, u)

                    def store(i, u):
                        pool.wait_ge(y_cp, 2 * i + (u + 3))
                        pool.dma_start(y_v[:, bass.ds(2 * i + u, 1), :]
                                       .rearrange("p n d -> p (n d)"), y[:, u, :]).then_inc(y_out[u], 16)

                    with pool.Fori(0, UN // 2 * (GROUPS - 1)) as i:
                        for u in range(2):
                            store(i, u)
                    for j in range(0, NT, TB):
                        pool.wait_ge(s_bias, j + 1)
                        diag = index[:, j, 0:P]
                        pool.affine_select(out=diag, in_=diag, compare_op=ALU.is_ge, fill=NEG, base=0,
                                           pattern=[[-1, P]], channel_multiplier=1).then_inc(s_fix, 1)
                    pool.wait_ge(s_fix, NB)
                    for n in range(UN * (GROUPS - 1), BLOCKS - 1):
                        store(n // 2, n % 2)

                @block.tensor
                def _(pe):
                    pe.sem_inc(xt_ps, 2)
                    pe.sem_inc(gu_ps, 2)
                    pe.sem_inc(y_ps, 2)

                    def enter(n, u):
                        pe.wait_ge(xg_in[u], 16 * ((n - u) // 2 + 1))
                        pe.wait_ge(xt_cp, n + 1)
                        for k in range(KD):
                            last = pe.transpose(ps[:, 4, k * P:(k + 1) * P], xg[:, u, k * P:(k + 1) * P],
                                                ident[:, :])
                        last.then_inc(xt_ps, 1)

                    def expand(n, u):
                        e = pe.value_load(block_expert[0:1, bass.ds(n, 1)], min_val=0, max_val=NE - 1)
                        pe.wait_ge(xt_cp, n + 2)
                        pe.wait_ge(s_hid, n + 1)
                        for bank, at in ((2 * u, G0), (2 * u + 1, U0)):
                            for k in range(KD):
                                last = pe.matmul(ps[:, bank, :], xT[:, u, k, :],
                                                 ewf[:, bass.ds(e * WE + (at + k * HE), HE)],
                                                 start=k == 0, stop=k == KD - 1)
                        last.then_inc(gu_ps, 1)

                    def leave(n, u):
                        e = pe.value_load(block_expert[0:1, bass.ds(n, 1)], min_val=0, max_val=NE - 1)
                        pe.wait_ge(ht_cp, n + 2)
                        pe.wait_ge(y_cp, n + 1)
                        for c in range(HC):
                            last = pe.matmul(ps[:, 6 + u, 0:D], hT[:, u, c, :],
                                             ewf[:, bass.ds(e * WE + (DN0 + c * D), D)],
                                             start=c == 0, stop=c == HC - 1)
                        last.then_inc(y_ps, 1)

                    def middle(n, u):
                        pe.wait_ge(s_hid, n + 3)
                        pe.wait_ge(ht_cp, n + 1)
                        for c in range(HC):
                            last = pe.transpose(ps[:, 5, c * P:(c + 1) * P], hid[:, u, c * P:(c + 1) * P],
                                                ident[:, :])
                        last.then_inc(ht_ps, 1)

                    blocks(pe, enter, expand, leave, middle)

                @block.scalar
                def _(act):
                    act.sem_inc(xt_cp, 1)
                    act.sem_inc(ht_cp, 1)

                    def enter(n, u):
                        act.wait_ge(xt_ps, n + 3)
                        act.wait_ge(gu_ps, n + 1)
                        act.activation(xT[:, u, :, :], ps[:, 4, 0:D].rearrange("p (k t) -> p k t", k=KD),
                                       ACT.Copy).then_inc(xt_cp, 1)

                    def expand(n, u):
                        act.wait_ge(gu_ps, n + 3)
                        act.activation(gate[:, u, :], ps[:, 2 * u, :], ACT.Silu).then_inc(s_silu, 1)

                    def middle(n, u):
                        act.wait_ge(ht_ps, n + 1)
                        act.wait_ge(y_ps, n + 1)
                        act.activation(hT[:, u, :, :], ps[:, 5, :].rearrange("p (c t) -> p c t", c=HC),
                                       ACT.Copy).then_inc(ht_cp, 1)

                    blocks(act, enter, expand, nothing, middle)

                @block.vector
                def _(dve):
                    dve.sem_inc(s_hid, 2)
                    dve.sem_inc(y_cp, 2)

                    def expand(n, u):
                        dve.wait_ge(s_silu, n + 1)
                        dve.tensor_tensor(hid[:, u, :], gate[:, u, :], ps[:, 2 * u + 1, :],
                                          ALU.mult).then_inc(s_hid, 1)

                    def leave(n, u):
                        dve.wait_ge(y_ps, n + 3)
                        if not isinstance(n, int) or n >= 2:
                            dve.wait_ge(y_out[u], 16 * ((n - u) // 2))
                        dve.tensor_copy(y[:, u, :], ps[:, 6 + u, 0:D]).then_inc(y_cp, 1)

                    def select(i, t, part):
                        tile = bass.ds(TI * i + t, 1)
                        done = 9 * (TI * i + t)
                        w = left[:, t, :]
                        if part == 0:
                            dve.tensor_copy(w, index[:, tile, :].rearrange("p a s -> p (a s)"))\
                                .then_inc(s_round, 1)
                        for r in ((0,), (1, 2), (3,))[part]:
                            dve.wait_ge(s_round, done + (2 * r + 1))
                            dve.sem_inc(stand, 1)
                            dve.max(m8[:, t, :], w).then_inc(s_round, 1)
                            dve.wait_ge(s_round, done + (2 * r + 2))
                            dve.sem_inc(stand, 1)
                            dve.match_replace(w, m8[:, t, :], w, TAKEN).then_inc(s_round, 1)
                        if part == 2:
                            dve.wait_ge(s_round, done + 9)
                            dve.tensor_scalar(index[:, tile, :].rearrange("p a s -> p (a s)"), w, TAKEN, NEG,
                                              ALU.not_equal, ALU.mult).then_inc(s_bias, 1)

                    def step(i, r, first=False):
                        n, u = (i * UN + r, r % 2)
                        there = not isinstance(n, int) or n < BLOCKS
                        if there:
                            expand(n, u)
                        if not first and (there or n == BLOCKS):
                            leave(n - 1, 1 - u)
                        ahead = r + AHEAD
                        if not isinstance(i, int) or i * UN + ahead < GROUPS * UN:
                            select(i + ahead // UN, ahead % UN // 3, ahead % 3)

                    AHEAD = 2
                    for r in range(AHEAD):
                        select(0, r // 3, r % 3)
                    for r in range(UN):
                        step(0, r, first=r == 0)
                    with dve.Fori(1, GROUPS - 1) as i:
                        for r in range(UN):
                            step(i, r)
                    for r in range(UN):
                        step(GROUPS - 1, r)
                    if GROUPS * UN == BLOCKS:
                        leave(BLOCKS - 1, 1)
        le.close()

        norm2 = Norm("norm2")
        fw_h = sb("fw_h", [P, 3 * KD * FI], F32R)
        fw_l = sb("fw_l", [P, 3 * KD * FI], F32R)
        with ExitStack() as c:
            s = sb_in(c)
            y_pick = (xn, s("y_pick", [P, NT, D]))
            wo_raw = s("wo_raw", [P, 2, D])
            wo_h = s("wo_h", [P, 2, D], F32R)
            wo_l = s("wo_l", [P, 2, D], F32R)
            qT_h = s("qT_h", [P, 2, S], F32R)
            qT_l = s("qT_l", [P, 2, S], F32R)
            sc = s("sc", [P, 2, TB, S])
            nmax = s("nmax", [P, 2, TB])
            rowsum = s("rowsum", [P, 2, TB])
            rrec = s("rrec", [P, 2, TB])
            pr = sc
            pT_h = s("pT_h", [P, 2, TB, S], F32R)
            pT_l = s("pT_l", [P, 2, TB, S], F32R)
            oT_h = s("oT_h", [P, 2, S], F32R)
            oT_l = s("oT_l", [P, 2, S], F32R)
            zero = s("zero", [P, S])
            FP = 3 * KD * FI // (NB * H // 2)
            f_raw = s("f_raw", [P, FP])
            f_in = sem("f_in")
            f_hi = sem("f_hi")
            f_split = sem("f_split")
            y_in = sem("a_y_in")
            y_sum = sem("a_y_sum")
            Y_STEPS = PICKS + 2
            o_in = [sem("a_o_in0"), sem("a_o_in1")]
            raw_free = sem("a_raw_free")
            wo_hi = sem("a_wo_hi")
            wo_ready = sem("a_wo_ready")
            wo_used = sem("a_wo_used")
            s_zero = sem("a_zero")
            q_hi = sem("a_q_hi")
            q_lo = sem("a_q_lo")
            sc_ps = sem("a_sc_ps")
            sc_ready = sem("a_sc_ready")
            exp_ready = sem("a_exp")
            r_ready = sem("a_r")
            pr_ready = sem("a_pr")
            pt_ps = sem("a_pt_ps")
            pt_hi = sem("a_pt_hi")
            pt_lo = sem("a_pt_lo")
            pv_ps = sem("a_pv_ps")
            o_hi = sem("a_o_hi")
            o_lo = sem("a_o_lo")
            s_res = sem("a_res")
            wo_v = wo.rearrange("(h p) n -> p h n", p=HD)
            Q, S0, PT0, PV, WO0 = 0, 1, 3, 5, 6

            def width(j):
                return (j + 1) * P

            def heads(eng, step):
                step(-1, 1, None, None, 0)
                step(0, 0, None, 0, 0)
                for b in range(NB):
                    with eng.Fori(0, H // 2 - 1) as i:
                        step(i * 2 + (b * H + 1), 1, b, b, b)
                        step(i * 2 + (b * H + 2), 0, b, b, b)
                    after = b + 1 if b + 1 < NB else None
                    step(b * H + H - 1, 1, b, b, after)
                    step(b * H + H, 0, b, after, after)

            def closes(h, before):
                return before is not None and isinstance(h, int) and h == (before + 1) * H

            with nc.Block() as block:
                @block.sync
                def _(sp):
                    def load_piece(n):
                        sp.dma_start(f_raw[:, :], f_weights[:, bass.ds(n * FP, FP)]).then_inc(f_in, 16)

                    def load_o(i, u):
                        sp.dma_start(wo_raw[:, u, :], wo_v[:, bass.ds(2 * i + u, 1), :]
                                     .rearrange("p h n -> p (h n)")).then_inc(o_in[u], 16)

                    for u in range(2):
                        load_o(0, u)
                    load_piece(0)
                    for b in range(NB):
                        with sp.Fori(0 if b else 1, H // 2) as i:
                            for u in range(2):
                                sp.wait_ge(raw_free, b * H + 2 * i + u - 1)
                                load_q(sp, i, u)
                                load_o(i, u)
                            sp.wait_ge(f_split, i + b * (H // 2))
                            load_piece(i + b * (H // 2))

                @block.gpsimd
                def _(pool):
                    pool.memset(zero[:, :], 0.0).then_inc(s_zero, 1)

                    def split_o(i, u):
                        pool.wait_ge(o_in[u], 16 * (i + 1))
                        pool.wait_ge(wo_used, 2 * i + (u + 1))
                        pool.sem_inc(stand, 1)
                        split_hi(pool, wo_h[:, u, :], wo_raw[:, u, :]).then_inc(wo_hi, 1)
                        pool.wait_ge(wo_hi, 2 * i + (u + 1))
                        pool.tensor_tensor(wo_l[:, u, :], wo_raw[:, u, :],
                                           wo_h[:, u, :].bitcast(F32), ALU.subtract).then_inc(wo_ready, 1)
                        pool.wait_ge(wq_ready, 2 * i + (u + 1))
                        pool.wait_ge(wo_ready, 2 * i + (u + 1))
                        pool.sem_inc(raw_free, 1)

                    def split(i, more=True):
                        if not isinstance(i, int) or i > 0:
                            split_q(pool, i, 1)
                        split_o(i, 0)
                        if more:
                            split_q(pool, i + 1, 0)
                        split_o(i, 1)
                        pool.wait_ge(f_in, 16 * (i + 1))
                        piece = bass.ds(i * FP, FP)
                        pool.tensor_copy(fw_h[:, piece], f_raw[:, :]).then_inc(f_hi, 1)
                        pool.wait_ge(f_hi, i + 1)
                        pool.tensor_tensor(fw_l[:, piece], f_raw[:, :], fw_h[:, piece].bitcast(F32),
                                           ALU.subtract).then_inc(f_split, 1)

                    n = [0]

                    def then(ins):
                        n[0] += 1
                        ins.then_inc(y_sum, 1)
                        pool.wait_ge(y_sum, n[0])

                    FETCH = 4
                    for u in range(2):
                        pool.wait_ge(y_out[u], 16 * ((BLOCKS - u) // 2))
                    pool.wait_ge(y_last, 16)
                    for i in range(FETCH):
                        split(i)
                        for j in range(i * NT // FETCH, (i + 1) * NT // FETCH):
                            for m in range(PICKS):
                                pool.indirect_dma_start(
                                    y_pick[m][:, j, :], None, y_dram,
                                    bass.IndirectOffsetOnAxis(slot[:, j, m:m + 1], 0)).then_inc(y_in, 16)
                    for j in range(NT):
                        split(FETCH + j)
                        pool.wait_ge(y_in, 16 * NT * PICKS)
                        for m in range(PICKS):
                            then(pool.tensor_scalar(y_pick[m][:, j, :], y_pick[m][:, j, :],
                                                    rw[:, j, m:m + 1], 1.0, ALU.mult, ALU.mult))
                        then(pool.tensor_tensor(y_pick[0][:, j, :], y_pick[0][:, j, :],
                                                y_pick[1][:, j, :], ALU.add))
                        then(pool.tensor_tensor(acc[:, j, :], acc[:, j, :], y_pick[0][:, j, :],
                                                ALU.add))
                    assert n[0] == Y_STEPS * NT
                    with pool.Fori(FETCH + NT, NB * H // 2 - 1) as i:
                        split(i)
                    split(NB * H // 2 - 1, more=False)

                @block.tensor
                def _(pe):
                    pe.sem_inc(a_q_ps, 2)
                    pe.sem_inc(wo_used, 2)

                    def clear_output():
                        pe.wait_ge(s_zero, 1)
                        for m in range(TB // 2):
                            pe.matmul(ps[:, WO0 + m, :], ident[:, :], zero[:, :], start=True, stop=False,
                                      skip_group_check=True)

                    def project(h, u, b):
                        pe.wait_ge(wq_ready, h + 1)
                        pe.wait_ge(q_lo, h + 1)
                        for k in range(KD):
                            last = matmul3(pe, ps[:, Q, :], wq_h[:, u, k, :], wq_l[:, u, k, :],
                                           xnT_h[:, k, b * S:(b + 1) * S],
                                           xnT_l[:, k, b * S:(b + 1) * S], k == 0, k == KD - 1)
                        last.then_inc(a_q_ps, 1)

                    def score(h, u, b, j):
                        if j == 0:
                            pe.wait_ge(q_lo, h + 2)
                        pe.wait_ge(sc_ready, TB * h + (j + 1))
                        matmul3(pe, ps[:, S0 + j % 2, 0:width(j)], qT_h[:, u, j * P:(j + 1) * P],
                                qT_l[:, u, j * P:(j + 1) * P], kT_h[:, b * S:b * S + width(j)],
                                kT_l[:, b * S:b * S + width(j)], True, True).then_inc(sc_ps, 1)

                    def turn(h, u, j):
                        pe.wait_ge(pr_ready, TB * h + (j + 1))
                        pe.wait_ge(pt_lo, TB * h + (j + 1))
                        for n in range(j + 1):
                            last = pe.transpose(ps[:, PT0 + j % 2, n * P:(n + 1) * P],
                                                pr[:, u, j, n * P:(n + 1) * P], ident[:, :])
                        last.then_inc(pt_ps, 1)

                    def weigh(h, u, b):
                        pe.wait_ge(pt_lo, TB * h + (2 + TB))
                        pe.wait_ge(o_lo, h + 1)
                        for n in range(TB):
                            last = matmul3(pe, ps[:, PV, n * P:S], v_h[:, b * TB + n, :],
                                           v_l[:, b * TB + n, :], pT_h[:, u, n, n * P:S],
                                           pT_l[:, u, n, n * P:S], n == 0, n == TB - 1)
                        last.then_inc(pv_ps, 1)

                    def output(h, u):
                        pe.wait_ge(wo_ready, h + 1)
                        pe.wait_ge(o_lo, h + 2)
                        for j in range(TB):
                            o = ps[:, WO0 + j // 2, (j % 2) * D:(j % 2 + 1) * D]
                            last = matmul3(pe, o, oT_h[:, u, j * P:(j + 1) * P],
                                           oT_l[:, u, j * P:(j + 1) * P], wo_h[:, u, :],
                                           wo_l[:, u, :], False, False, skip_group_check=True)
                        last.then_inc(wo_used, 1)

                    def step(h, u, before, now, after):
                        v = 1 - u
                        if now is not None:
                            turn(h, u, 0)
                        if after is not None:
                            project(h + 1, v, after)
                        if now is not None:
                            turn(h, u, 1)
                        if before is not None:
                            weigh(h - 1, v, before)
                        if after is not None:
                            score(h + 1, v, after, 0)
                        if now is not None:
                            turn(h, u, 2)
                        if after is not None:
                            score(h + 1, v, after, 1)
                        if now is not None:
                            turn(h, u, 3)
                        if before is not None:
                            output(h - 1, v)
                        if after is not None:
                            score(h + 1, v, after, 2)
                            score(h + 1, v, after, 3)
                        if isinstance(h, int) and h == 0:
                            clear_output()
                        if closes(h, before) and now is not None:
                            pe.wait_ge(s_res, (before + 1) * TB)
                            clear_output()

                    heads(pe, step)

                @block.scalar
                def _(act):
                    def query(h, u):
                        act.wait_ge(a_q_ps, h + 3)
                        act.activation(qT_h[:, u, :], ps[:, Q, :], ACT.Copy).then_inc(q_hi, 1)

                    def turned(h, u, j):
                        act.wait_ge(pt_ps, TB * h + (j + 1))
                        act.activation(
                            pT_h[:, u, 0:j + 1, j * P:(j + 1) * P],
                            ps[:, PT0 + j % 2, 0:width(j)].rearrange("p (c t) -> p c t", t=P),
                            ACT.Copy).then_inc(pt_hi, 1)

                    def exponential(h, u, j):
                        act.wait_ge(sc_ready, TB * h + (j + 2 + 1))
                        act.activation(pr[:, u, j, 0:width(j)], sc[:, u, j, 0:width(j)],
                                       ACT.Exp, bias=nmax[:, u, j:j + 1], scale=-1.0,
                                       accum_out=rowsum[:, u, j:j + 1]).then_inc(exp_ready, 1)

                    def weighed(h, u):
                        act.wait_ge(pv_ps, h + 1)
                        act.activation(oT_h[:, u, :], ps[:, PV, :], ACT.Copy).then_inc(o_hi, 1)

                    def step(h, u, before, now, after):
                        v = 1 - u
                        if now is not None:
                            turned(h, u, 0)
                        if after is not None:
                            query(h + 1, v)
                        if now is not None:
                            exponential(h, u, 3)
                            turned(h, u, 1)
                        if before is not None:
                            weighed(h - 1, v)
                        if now is not None:
                            turned(h, u, 2)
                            turned(h, u, 3)
                        if after is not None:
                            exponential(h + 1, v, 0)
                            exponential(h + 1, v, 1)
                            exponential(h + 1, v, 2)

                    heads(act, step)
                    norm_root(act, 0, norm2)

                @block.vector
                def _(dve):
                    dve.sem_inc(q_lo, 1)
                    dve.sem_inc(o_lo, 1)
                    dve.sem_inc(sc_ready, 2)
                    dve.sem_inc(pt_lo, 2)

                    def query(h, u):
                        dve.wait_ge(q_hi, h + 1)
                        dve.tensor_tensor(qT_l[:, u, :], ps[:, Q, :], qT_h[:, u, :].bitcast(F32),
                                          ALU.subtract).then_inc(q_lo, 1)

                    def masked(h, u, b, j):
                        dve.wait_ge(sc_ps, TB * h + (j + 1))
                        dve.sem_inc(stand, 1)
                        dve.tensor_tensor_reduce(
                            sc[:, u, j, 0:width(j)], ps[:, S0 + j % 2, 0:width(j)],
                            index[:, b * TB + j, 0:width(j)], -SCALE, 3e38, ALU.add, ALU.min,
                            nmax[:, u, j:j + 1]).then_inc(sc_ready, 1)

                    def normalise(h, u, j):
                        dve.wait_ge(exp_ready, TB * h + (j + 1))
                        dve.reciprocal(rrec[:, u, j:j + 1], rowsum[:, u, j:j + 1]).then_inc(r_ready, 1)
                        dve.wait_ge(r_ready, TB * h + (j + 1))
                        dve.tensor_scalar(pr[:, u, j, 0:width(j)], pr[:, u, j, 0:width(j)],
                                          rrec[:, u, j:j + 1], None, ALU.mult).then_inc(pr_ready, 1)

                    def turned(h, u, j):
                        dve.wait_ge(pt_hi, TB * h + (j + 1))
                        dve.tensor_tensor(
                            pT_l[:, u, 0:j + 1, j * P:(j + 1) * P],
                            ps[:, PT0 + j % 2, 0:width(j)].rearrange("p (c t) -> p c t", t=P),
                            pT_h[:, u, 0:j + 1, j * P:(j + 1) * P].bitcast(F32),
                            ALU.subtract).then_inc(pt_lo, 1)

                    def weighed(h, u):
                        dve.wait_ge(o_hi, h + 1)
                        dve.tensor_tensor(oT_l[:, u, :], ps[:, PV, :], oT_h[:, u, :].bitcast(F32),
                                          ALU.subtract).then_inc(o_lo, 1)

                    def step(h, u, before, now, after):
                        v = 1 - u
                        last = isinstance(h, int) and h == NB * H
                        if last:
                            norm_stats(dve, 0, norm2)
                        if now is not None:
                            normalise(h, u, 2)
                        if after is not None:
                            query(h + 1, v)
                        if now is not None:
                            turned(h, u, 0)
                            turned(h, u, 1)
                            normalise(h, u, 3)
                        if before is not None:
                            weighed(h - 1, v)
                        if after is not None:
                            masked(h + 1, v, after, 0)
                        if now is not None:
                            turned(h, u, 2)
                        if after is not None:
                            masked(h + 1, v, after, 1)
                        if now is not None:
                            turned(h, u, 3)
                        if after is not None:
                            normalise(h + 1, v, 0)
                            normalise(h + 1, v, 1)
                            masked(h + 1, v, after, 2)
                            masked(h + 1, v, after, 3)
                        if last:
                            norm_scale(dve, 0, norm2)
                        if closes(h, before):
                            dve.wait_ge(y_sum, Y_STEPS * TB * (before + 1))
                            dve.wait_ge(wo_used, (before + 1) * H + 2)
                            for j in range(TB):
                                row = acc[:, before * TB + j, :]
                                dve.tensor_tensor(row, ps[:, WO0 + j // 2, (j % 2) * D:(j % 2 + 1) * D],
                                                  row, ALU.add).then_inc(s_res, 1)

                    heads(dve, step)

        CH = KD
        XR = R + 2 * NS
        TS = TOK // P
        assert w_x.shape[1] == XR and NS == 2 * TS
        with ExitStack() as c:
            s = sb_in(c)
            w_xs = s("w_xs", [P, KD, XR])
            w_xh = s("w_xh", [P, KD, XR], F32R)
            w_xl = s("w_xl", [P, KD, XR], F32R)
            w_ds = s("w_ds", [R, D])
            w_dh = s("w_dh", [R, D], F32R)
            w_dl = s("w_dl", [R, D], F32R)
            bd = s("bd", [P, CH])
            dskip = s("dskip", [P, 1, D])
            bc = s("bc", [XR, TOK])
            crow = s("crow", [P, NT, 2 * NS])
            dt = s("dt", [P, CH, TOK])
            xdt = s("xdt", [P, CH, TOK])
            a_neg = s("a_neg", [P, CH, NS])
            bcast = index[:, 0:NT // 2, :].rearrange("p (u a) s -> p u (a s)", u=2)
            xd = index[:, NT // 2:, :].rearrange("p a (b d) -> p (a b) d", d=D)
            da = s("da", [P, 2, CH, NB, S])
            dbx = s("dbx", [P, 2, CH, TOK])
            xf = dbx[:, 0, :, :]
            soft = dbx[:, 1, :, :]
            xcur_h, xcur_l = wq_h[:, 0, :, :], wq_l[:, 0, :, :]
            wg_h, wg_l, wu_h, wu_l = (
                w[:, at * KD * FI:(at + 1) * KD * FI].rearrange("p (k n) -> p k n", k=KD)
                for at in range(2) for w in (fw_h, fw_l))
            wd_h, wd_l = (w[:, 2 * KD * FI:].rearrange("p (c n) -> p c n", c=FC) for w in (fw_h, fw_l))
            HF = FI // 2
            sil = s("sil", [P, 2, HF])
            hid = s("f_hid", [P, FI])
            mag = xn[:, 0:FI // D, :].rearrange("p j d -> p (j d)")
            hT = xn[:, FI // D:, :].rearrange("p j (c t) -> p (j c) t", t=P)
            hc = s("hc", [P, 2, 2, D])
            hT_h = s("f_hT_h", [P, FC, P], F32R)
            hT_l = s("f_hT_l", [P, FC, P], F32R)
            dl_h, dl_l = (t[0:R, :, :].rearrange("p c t -> p (c t)") for t in (hT_h, hT_l))
            cmp = s("f_cmp", [P, 6, FI // 4], BF16)
            win = s("f_win", [P, 8, FI // 4], BF16)
            wx_in = sem("m_wx_in")
            wd_in = sem("m_wd_in")
            al_in = sem("m_al_in")
            ds_in = sem("m_ds_in")
            wx_split = sem("m_wx_split")
            wd_split = sem("m_wd_split")
            s_xt = sem("m_xt")
            xt_hi = sem("m_xt_hi")
            xt_lo = sem("m_xt_lo")
            xp_ps = sem("m_xp_ps")
            dl_hi = sem("m_dl_hi")
            dl_lo = sem("m_dl_lo")
            s_bc = sem("m_bc")
            bc_out = sem("m_bc_out")
            c_ps = sem("m_c_ps")
            c_ready = sem("m_c_ready")
            dt_ps = sem("m_dt_ps")
            u_abs = sem("m_u_abs")
            s_soft = sem("m_soft")
            s_relu = sem("m_relu")
            s_dt = sem("m_dt")
            s_xdt = sem("m_xdt")
            s_xdt0 = sem("m_xdt0")
            s_a = sem("m_a")
            a_ready = sem("m_a_ready")
            d_added = sem("m_d_added")
            bc_in = [sem("z_bc0"), sem("z_bc1")]
            da_zero = sem("z_da_zero")
            da_ready = sem("z_da")
            dbx_ready = [sem("z_dbx0"), sem("z_dbx1")]
            s_scan = sem("z_scan")
            h_ps = sem("z_h_ps")
            y_add = sem("z_y_add")
            hc_ready = sem("z_hc")
            y_pool = sem("z_y_pool")
            GV = NT // 2 - 1
            VT = 2 * GV
            x_cur = sem("z_x_cur")
            gu_ps = sem("z_gu_ps")
            s_silu = sem("z_silu")
            s_prod = sem("z_prod")
            s_abs = sem("z_abs")
            s_cmp = sem("z_cmp")
            s_sparse = sem("z_sparse")
            ht_ps = sem("z_ht_ps")
            ht_cp = sem("z_ht_cp")
            ht_lo = sem("z_ht_lo")
            dn_ps = sem("z_dn_ps")
            acc_add = sem("z_acc_add")
            out_done = sem("z_out_done")
            GU, HT, ST = 0, 2, 4
            DT = (6, 7, 2, 3)

            def steps(eng, step):
                step(0, True, True)
                with eng.Fori(1, NT - 2) as i:
                    step(i, True, True)
                step(NT - 2, True, False)
                step(NT - 1, False, False)

            with nc.Block() as block:
                @block.sync
                def _(sp):
                    sp.dma_start(w_xs[:, :, :], w_x.rearrange("(k p) n -> p k n", p=P)).then_inc(wx_in, 16)
                    sp.dma_start(w_ds[:, :], w_dt).then_inc(wd_in, 16)
                    sp.dma_start(dskip[:, :, :], d_skip.rearrange("(o a) n -> o a n", o=1)
                                 .broadcast_to([P, 1, D])).then_inc(ds_in, 16)
                    sp.dma_start(a_neg[:, :, :], a_log.rearrange("(k p) n -> p k n", p=P)).then_inc(al_in, 16)
                    sp.dma_start(bd[:, :], b_dt).then_inc(al_in, 16)
                    sp.wait_ge(s_bc, NB)
                    sp.dma_start(b_dram, bc[R:R + NS, :]).then_inc(bc_out, 16)
                    sp.wait_ge(bc_out, 16)

                    def load(i, u):
                        sp.dma_start(bcast[:, u:u + 1, :], b_rows[bass.ds(2 * i + u, 1), :, :]
                                     .broadcast_to([P, 1, TOK])).then_inc(bc_in[u], 16)

                    load(0, 0)
                    load(0, 1)
                    with sp.Fori(1, NS // 2) as i:
                        for u in range(2):
                            sp.wait_ge(dbx_ready[u], i)
                            load(i, u)
                    for g in range(NT // 2):
                        if g < GV:
                            sp.wait_ge(y_add, VT * NS + 2 * g + 2)
                        else:
                            sp.wait_ge(y_pool, NS + 2)
                        sp.dma_start(out_rows[:, 2 * g:2 * g + 2, :],
                                     acc[:, 2 * g:2 * g + 2, :]).then_inc(out_done, 16)
                    sp.wait_ge(out_done, 16 * NT // 2)

                @block.gpsimd
                def _(pool):
                    pool.sem_inc(ht_lo, 1)
                    pool.sem_inc(y_pool, 2)
                    pool.wait_ge(wx_in, 16)
                    split_hi(pool, w_xh[:, :, :], w_xs[:, :, :]).then_inc(wx_split, 1)
                    pool.wait_ge(wx_split, 1)
                    pool.tensor_tensor(w_xl[:, :, :], w_xs[:, :, :], w_xh[:, :, :].bitcast(F32),
                                       ALU.subtract).then_inc(wx_split, 1)
                    pool.wait_ge(wd_in, 16)
                    split_hi(pool, w_dh[:, :], w_ds[:, :]).then_inc(wd_split, 1)
                    pool.wait_ge(wd_split, 1)
                    pool.tensor_tensor(w_dl[:, :], w_ds[:, :], w_dh[:, :].bitcast(F32),
                                       ALU.subtract).then_inc(wd_split, 1)
                    for u in range(2):
                        for k in range(CH):
                            pool.memset(da[:, u, k, :, 0:1], 0.0).then_inc(da_zero, 1)
                    pool.wait_ge(ds_in, 16)
                    pool.wait_ge(norm2.xn, NT)
                    pool.tensor_tensor(xd, xn[:, :, :], dskip[:, :, :].broadcast_to([P, NT, D]),
                                       ALU.mult).then_inc(d_added, 1)
                    pool.wait_ge(d_added, 1)
                    pool.tensor_tensor(acc[:, :, :], acc[:, :, :], xd, ALU.add).then_inc(d_added, 1)

                    def dbx_of(u):
                        pool.tensor_tensor(dbx[:, u, :, :], xdt[:, :, :],
                                           bcast[:, u:u + 1, :].broadcast_to([P, CH, TOK]),
                                           ALU.mult).then_inc(dbx_ready[u], 1)

                    pool.wait_ge(bc_in[1], 16)
                    pool.wait_ge(s_dt, 1)
                    pool.tensor_tensor(xdt[:, 0, :], dt[:, 0, :], xf[:, 0, :], ALU.mult).then_inc(s_xdt0, 1)
                    pool.wait_ge(s_xdt, 1)
                    pool.wait_ge(s_xdt0, 1)
                    dbx_of(1)

                    def add_state(i, u):
                        pool.wait_ge(hc_ready, 2 * i + (u + 2))
                        pool.wait_ge(y_pool, 2 * i + (u + 2))
                        pool.wait_ge(acc_add, i + (u + 1))
                        pool.tensor_tensor(acc[:, VT:, :], acc[:, VT:, :], hc[:, u, :, :],
                                           ALU.add).then_inc(y_pool, 1)

                    def lo_parts(i):
                        pool.wait_ge(ht_cp, 4 * i + 4)
                        pool.wait_ge(dn_ps, i + 1)
                        pool.sem_inc(stand, 1)
                        pool.tensor_tensor(hT_l[:, :, :], hT[:, :, :], hT_h[:, :, :].bitcast(F32),
                                           ALU.subtract).then_inc(ht_lo, 1)

                    def next_dbx(i, u):
                        pool.wait_ge(bc_in[u], 16 * (i + 2))
                        pool.wait_ge(h_ps, 8 * i + (4 * u + 4))
                        dbx_of(u)

                    def step(i, next1, next2):
                        lo_parts(i)
                        if next1:
                            next_dbx(i, 0)
                        add_state(i, 0)
                        if next1:
                            next_dbx(i, 1)
                        add_state(i, 1)

                    steps(pool, step)

                @block.tensor
                def _(pe):
                    pe.sem_inc(dn_ps, 1)
                    transpose_rows(pe, norm2.xn, s_xt)
                    pe.wait_ge(wx_split, 2)
                    for b in range(NB):
                        pe.wait_ge(xt_lo, (b + 1) * TB // 2)
                        for k in range(KD):
                            last = matmul3(pe, ps[0:XR, 4 + b, :], w_xh[:, k, :], w_xl[:, k, :],
                                           xnT_h[:, k, b * S:(b + 1) * S], xnT_l[:, k, b * S:(b + 1) * S],
                                           k == 0, k == KD - 1)
                        last.then_inc(xp_ps, 1)

                    def gate_up(i, m):
                        if m == 0:
                            pe.wait_ge(x_cur, 2 * i + 2)
                        if not (isinstance(i, int) and i == 0 and m == 0):
                            pe.wait_ge(s_prod, 2 * i + m)
                        for bank, wh, wl in ((GU, wg_h, wg_l), (GU + 1, wu_h, wu_l)):
                            for k in range(KD):
                                last = matmul3(pe, ps[:, bank, :], xcur_h[:, k, :], xcur_l[:, k, :],
                                               wh[:, k, m * HF:(m + 1) * HF],
                                               wl[:, k, m * HF:(m + 1) * HF], k == 0, k == KD - 1)
                        last.then_inc(gu_ps, 1)

                    def turn_hidden(i):
                        pe.wait_ge(s_sparse, 4 * i + 4)
                        for m in range(2):
                            if m == 1:
                                pe.wait_ge(acc_add, i + 1)
                            for n in range(4):
                                q = 4 * m + n
                                last = pe.transpose(ps[:, HT + m, n * P:(n + 1) * P],
                                                    hid[:, q * P:(q + 1) * P], ident[:, :])
                            last.then_inc(ht_ps, 1)

                    def down(i):
                        pe.wait_ge(ht_lo, i + 2)
                        for n in range(FC):
                            last = matmul3(pe, ps[:, HT + 1, 0:D], hT_h[:, n, :], hT_l[:, n, :],
                                           wd_h[:, n, :], wd_l[:, n, :], n == 0, n == FC - 1)
                        last.then_inc(dn_ps, 1)

                    def turn_state(i, u, groups):
                        pe.wait_ge(s_scan, 2 * i + (u + 1))
                        for g in groups:
                            if g < GV:
                                pe.wait_ge(y_add, 2 * VT * i + (VT * u + 2 * g + 2))
                            else:
                                pe.wait_ge(hc_ready, 2 * i + (u + 1))
                            for m in range(2):
                                for k in range(CH):
                                    last = pe.transpose(ps[:, ST + g, (2 * m + k) * P:(2 * m + k + 1) * P],
                                                        dbx[:, u, k, (2 * g + m) * P:(2 * g + m + 1) * P],
                                                        ident[:, :])
                            last.then_inc(h_ps, 1)

                    gate_up(0, 0)
                    pe.wait_ge(wd_split, 2)
                    for b in range(NB):
                        pe.wait_ge(dl_lo, b + 1)
                        for k in range(CH):
                            matmul3(pe, ps[:, DT[b * CH + k], :], w_dh[:, k * P:(k + 1) * P],
                                    w_dl[:, k * P:(k + 1) * P], dl_h[:, b * S:(b + 1) * S],
                                    dl_l[:, b * S:(b + 1) * S], True, True).then_inc(dt_ps, 1)
                    gate_up(0, 1)
                    for j in range(NT):
                        last = pe.transpose(ps[:, 4, 2 * NS * j:2 * NS * (j + 1)],
                                            bc[R:XR, j * P:(j + 1) * P], ident[R:XR, R:XR])
                    last.then_inc(c_ps, 1)
                    gate_up(1, 0)
                    pe.wait_ge(s_relu, NB * CH)
                    pe.wait_ge(c_ready, 1)

                    def step(i, next1, next2):
                        turn_hidden(i)
                        if next1:
                            gate_up(i + 1, 1)
                        turn_state(i, 0, range(NT // 2))
                        turn_state(i, 1, (0,))
                        down(i)
                        turn_state(i, 1, (1, 2, 3))
                        if next2:
                            gate_up(i + 2, 0)

                    steps(pe, step)

                @block.scalar
                def _(act):
                    def decay(i, u):
                        for k in range(CH):
                            act.activation(da[:, u, k, :, 1:S],
                                           dt[:, k, :].rearrange("p (b t) -> p b t", b=NB)[:, :, 1:S],
                                           ACT.Exp, scale=a_neg[:, k, bass.ds(2 * i + u, 1)])\
                                .then_inc(da_ready, 1)

                    def silu(i, m):
                        act.wait_ge(gu_ps, 2 * i + (m + 1))
                        act.activation(sil[:, m, :], ps[:, GU, :], ACT.Silu).then_inc(s_silu, 1)

                    def magnitude(i, m):
                        act.wait_ge(s_prod, 2 * i + (m + 1))
                        half = slice(m * HF, (m + 1) * HF)
                        act.activation(mag[:, half], hid[:, half], ACT.Abs).then_inc(s_abs, 1)

                    def fetch(i):
                        for src, dst in ((xnT_h, xcur_h), (xnT_l, xcur_l)):
                            act.activation(dst, src[:, :, bass.ds(i * P, P)], ACT.Copy)\
                                .then_inc(x_cur, 1)

                    def turned(i):
                        act.wait_ge(ht_lo, i + 1)
                        act.wait_ge(dn_ps, i + 1)
                        for m in range(2):
                            act.wait_ge(ht_ps, 2 * i + (m + 1))
                            for to in (hT_h, hT):
                                act.activation(to[:, 4 * m:4 * m + 4, :],
                                               ps[:, HT + m, :].rearrange("p (c t) -> p c t", t=P),
                                               ACT.Copy).then_inc(ht_cp, 1)

                    norm_root(act, 1, norm2)
                    for g in range(NT // 2):
                        act.wait_ge(s_xt, g + 1)
                        act.activation(pair(xnT_h, g), bank_pair(g), ACT.Copy).then_inc(xt_hi, 1)
                        act.activation(pair(xf, g), bank_pair(g), ACT.Copy).then_inc(xt_hi, 1)
                    act.wait_ge(xt_lo, 1)
                    fetch(0)
                    for b in range(NB):
                        act.wait_ge(xp_ps, b + 1)
                        act.activation(dl_h[:, b * S:(b + 1) * S], ps[0:R, 4 + b, :], ACT.Copy).then_inc(dl_hi, 1)
                        act.activation(bc[R:XR, b * S:(b + 1) * S], ps[R:XR, 4 + b, :],
                                       ACT.Copy).then_inc(s_bc, 1)
                    silu(0, 0)
                    act.wait_ge(al_in, 32)
                    for n in range(NB * CH):
                        b, k = n // CH, n % CH
                        act.wait_ge(dt_ps, n + 1)
                        act.activation(soft[:, k, b * S:(b + 1) * S], ps[:, DT[n], :], ACT.Abs,
                                       bias=bd[:, k:k + 1]).then_inc(u_abs, 1)
                    silu(0, 1)
                    fetch(1)
                    act.wait_ge(d_added, 1)
                    magnitude(0, 0)
                    magnitude(0, 1)
                    act.activation(a_neg[:, :, :], a_neg[:, :, :], ACT.Exp).then_inc(s_a, 1)
                    act.wait_ge(u_abs, NB * CH)
                    act.activation(soft, soft, ACT.Exp, scale=-1.0).then_inc(s_soft, 1)
                    act.wait_ge(s_soft, 1)
                    for k in range(CH):
                        act.activation(soft[:, k, :], soft[:, k, :], ACT.Ln, bias=1.0).then_inc(s_soft, 1)
                    silu(1, 0)
                    act.wait_ge(c_ps, 1)
                    act.activation(crow[:, :, :], ps[:, 4, 0:NT * 2 * NS].rearrange("p (j n) -> p j n", n=2 * NS),
                                   ACT.Copy).then_inc(c_ready, 1)
                    act.wait_ge(da_zero, 2 * CH)
                    act.wait_ge(a_ready, 1)
                    act.wait_ge(s_dt, CH)
                    act.sem_inc(hc_ready, 1)
                    decay(0, 0)
                    decay(0, 1)

                    def scale_state(i, u):
                        act.wait_ge(h_ps, 8 * i + (4 * u + 4))
                        act.wait_ge(y_pool, 2 * i + (u + 1))
                        for m in range(2):
                            last = act.activation(hc[:, u, m, :], ps[:, ST + GV, m * D:(m + 1) * D], ACT.Copy,
                                                  scale=crow[:, VT + m, bass.ds(2 * i + (u + NS), 1)])
                        last.then_inc(hc_ready, 1)

                    def step(i, next1, next2):
                        if next1:
                            if not isinstance(i, int) or i > 0:
                                silu(i + 1, 0)
                        turned(i)
                        if next1:
                            silu(i + 1, 1)
                            magnitude(i + 1, 0)
                        scale_state(i, 0)
                        if next2:
                            act.wait_ge(gu_ps, 2 * i + 4)
                            fetch(i + 2)
                        if next1:
                            magnitude(i + 1, 1)
                            act.wait_ge(s_scan, 2 * i + 1)
                            decay(i + 1, 0)
                            act.wait_ge(s_scan, 2 * i + 2)
                            decay(i + 1, 1)
                        scale_state(i, 1)

                    steps(act, step)

                @block.vector
                def _(dve):
                    dve.sem_inc(y_add, VT)
                    dve.sem_inc(acc_add, 1)

                    def scan(i, u):
                        dve.wait_ge(dbx_ready[u], i + 1)
                        dve.wait_ge(da_ready, 4 * i + (2 * u + 2))
                        dve.sem_inc(stand, 1)
                        h = dbx[:, u, :, :].rearrange("p k t -> p (k t)")
                        dve.tensor_tensor_scan(h, da[:, u, :, :, :].rearrange("p k b t -> p (k b t)"),
                                               h, 0.0, ALU.mult, ALU.add).then_inc(s_scan, 1)

                    def add_state(i, u, groups):
                        dve.wait_ge(y_add, 2 * VT * i + (VT * u + VT))
                        dve.wait_ge(acc_add, i + (1 + u))
                        for g in groups:
                            dve.wait_ge(h_ps, 8 * i + (4 * u + g + 1))
                            dve.sem_inc(stand, 1)
                            for m in range(2):
                                j = 2 * g + m
                                dve.scalar_tensor_tensor(
                                    acc[:, j, :], ps[:, ST + g, m * D:(m + 1) * D],
                                    crow[:, j, bass.ds(2 * i + (u + NS), 1)], acc[:, j, :],
                                    ALU.mult, ALU.add).then_inc(y_add, 1)

                    def product(i, m):
                        if not isinstance(i, int) or i > 0:
                            dve.wait_ge(ht_ps, 2 * i + (m - 1))
                        dve.wait_ge(s_silu, 2 * i + (m + 1))
                        dve.tensor_tensor(hid[:, m * HF:(m + 1) * HF], sil[:, m, :], ps[:, GU + 1, :],
                                          ALU.mult).then_inc(s_prod, 1)

                    def sparsify(i):
                        h4 = hid[:, :].rearrange("p (g f) -> p f g", f=4)
                        a4 = mag.rearrange("p (g f) -> p f g", f=4)
                        G = FI // 4
                        dve.wait_ge(s_abs, 2 * i + 2)
                        for at, first, n in ((0, 0, 3), (3, 1, 2), (5, 2, 1)):
                            dve.tensor_tensor(cmp[:, at:at + n, :],
                                              a4[:, first:first + 1, :].broadcast_to([P, n, G]),
                                              a4[:, first + 1:4, :], ALU.is_ge).then_inc(s_cmp, 1)
                        c01, c02, c03, c12, c13, c23 = (cmp[:, n, :] for n in range(6))
                        dve.wait_ge(s_cmp, 10 * i + 3)
                        dve.tensor_tensor(win[:, 0, :], c01, c02, ALU.add).then_inc(s_cmp, 1)
                        dve.tensor_tensor(win[:, 1:3, :], cmp[:, 3:5, :], cmp[:, 4:6, :], ALU.add)\
                            .then_inc(s_cmp, 1)
                        dve.tensor_tensor(win[:, 3, :], c02, c12, ALU.add).then_inc(s_cmp, 1)
                        dve.wait_ge(s_cmp, 10 * i + 6)
                        dve.tensor_tensor(win[:, 5, :], win[:, 1, :], c01, ALU.subtract).then_inc(s_cmp, 1)
                        dve.tensor_tensor(win[:, 4, :], win[:, 0, :], c03, ALU.add).then_inc(s_cmp, 1)
                        dve.tensor_tensor(win[:, 7, :], win[:, 2, :], c03, ALU.add).then_inc(s_cmp, 1)
                        dve.tensor_tensor(win[:, 6, :], c23, win[:, 3, :], ALU.subtract).then_inc(s_cmp, 1)
                        dve.wait_ge(s_cmp, 10 * i + 10)
                        for f, bound, op in ((0, 2.0, ALU.is_ge), (1, 1.0, ALU.is_ge), (3, 1.0, ALU.is_le),
                                             (2, 0.0, ALU.is_ge)):
                            dve.scalar_tensor_tensor(h4[:, f, :], win[:, 4 + f, :], bound, h4[:, f, :],
                                                     op, ALU.mult).then_inc(s_sparse, 1)

                    def residual(i):
                        dve.wait_ge(y_add, 2 * VT * i + 2 * VT)
                        dve.wait_ge(y_pool, 2 * i + 3)
                        dve.wait_ge(dn_ps, i + 2)
                        row = acc[:, bass.ds(i, 1), :].rearrange("p a d -> p (a d)")
                        dve.tensor_tensor(row, ps[:, HT + 1, 0:D], row, ALU.add).then_inc(acc_add, 1)

                    norm_stats(dve, 1, norm2)
                    norm_scale(dve, 1, norm2)
                    for g in range(NT // 2):
                        dve.wait_ge(xt_hi, 2 * g + 2)
                        dve.tensor_tensor(pair(xnT_l, g), pair(xf, g), pair(xnT_h, g).bitcast(F32),
                                          ALU.subtract).then_inc(xt_lo, 1)
                    for b in range(NB):
                        dve.wait_ge(dl_hi, b + 1)
                        dve.wait_ge(s_bc, b + 1)
                        dve.tensor_tensor(dl_l[:, b * S:(b + 1) * S], ps[0:R, 4 + b, :],
                                          dl_h[:, b * S:(b + 1) * S].bitcast(F32),
                                          ALU.subtract).then_inc(dl_lo, 1)
                    product(0, 0)
                    for n in range(NB * CH):
                        b, k = n // CH, n % CH
                        dve.wait_ge(u_abs, n + 1)
                        dve.tensor_scalar(dt[:, k, b * S:(b + 1) * S], ps[:, DT[n], :], bd[:, k:k + 1], 0.0,
                                          ALU.add, ALU.max).then_inc(s_relu, 1)
                    product(0, 1)
                    sparsify(0)
                    dve.wait_ge(s_a, 1)
                    dve.tensor_scalar(a_neg[:, :, :], a_neg[:, :, :], -1.0, None, ALU.mult).then_inc(a_ready, 1)
                    dve.wait_ge(s_relu, NB * CH)
                    for k in range(CH):
                        dve.wait_ge(s_soft, k + 2)
                        dve.tensor_tensor(dt[:, k, :], dt[:, k, :], soft[:, k, :],
                                          ALU.add).then_inc(s_dt, 1)
                    dve.wait_ge(s_dt, CH)
                    dve.tensor_tensor(xdt[:, 1, :], dt[:, 1, :], xf[:, 1, :], ALU.mult).then_inc(s_xdt, 1)
                    dve.wait_ge(s_xdt, 1)
                    dve.wait_ge(s_xdt0, 1)
                    product(1, 0)
                    dve.wait_ge(bc_in[0], 16)
                    dve.tensor_tensor(dbx[:, 0, :, :], xdt[:, :, :],
                                      bcast[:, 0:1, :].broadcast_to([P, CH, TOK]),
                                      ALU.mult).then_inc(dbx_ready[0], 1)
                    scan(0, 0)
                    dve.wait_ge(c_ready, 1)
                    dve.wait_ge(d_added, 2)

                    def step(i, next1, next2):
                        scan(i, 1)
                        if next1:
                            product(i + 1, 1)
                        add_state(i, 0, range(GV))
                        if next1:
                            sparsify(i + 1)
                        residual(i)
                        if next1:
                            scan(i + 1, 0)
                        if next2:
                            product(i + 2, 0)
                        add_state(i, 1, range(GV))

                    steps(dve, step)


_INS = ['L0_attn_x', 'L0_attn_wq_idx', 'L0_attn_wk_idx', 'L0_attn_w_iw', 'L0_attn_wq', 'L0_attn_wk',
        'L0_attn_wv', 'L0_attn_wo', 'L0_ffn_w_router', 'L0_experts',
        'L1_attn_A_log', 'L1_attn_D_skip', 'L1_attn_W_x', 'L1_attn_W_dt', 'L1_attn_b_dt', 'L1_mlp']


def kernel(**inputs):
    import numpy as _np
    import concourse.bacc as _bacc
    from concourse import mybir as _mybir
    from concourse.bass_utils import run_bass_kernel_spmd as _run

    def by_partition(w):
        w = w.reshape(*w.shape[:-2], -1, P, w.shape[-1])
        w = _np.moveaxis(w, -3, -2)
        return w.reshape(*w.shape[:-2], -1)

    given = dict(inputs)
    for name, layer in (('L0_experts', 'L0_ffn'), ('L1_mlp', 'L1_ffn')):
        given[name] = _np.concatenate([by_partition(_np.asarray(inputs[f'{layer}_{w}']))
                                       for w in ('w_gate', 'w_up', 'w_down')], axis=-1)

    nc = _bacc.Bacc("TRN2", target_bir_lowering=False, num_devices=1)
    arrays, args = {}, []
    for name in _INS:
        a = given[name]
        if name == 'L1_attn_D_skip':
            a = a.reshape(1, -1)
        elif a.ndim == 1:
            a = a.reshape(-1, P).T
        a = _np.ascontiguousarray(a)
        arrays[f"in_{name}"] = a
        args.append(nc.dram_tensor(f"in_{name}", a.shape, _mybir.dt.from_np(a.dtype), kind="ExternalInput").ap())
    shape = inputs['L0_attn_x'].shape
    args.append(nc.dram_tensor("out", shape, _mybir.dt.float32, kind="ExternalOutput").ap())
    two_layers(nc, *args)
    r = _run(nc, [arrays], core_ids=[0])
    return r.results[0]["out"]
```
